# Optimizing a Trainium2 kernel written in Bass

```python
import numpy as np
import jax
import jax.numpy as jnp

def _softmax(x, axis=-1):
    return jax.nn.softmax(x, axis=axis)

def _gelu(x):
    return jax.nn.gelu(x, approximate=True)

def _silu(x):
    return jax.nn.silu(x)

def _sigmoid(x):
    return jax.nn.sigmoid(x)

def _layernorm(x, axis=-1, eps=1e-05):
    m = jnp.mean(x, axis=axis, keepdims=True)
    v = jnp.var(x, axis=axis, keepdims=True)
    return (x - m) / jnp.sqrt(v + eps)

def _scatter_add(tgt, idx, src, axis=0):
    return tgt.at[idx].add(src)

def _segment_sum(src, seg, n):
    return jax.ops.segment_sum(src, seg, n)
kernel_name = 'mk_flamingo_gated_d2_seqx_r4_1cf4bb'

def setup_inputs(seed: int=0):
    np.random.seed(seed)
    _w = jnp.asarray

    def _rec_inputs():
        import jax
        import jax.numpy as jnp
        _rk = jax.random.key(seed)
        x = -0.0003929 + 0.9999 * jax.random.normal(jax.random.fold_in(_rk, 1), (16, 256, 512), jnp.float32)
        _lenS = 256 - jax.random.randint(jax.random.fold_in(_rk, 7), (16,), 0, max(1, 256 // 4) + 1, jnp.int32)
        _lenS2 = 256 - jax.random.randint(jax.random.fold_in(_rk, 8), (16,), 0, max(1, 256 // 4) + 1, jnp.int32)
        _ctx_1024P = jax.random.normal(jax.random.fold_in(_rk, 11), (16, 16, 256), jnp.float32)
        _ctx_1024c = jax.random.dirichlet(jax.random.fold_in(_rk, 511), 0.3 * jnp.ones((16,), jnp.float32), (16, 256))
        _ctx_1024t = jnp.einsum('bsk,bkd->bsd', _ctx_1024c, _ctx_1024P)
        _ctx_1024t = _ctx_1024t * jax.lax.rsqrt(jnp.mean(jnp.square(_ctx_1024t)) + 1e-12) * 0.953939
        ctx_1024 = -0.000494167 + 1.00018 * (_ctx_1024t + 0.3 * jax.random.normal(jax.random.fold_in(_rk, 611), (16, 256, 256), jnp.float32))
        _validS = jnp.arange(256)[None, :] < _lenS[:, None]
        _validS2 = jnp.arange(256)[None, :] < _lenS2[:, None]
        _causal = jnp.tril(jnp.ones((256, 256), dtype=bool))
        mask_BxS2_bf1 = jnp.ones((16, 256), dtype=bool)
        _g = jax.random.normal(jax.random.fold_in(_rk, 9001), (2, 2), jnp.float32)
        _g = jnp.sign(_g) * jnp.maximum(jnp.abs(_g), 1.0) + (_g == 0) * 1.0
        g_xattn = _g[0]
        g_ffn = _g[1]
        return (x, ctx_1024, mask_BxS2_bf1, g_xattn, g_ffn)
    x, ctx_1024, mask_BxS2_bf1, g_xattn, g_ffn = _rec_inputs()

    def _L0_xattn_setup():
        import jax, jax.numpy as jnp
        import numpy as np
        N_HEADS = 16
        N_KV_HEADS = 8
        HEAD_DIM = 128
        D_TEXT = 512
        D_VISION = 256
        GROUPS = N_HEADS // N_KV_HEADS
        key = jax.random.key(seed)
        ks = jax.random.split(key, 6)
        B, T_text, T_vis = (4, 512, 144)
        text_hidden = jax.random.normal(ks[0], (B, T_text, D_TEXT), dtype=jnp.float32)
        vision_tokens = jax.random.normal(ks[1], (B, T_vis, D_VISION), dtype=jnp.float32)
        vision_mask = jnp.ones((B, T_vis), dtype=bool)
        s = 0.02
        Wq = jax.random.normal(ks[2], (D_TEXT, N_HEADS * HEAD_DIM), dtype=jnp.float32) * s
        Wk = jax.random.normal(ks[3], (D_VISION, N_KV_HEADS * HEAD_DIM), dtype=jnp.float32) * s
        Wv = jax.random.normal(ks[4], (D_VISION, N_KV_HEADS * HEAD_DIM), dtype=jnp.float32) * s
        Wo = jax.random.normal(ks[5], (N_HEADS * HEAD_DIM, D_TEXT), dtype=jnp.float32) * s
        return {'text_hidden': text_hidden, 'vision_tokens': vision_tokens, 'vision_mask': vision_mask, 'Wq': Wq, 'Wk': Wk, 'Wv': Wv, 'Wo': Wo}
    _L0_xattn_all = _L0_xattn_setup()
    _L0_xattn_in = {k: v for k, v in _L0_xattn_all.items() if k in ('Wq', 'Wk', 'Wv', 'Wo')}
    del _L0_xattn_all

    def _L0_ffn_setup():
        import jax, jax.numpy as jnp
        import numpy as np
        TOP_K = 2
        key = jax.random.key(seed)
        ks = jax.random.split(key, 4)
        G, S, F, E, H = (4, 512, 512, 8, 512)
        return {'x': jax.random.normal(ks[0], (G, S, F), dtype=jnp.float32), 'router_logits': jax.random.normal(ks[1], (F, E), dtype=jnp.float32) * 0.02, 'gating_einsum': jax.random.normal(ks[2], (E, 2, H, F), dtype=jnp.float32) * 0.02, 'linear': jax.random.normal(ks[3], (E, H, F), dtype=jnp.float32) * 0.02, 'per_expert_scale': jnp.ones((E,), dtype=jnp.float32), 'router_scale': jnp.ones((F,), dtype=jnp.float32)}
    _L0_ffn_all = _L0_ffn_setup()
    _L0_ffn_in = {k: v for k, v in _L0_ffn_all.items() if k in ('router_logits', 'gating_einsum', 'linear', 'per_expert_scale', 'router_scale')}
    del _L0_ffn_all

    def _L1_xattn_setup():
        import jax, jax.numpy as jnp
        import numpy as np
        B, S1, S2, DCA = (2, 512, 256, 16)
        QDIM, KDIM, H = (512, 256, 16)
        HD = QDIM // H
        SCALE = HD ** (-0.5)
        EPS = 1e-06
        DCA_WEIGHT = 1.0

        def _ln(t, w, b):
            m = jnp.mean(t, axis=-1, keepdims=True)
            v = jnp.var(t, axis=-1, keepdims=True)
            return (t - m) * jax.lax.rsqrt(v + EPS) * w + b

        def _attn(q, k, v):
            s = jnp.einsum('bhqd,bhkd->bhqk', q, k) * SCALE
            p = jax.nn.softmax(s, axis=-1)
            return jnp.einsum('bhqk,bhkd->bhqd', p, v)
        key = jax.random.key(seed)
        ks = jax.random.split(key, 8)
        w = lambda k, shape: jax.random.normal(k, shape, jnp.float32) * 0.02
        return {'x': jax.random.normal(ks[0], (B, S1, QDIM), jnp.float32), 'y': jax.random.normal(ks[1], (B, S2 + DCA, KDIM), jnp.float32), 'Wq': w(ks[2], (QDIM, QDIM)), 'bq': jnp.zeros((QDIM,), jnp.float32), 'Wk': w(ks[3], (KDIM, QDIM)), 'bk': jnp.zeros((QDIM,), jnp.float32), 'Wv': w(ks[4], (KDIM, QDIM)), 'bv': jnp.zeros((QDIM,), jnp.float32), 'Wkv_dca': w(ks[5], (KDIM, 2 * QDIM)), 'bkv_dca': jnp.zeros((2 * QDIM,), jnp.float32), 'qn_w': jnp.ones((HD,), jnp.float32), 'qn_b': jnp.zeros((HD,), jnp.float32), 'kn_w': jnp.ones((HD,), jnp.float32), 'kn_b': jnp.zeros((HD,), jnp.float32), 'kn_dca_w': jnp.ones((HD,), jnp.float32), 'kn_dca_b': jnp.zeros((HD,), jnp.float32), 'Wo': w(ks[6], (QDIM, QDIM)), 'bo': jnp.zeros((QDIM,), jnp.float32)}
    _L1_xattn_all = _L1_xattn_setup()
    _L1_xattn_in = {k: v for k, v in _L1_xattn_all.items() if k in ('Wq', 'bq', 'Wk', 'bk', 'Wv', 'bv', 'Wkv_dca', 'bkv_dca', 'qn_w', 'qn_b', 'kn_w', 'kn_b', 'kn_dca_w', 'kn_dca_b', 'Wo', 'bo')}
    del _L1_xattn_all

    def _L1_ffn_setup():
        import jax, jax.numpy as jnp
        import numpy as np
        L, N, E, H, K = (512, 8, 512, 2048, 8)
        key = jax.random.key(seed)
        ks = jax.random.split(key, 6)
        return {'x': jax.random.normal(ks[0], (L, N, E), dtype=jnp.float32), 'proj1': jax.random.normal(ks[1], (H, E), dtype=jnp.float32) * 0.02, 'proj1_bias': jax.random.normal(ks[2], (H,), dtype=jnp.float32) * 0.02, 'proj2': jax.random.normal(ks[3], (E, H), dtype=jnp.float32) * 0.02, 'proj2_bias': jax.random.normal(ks[4], (E,), dtype=jnp.float32) * 0.02, 'gate_w': jax.random.normal(ks[5], (E, K), dtype=jnp.float32)}
    _L1_ffn_all = _L1_ffn_setup()
    _L1_ffn_in = {k: v for k, v in _L1_ffn_all.items() if k in ('proj1', 'proj1_bias', 'proj2', 'proj2_bias', 'gate_w')}
    del _L1_ffn_all
    return {'x': x, 'ctx_1024': ctx_1024, 'mask_BxS2_bf1': mask_BxS2_bf1, 'g_xattn': g_xattn, 'g_ffn': g_ffn, 'L0_xattn_Wq': _L0_xattn_in['Wq'], 'L0_xattn_Wk': _L0_xattn_in['Wk'], 'L0_xattn_Wv': _L0_xattn_in['Wv'], 'L0_xattn_Wo': _L0_xattn_in['Wo'], 'L0_ffn_router_logits': _L0_ffn_in['router_logits'], 'L0_ffn_gating_einsum': _L0_ffn_in['gating_einsum'], 'L0_ffn_linear': _L0_ffn_in['linear'], 'L0_ffn_per_expert_scale': _L0_ffn_in['per_expert_scale'], 'L0_ffn_router_scale': _L0_ffn_in['router_scale'], 'L1_xattn_Wq': _L1_xattn_in['Wq'], 'L1_xattn_bq': _L1_xattn_in['bq'], 'L1_xattn_Wk': _L1_xattn_in['Wk'], 'L1_xattn_bk': _L1_xattn_in['bk'], 'L1_xattn_Wv': _L1_xattn_in['Wv'], 'L1_xattn_bv': _L1_xattn_in['bv'], 'L1_xattn_Wkv_dca': _L1_xattn_in['Wkv_dca'], 'L1_xattn_bkv_dca': _L1_xattn_in['bkv_dca'], 'L1_xattn_qn_w': _L1_xattn_in['qn_w'], 'L1_xattn_qn_b': _L1_xattn_in['qn_b'], 'L1_xattn_kn_w': _L1_xattn_in['kn_w'], 'L1_xattn_kn_b': _L1_xattn_in['kn_b'], 'L1_xattn_kn_dca_w': _L1_xattn_in['kn_dca_w'], 'L1_xattn_kn_dca_b': _L1_xattn_in['kn_dca_b'], 'L1_xattn_Wo': _L1_xattn_in['Wo'], 'L1_xattn_bo': _L1_xattn_in['bo'], 'L1_ffn_proj1': _L1_ffn_in['proj1'], 'L1_ffn_proj1_bias': _L1_ffn_in['proj1_bias'], 'L1_ffn_proj2': _L1_ffn_in['proj2'], 'L1_ffn_proj2_bias': _L1_ffn_in['proj2_bias'], 'L1_ffn_gate_w': _L1_ffn_in['gate_w']}

def reference(x, ctx_1024, mask_BxS2_bf1, g_xattn, g_ffn, L0_xattn_Wq, L0_xattn_Wk, L0_xattn_Wv, L0_xattn_Wo, L0_ffn_router_logits, L0_ffn_gating_einsum, L0_ffn_linear, L0_ffn_per_expert_scale, L0_ffn_router_scale, L1_xattn_Wq, L1_xattn_bq, L1_xattn_Wk, L1_xattn_bk, L1_xattn_Wv, L1_xattn_bv, L1_xattn_Wkv_dca, L1_xattn_bkv_dca, L1_xattn_qn_w, L1_xattn_qn_b, L1_xattn_kn_w, L1_xattn_kn_b, L1_xattn_kn_dca_w, L1_xattn_kn_dca_b, L1_xattn_Wo, L1_xattn_bo, L1_ffn_proj1, L1_ffn_proj1_bias, L1_ffn_proj2, L1_ffn_proj2_bias, L1_ffn_gate_w):
    import jax
    import jax.numpy as jnp

    def _L0_xattn_ref(text_hidden, vision_tokens, vision_mask, Wq, Wk, Wv, Wo):
        import jax, jax.numpy as jnp
        import numpy as np
        N_HEADS = 16
        N_KV_HEADS = 8
        HEAD_DIM = 128
        D_TEXT = 512
        D_VISION = 256
        GROUPS = N_HEADS // N_KV_HEADS
        B, T_text, _ = text_hidden.shape
        T_vis = vision_tokens.shape[1]
        scale = jnp.float32(np.sqrt(HEAD_DIM))
        q = (text_hidden @ Wq).reshape(B, T_text, N_HEADS, HEAD_DIM).transpose(0, 2, 1, 3)
        k = (vision_tokens @ Wk).reshape(B, T_vis, N_KV_HEADS, HEAD_DIM).transpose(0, 2, 1, 3)
        v = (vision_tokens @ Wv).reshape(B, T_vis, N_KV_HEADS, HEAD_DIM).transpose(0, 2, 1, 3)
        k = jnp.repeat(k, GROUPS, axis=1)
        v = jnp.repeat(v, GROUPS, axis=1)
        scores = jnp.einsum('bhtd,bhsd->bhts', q, k) / scale
        mask = vision_mask[:, None, None, :]
        scores = jnp.where(mask, scores, -jnp.inf)
        attn = jax.nn.softmax(scores, axis=-1)
        attn = jnp.nan_to_num(attn, nan=0.0)
        out = jnp.einsum('bhts,bhsd->bhtd', attn, v)
        out = out.transpose(0, 2, 1, 3).reshape(B, T_text, N_HEADS * HEAD_DIM)
        return out @ Wo

    def _L0_ffn_ref(x, router_logits, gating_einsum, linear, per_expert_scale, router_scale):
        import jax, jax.numpy as jnp
        import numpy as np
        TOP_K = 2
        G, S, F = x.shape
        E = router_logits.shape[-1]
        H = linear.shape[1]
        k = TOP_K
        dtype = x.dtype
        var = jnp.mean(jnp.square(x.astype(jnp.float32)), axis=-1, keepdims=True)
        router_input = x * jax.lax.rsqrt(var + 1e-06).astype(dtype)
        root_size = jax.lax.rsqrt(jnp.array(F, dtype=dtype))
        router_input = router_input * root_size * router_scale.astype(dtype)
        logits = jnp.einsum('gsd,de->gse', router_input, router_logits.astype(dtype))
        logits32 = logits.astype(jnp.float32)
        probs = jax.nn.softmax(logits32, axis=-1)
        _, choices = jax.lax.approx_max_k(logits32, k=k)
        indicator = jax.nn.one_hot(choices, E, dtype=probs.dtype).sum(axis=-2)
        renorm = jnp.sum(indicator * probs, axis=-1, keepdims=True)
        renorm = jnp.where(renorm > 0.0, renorm, 1.0)
        weights = probs / renorm
        x_flat = x.reshape((-1, F))
        batch_size = G * S
        choices_flat = choices.ravel()
        xs_order = choices_flat.argsort()
        xs_reverse_argsort = xs_order.argsort()
        xs_indices = jnp.repeat(jnp.arange(batch_size), k)[xs_order]
        sorted_xs = x_flat[xs_indices, :]
        choices_oh = jax.nn.one_hot(choices, num_classes=E, dtype=jnp.int32)
        tokens_per_expert = jnp.sum(choices_oh, axis=(0, 1, 2))
        combine_weights = (choices_oh.astype(jnp.float32) * jnp.expand_dims(weights, axis=2)).sum(axis=-1).astype(weights.dtype)
        w_gate = jnp.transpose(gating_einsum, (0, 3, 1, 2)).reshape(E, F, 2 * H)
        gate_out = jax.lax.ragged_dot(sorted_xs, w_gate.astype(dtype), group_sizes=tokens_per_expert)
        gate_out = gate_out.reshape(gate_out.shape[0], 2, H)
        activation = jax.nn.gelu(gate_out[:, 0, :]) * gate_out[:, 1, :]
        expert_outputs = jax.lax.ragged_dot(activation, linear.astype(dtype), group_sizes=tokens_per_expert)
        expert_indices = jnp.repeat(jnp.arange(E), tokens_per_expert, total_repeat_length=expert_outputs.shape[0])
        expert_outputs = expert_outputs * per_expert_scale.astype(expert_outputs.dtype)[expert_indices, None]
        out = expert_outputs[xs_reverse_argsort].reshape((G, S, k, -1))
        out = jnp.einsum('blkd,blk->bld', out, combine_weights, preferred_element_type=out.dtype)
        return out

    def _L1_xattn_ref(x, y, Wq, bq, Wk, bk, Wv, bv, Wkv_dca, bkv_dca, qn_w, qn_b, kn_w, kn_b, kn_dca_w, kn_dca_b, Wo, bo):
        import jax, jax.numpy as jnp
        import numpy as np
        B, S1, S2, DCA = (2, 512, 256, 16)
        QDIM, KDIM, H = (512, 256, 16)
        HD = QDIM // H
        SCALE = HD ** (-0.5)
        EPS = 1e-06
        DCA_WEIGHT = 1.0

        def _ln(t, w, b):
            m = jnp.mean(t, axis=-1, keepdims=True)
            v = jnp.var(t, axis=-1, keepdims=True)
            return (t - m) * jax.lax.rsqrt(v + EPS) * w + b

        def _attn(q, k, v):
            s = jnp.einsum('bhqd,bhkd->bhqk', q, k) * SCALE
            p = jax.nn.softmax(s, axis=-1)
            return jnp.einsum('bhqk,bhkd->bhqd', p, v)
        b, s1, _ = x.shape
        y_dca = y[:, -DCA:, :]
        y_main = y[:, :-DCA, :]
        kv_dca = (y_dca @ Wkv_dca + bkv_dca).reshape(b, DCA, 2, H, HD)
        k_dca = _ln(kv_dca[:, :, 0], kn_dca_w, kn_dca_b)
        v_dca = kv_dca[:, :, 1]
        s2 = y_main.shape[1]
        q = _ln((x @ Wq + bq).reshape(b, s1, H, HD), qn_w, qn_b)
        kv = jnp.concatenate([y_main @ Wk + bk, y_main @ Wv + bv], axis=-1)
        kv = kv.reshape(b, s2, H, 2 * HD)
        k = _ln(kv[..., :HD], kn_w, kn_b)
        v = kv[..., HD:]
        qT = q.transpose(0, 2, 1, 3)
        ctx = _attn(qT, k.transpose(0, 2, 1, 3), v.transpose(0, 2, 1, 3))
        ctx = ctx.transpose(0, 2, 1, 3).reshape(b, s1, QDIM)
        ctx_dca = _attn(qT, k_dca.transpose(0, 2, 1, 3), v_dca.transpose(0, 2, 1, 3))
        ctx_dca = ctx_dca.transpose(0, 2, 1, 3).reshape(b, s1, QDIM)
        ctx = ctx + DCA_WEIGHT * ctx_dca
        return ctx @ Wo + bo

    def _L1_ffn_ref(x, proj1, proj1_bias, proj2, proj2_bias, gate_w):
        import jax, jax.numpy as jnp
        import numpy as np
        L, N, E, H, K = (512, 8, 512, 2048, 8)
        dst = jnp.argmax(jnp.einsum('lne,ek->lnk', x, gate_w), axis=-1)
        h = jax.nn.gelu(jnp.einsum('lne,he->lnh', x, proj1) + proj1_bias, approximate=False)
        out = jnp.einsum('lnh,eh->lne', h, proj2) + proj2_bias
        del dst
        return out
    x = x + jnp.tanh(g_xattn[0]) * _L0_xattn_ref(_layernorm(x, axis=-1), ctx_1024, mask_BxS2_bf1, L0_xattn_Wq, L0_xattn_Wk, L0_xattn_Wv, L0_xattn_Wo)
    x = x + jnp.tanh(g_ffn[0]) * _L0_ffn_ref(_layernorm(x, axis=-1), L0_ffn_router_logits, L0_ffn_gating_einsum, L0_ffn_linear, L0_ffn_per_expert_scale, L0_ffn_router_scale)
    x = x + jnp.tanh(g_xattn[1]) * _L1_xattn_ref(_layernorm(x, axis=-1), ctx_1024, L1_xattn_Wq, L1_xattn_bq, L1_xattn_Wk, L1_xattn_bk, L1_xattn_Wv, L1_xattn_bv, L1_xattn_Wkv_dca, L1_xattn_bkv_dca, L1_xattn_qn_w, L1_xattn_qn_b, L1_xattn_kn_w, L1_xattn_kn_b, L1_xattn_kn_dca_w, L1_xattn_kn_dca_b, L1_xattn_Wo, L1_xattn_bo)
    x = x + jnp.tanh(g_ffn[1]) * _L1_ffn_ref(_layernorm(x, axis=-1), L1_ffn_proj1, L1_ffn_proj1_bias, L1_ffn_proj2, L1_ffn_proj2_bias, L1_ffn_gate_w)
    return x

_drawn_inputs = setup_inputs


def setup_inputs(seed=0):
    import zlib

    import numpy as np

    out = dict(_drawn_inputs(seed))
    spreads = {'g_ffn': (-1.0, 0.6),
     'L0_ffn_per_expert_scale': (1.0, 0.6),
     'L0_ffn_router_scale': (1.0, 0.6),
     'L1_xattn_bq': (0.0, 0.774),
     'L1_xattn_bk': (0.0, 0.29),
     'L1_xattn_bv': (0.0, 0.272),
     'L1_xattn_bkv_dca': (0.0, 0.1),
     'L1_xattn_qn_w': (1.0, 0.6),
     'L1_xattn_qn_b': (0.0, 0.8),
     'L1_xattn_kn_w': (1.0, 0.6),
     'L1_xattn_kn_b': (0.0, 0.8),
     'L1_xattn_kn_dca_w': (1.0, 0.6),
     'L1_xattn_kn_dca_b': (0.0, 0.8),
     'L1_xattn_bo': (0.0, 0.1)}
    factors = {'L0_xattn_Wq': 8.0,
     'L0_xattn_Wk': 8.0,
     'L1_ffn_proj1_bias': 6.49,
     'L1_ffn_proj2_bias': 3.651}
    for name, (base, spread) in spreads.items():
        noise = np.random.default_rng([zlib.crc32(name.encode()), seed]).standard_normal(out[name].shape)
        drawn = base * np.exp(spread * noise) if base else spread * noise
        out[name] = jnp.asarray(drawn.astype(out[name].dtype))
    for name, factor in factors.items():
        out[name] = (out[name] * factor).astype(out[name].dtype)
    return out
```

```python
from contextlib import ExitStack

import numpy as np

import concourse.bass as bass
from concourse import mybir

F32, F32R, U8, U32, I32 = mybir.dt.float32, mybir.dt.float32r, mybir.dt.uint8, mybir.dt.uint32, mybir.dt.int32
ALU = mybir.AluOpType
ACT = mybir.ActivationFunctionType
AX = mybir.AxisListType
P = 128
B, S, D, DC = 16, 256, 512, 256
TOK = B * S
NHEAD0, DH0 = 16, 128
LN_EPS = 1e-5
E, H0, TOPK = 8, 512, 2
ROUTER_EPS = 1e-6
NHEAD1, DCA = 16, 16
HEAD_EPS = 1e-6
H1 = 2048
TILE = 256
TILES = TOK * TOPK // TILE + E - 1
SLOTS = E * TOK + 2 * E * TILE
MASKED = -1.0e30
TINY = 1.0e-30
NEG_INF = -3.0e38

ROOT_MAGIC = 1597463007.0
ROOT_TURNS = 3
ROOT_LINKS = 3 + 3 * ROOT_TURNS


def inverse_root(eng, ops, chain, at, var, eps, tmp, y):
    v, w, t = (x[:] for x in tmp)
    eng.wait_ge(chain, at)
    ops.tensor_scalar(v, var, eps, None, ALU.add).then_inc(chain, 1)
    eng.wait_ge(chain, at + 1)
    ops.tensor_scalar(w, v, -0.5, None, ALU.mult).then_inc(chain, 1)
    ops.tensor_scalar(y.bitcast(I32), v.bitcast(I32), -0.5, ROOT_MAGIC, ALU.mult, ALU.add).then_inc(chain, 1)
    for n in range(ROOT_TURNS):
        eng.wait_ge(chain, at + 3 + 3 * n)
        ops.tensor_tensor(t, y, y, ALU.mult).then_inc(chain, 1)
        eng.wait_ge(chain, at + 4 + 3 * n)
        ops.tensor_tensor(t, t, w, ALU.mult).then_inc(chain, 1)
        eng.wait_ge(chain, at + 5 + 3 * n)
        ops.scalar_tensor_tensor(y, t, 1.5, y, ALU.add, ALU.mult).then_inc(chain, 1)
    eng.wait_ge(chain, at + ROOT_LINKS)


def clear(nc, semaphores):
    nc.clear_and_free_semaphores(semaphores)
    nc.all_engine_barrier()


def gated_cross_attention(nc, half, x_ln, x_res, x_out, ctx_t, mask, gate, wq, wk, wv, wo, identity, tag):
    HEADS = NHEAD0 // 2
    GROUPS = HEADS // 2
    C0 = half * HEADS * DH0
    G0 = half * GROUPS * DH0
    SCALE = 1.0 / float(np.sqrt(DH0))
    PAIR = 2 * HEADS
    ITEMS = 6 + HEADS
    FC, CC = D // P, DC // P

    used = []
    with ExitStack() as ctx:
        def sb(name, shape, dt=F32):
            return ctx.enter_context(nc.sbuf_tensor(tag + name, shape, dt))

        def bank(name):
            return ctx.enter_context(nc.psum_tensor(tag + name, [P, 512], F32))

        def sem(name):
            used.append(nc.alloc_semaphore(tag + name))
            return used[-1]

        wq_hi, wq_lo = sb("wq_hi", [P, FC, HEADS * DH0], F32R), sb("wq_lo", [P, FC, HEADS * DH0], F32R)
        wk_hi, wk_lo = sb("wk_hi", [P, CC, GROUPS * DH0], F32R), sb("wk_lo", [P, CC, GROUPS * DH0], F32R)
        wv_hi, wv_lo = sb("wv_hi", [P, CC, GROUPS * DH0], F32R), sb("wv_lo", [P, CC, GROUPS * DH0], F32R)
        wo_hi, wo_lo = sb("wo_hi", [P, HEADS, D], F32R), sb("wo_lo", [P, HEADS, D], F32R)
        w_raw = sb("w_raw", [P, 2, 2048])
        ident = sb("ident", [P, P])
        mask_u8 = sb("mask_u8", [P, B * S], U8)
        maskb = sb("maskb", [P, 2, S])
        gate_t = sb("gate_t", [P, 1])
        x_sb = sb("x_sb", [P, 2, 2, D])
        xr_sb = sb("xr_sb", [P, 2, 2, D])
        xo_sb = sb("xo_sb", [P, 2, 2, D])
        xn = sb("xn", [P, 2, D])
        stats = sb("stats", [P, 2, 6])
        mv = sb("mv", [P, 2, 2])
        rstd = sb("rstd", [P, 2])
        root = [sb(f"root{n}", [P, 2]) for n in range(3)]
        ctx_raw = sb("ctx_raw", [P, 2, CC, S])
        ctx_hi, ctx_lo = sb("ctx_hi", [P, CC, S], F32R), sb("ctx_lo", [P, CC, S], F32R)
        xt_hi, xt_lo = sb("xt_hi", [P, 2, FC, S], F32R), sb("xt_lo", [P, 2, FC, S], F32R)
        k_hi, k_lo = sb("k_hi", [P, 2, GROUPS, S], F32R), sb("k_lo", [P, 2, GROUPS, S], F32R)
        v_hi, v_lo = sb("v_hi", [P, 2, 2, GROUPS * DH0], F32R), sb("v_lo", [P, 2, 2, GROUPS * DH0], F32R)
        q_hi, q_lo = sb("q_hi", [P, 2, S], F32R), sb("q_lo", [P, 2, S], F32R)
        prob = sb("prob", [P, 2, 2, S])
        mx = sb("mx", [P, 2, 2])
        nbias = sb("nbias", [P, 2, 2])
        rsum = sb("rsum", [P, 2, 2])
        rinv = sb("rinv", [P, 2, 2])
        rsafe = sb("rsafe", [P, 2, 2])
        pt_hi, pt_lo = sb("pt_hi", [P, 2, 2, S], F32R), sb("pt_lo", [P, 2, 2, S], F32R)
        ot_hi, ot_lo = sb("ot_hi", [P, 2, S], F32R), sb("ot_lo", [P, 2, S], F32R)

        pj = [bank("pj0"), bank("pj1")]
        sc = [bank("sc0"), bank("sc1")]
        ptb, avb = bank("ptb"), bank("avb")
        ob = [bank("ob0"), bank("ob1")]

        w_loaded = [sem("w_loaded0"), sem("w_loaded1")]
        w_hi, w_lo = sem("w_hi"), sem("w_lo")
        m_loaded, g_loaded, g_done, id_done = sem("m_loaded"), sem("g_loaded"), sem("g_done"), sem("id_done")
        x_loaded = [sem("x_loaded0"), sem("x_loaded1")]
        c_loaded = [sem("c_loaded0"), sem("c_loaded1")]
        chain = sem("chain")
        xn_done, c_hi, c_lo = sem("xn_done"), sem("c_hi"), sem("c_lo")
        pj_ready, pj_hi, pj_lo = sem("pj_ready"), sem("pj_hi"), sem("pj_lo")
        s_ready, s_max, s_bias, e_done, r_half, r_done, p_done = (
            sem("s_ready"), sem("s_max"), sem("s_bias"), sem("e_done"), sem("r_half"), sem("r_done"), sem("p_done"))
        t_ready, pt_hid, pt_lod = sem("t_ready"), sem("pt_hid"), sem("pt_lod")
        av_ready, ot_hid, ot_lod = sem("av_ready"), sem("ot_hid"), sem("ot_lod")
        o_ready, o_free, x_stored = sem("o_ready"), sem("o_free"), [sem("x_stored0"), sem("x_stored1")]

        pieces = [(wk[:, :, G0:G0 + GROUPS * DH0], wk_hi[:], wk_lo[:]), (wv[:, :, G0:G0 + GROUPS * DH0], wv_hi[:], wv_lo[:])]
        for c in range(0, FC, 2):
            pieces.append((wq[:, c:c + 2, C0:C0 + HEADS * DH0], wq_hi[:, c:c + 2], wq_lo[:, c:c + 2]))
        for h in range(0, HEADS, 4):
            pieces.append((wo[:, half * HEADS + h:half * HEADS + h + 4], wo_hi[:, h:h + 4], wo_lo[:, h:h + 4]))

        def raw(n):
            a, b = pieces[n][0].shape[1:]
            return w_raw[:, n % 2, 0:a * b].rearrange("p (a b) -> p a b", a=a)

        STEPS = range(-1, PAIR + 3)
        AHEAD = HEADS // 2

        def shared(u):
            return {-1: 0, AHEAD: 1}.get(u)

        order = []
        for u in STEPS:
            if shared(u) is not None:
                order += [(shared(u), j) for j in range(6)]
            if u + 1 < PAIR:
                order.append(((u + 1) // HEADS, 6 + (u + 1) % HEADS))
        place = {what: n for n, what in enumerate(order)}

        def made(i, bb, j):
            return len(order) * i + place[bb, j] + 1

        def item(bb, j):
            if j < 2:
                return xt_hi[:, bb, 2 * j:2 * j + 2], xt_lo[:, bb, 2 * j:2 * j + 2]
            if j < 4:
                g = 2 * (j - 2)
                return k_hi[:, bb, g:g + 2], k_lo[:, bb, g:g + 2]
            if j < 6:
                return v_hi[:, bb, j - 4], v_lo[:, bb, j - 4]
            return q_hi[:, j % 2], q_lo[:, j % 2]

        def item_psum(bb, j):
            b = pj[place[bb, j] % 2]
            if j < 4:
                return b[:].rearrange("p (a s) -> p a s", a=2)
            return b[:] if j < 6 else b[:, 0:S]

        block = ctx.enter_context(nc.Block())

        @block.sync
        def _(sp):
            sp.dma_start(gate_t[:], gate).then_inc(g_loaded, 16)
            sp.dma_start(mask_u8[:], mask).then_inc(m_loaded, 16)
            for n, (src, _, _) in enumerate(pieces):
                if n >= 2:
                    sp.wait_ge(w_lo, n - 1)
                sp.dma_start(raw(n), src).then_inc(w_loaded[n % 2], 16)
            with sp.Fori(0, B // 2) as i:
                for bb in range(2):
                    sp.wait_ge(o_free, 2 * i + bb + 1)
                    rows = bass.ds((2 * i + bb) * S, S)
                    sp.dma_start(x_sb[:, bb], x_ln[rows, :].rearrange("(t p) d -> p t d", p=P)).then_inc(x_loaded[bb], 16)
                    sp.dma_start(xr_sb[:, bb], x_res[rows, :].rearrange("(t p) d -> p t d", p=P)).then_inc(x_loaded[bb], 16)
                    sp.dma_start(ctx_raw[:, bb], ctx_t[bass.ds(2 * i + bb, 1)].rearrange("o (c p) s -> p (o c) s", p=P)).then_inc(c_loaded[bb], 16)

        @block.tensor
        def _(pe):
            def three(out, a_hi, a_lo, b_hi, b_lo, start, stop):
                nc.tensor.matmul(out, a_hi, b_hi, start=start, stop=False)
                nc.tensor.matmul(out, a_hi, b_lo, start=False, stop=False)
                return nc.tensor.matmul(out, a_lo, b_hi, start=False, stop=stop)

            def items(i, bb):
                if bb == 0:
                    pe.wait_ge(xn_done, 2 * i + 1)
                else:
                    pe.wait_ge(xn_done, 2 * i + 2)
                for j in range(6):
                    if place[bb, j] >= 2:
                        pe.wait_ge(pj_lo, made(i, bb, j) - 2)
                    out = item_psum(bb, j)
                    if j < 2:
                        for c in range(2):
                            for t in range(2):
                                mm = nc.tensor.transpose(out[:, c, t * P:(t + 1) * P], xn[:, t, (2 * j + c) * P:(2 * j + c + 1) * P], ident[:])
                    elif j < 4:
                        if j == 2:
                            pe.wait_ge(c_lo, 2 * i + bb + 1)
                        for a in range(2):
                            g = (2 * (j - 2) + a) * DH0
                            for c in range(CC):
                                mm = three(out[:, a], wk_hi[:, c, g:g + DH0], wk_lo[:, c, g:g + DH0],
                                           ctx_hi[:, c], ctx_lo[:, c], c == 0, c == CC - 1)
                    else:
                        t = (j - 4) * P
                        for c in range(CC):
                            mm = three(out, ctx_hi[:, c, t:t + P], ctx_lo[:, c, t:t + P], wv_hi[:, c], wv_lo[:, c], c == 0, c == CC - 1)
                    mm.then_inc(pj_ready, 1)

            def query(i, u):
                bb, h = divmod(u, HEADS)
                pe.wait_ge(pj_lo, made(i, bb, 6 + h) - 2)
                if h == 0:
                    pe.wait_ge(pj_lo, made(i, bb, 1))
                for c in range(FC):
                    mm = three(item_psum(bb, 6 + h), wq_hi[:, c, h * DH0:(h + 1) * DH0], wq_lo[:, c, h * DH0:(h + 1) * DH0],
                               xt_hi[:, bb, c], xt_lo[:, bb, c], c == 0, c == FC - 1)
                mm.then_inc(pj_ready, 1)

            def scores(i, u):
                bb, h = divmod(u, HEADS)
                pe.wait_ge(pj_lo, made(i, bb, 6 + h))
                if u >= 2:
                    pe.wait_ge(s_max, PAIR * i + u - 1)
                out = sc[u % 2][:].rearrange("p (t s) -> p t s", t=2)
                for t in range(2):
                    mm = three(out[:, t], q_hi[:, h % 2, t * P:(t + 1) * P], q_lo[:, h % 2, t * P:(t + 1) * P],
                               k_hi[:, bb, h // 2], k_lo[:, bb, h // 2], True, True)
                mm.then_inc(s_ready, 1)

            def turn(i, u):
                pe.wait_ge(p_done, PAIR * i + u + 1)
                if u >= 1:
                    pe.wait_ge(pt_lod, PAIR * i + u)
                out = ptb[:].rearrange("p (k s) -> p k s", k=2)
                for k in range(2):
                    for t in range(2):
                        mm = nc.tensor.transpose(out[:, k, t * P:(t + 1) * P], prob[:, u % 2, t, k * P:(k + 1) * P], ident[:])
                mm.then_inc(t_ready, 1)

            def values(i, u):
                bb, h = divmod(u, HEADS)
                g = (h // 2) * DH0
                pe.wait_ge(pt_lod, PAIR * i + u + 1)
                if u >= 1:
                    pe.wait_ge(ot_lod, PAIR * i + u)
                for k in range(2):
                    mm = three(avb[:, 0:S], v_hi[:, bb, k, g:g + DH0], v_lo[:, bb, k, g:g + DH0],
                               pt_hi[:, u % 2, k], pt_lo[:, u % 2, k], k == 0, k == 1)
                mm.then_inc(av_ready, 1)

            def project(i, u):
                bb, h = divmod(u, HEADS)
                pe.wait_ge(ot_lod, PAIR * i + u + 1)
                if h == 0:
                    pe.wait_ge(o_free, 2 * i + bb + 2)
                for t in range(2):
                    mm = three(ob[t][:], ot_hi[:, u % 2, t * P:(t + 1) * P], ot_lo[:, u % 2, t * P:(t + 1) * P],
                               wo_hi[:, h], wo_lo[:, h], h == 0, h == HEADS - 1)
                if h == HEADS - 1:
                    mm.then_inc(o_ready, 1)

            pe.wait_ge(id_done, 16)
            pe.wait_ge(w_lo, len(pieces))
            with pe.Fori(0, B // 2) as i:
                for u in STEPS:
                    if shared(u) is not None:
                        items(i, shared(u))
                    if u + 1 < PAIR:
                        query(i, u + 1)
                    if 0 <= u < PAIR:
                        scores(i, u)
                    if 0 <= u - 1 < PAIR:
                        turn(i, u - 1)
                    if 0 <= u - 2 < PAIR:
                        values(i, u - 2)
                    if 0 <= u - 3 < PAIR:
                        project(i, u - 3)

        @block.scalar
        def _(act):
            act.wait_ge(g_loaded, 16)
            nc.scalar.activation(gate_t[:], gate_t[:], ACT.Tanh).then_inc(g_done, 1)
            for n in range(len(pieces)):
                act.wait_ge(w_loaded[n % 2], 16 * (n // 2 + 1))
                nc.scalar.copy(pieces[n][1], raw(n)).then_inc(w_hi, 1)

            def high(i, bb, j):
                act.wait_ge(pj_ready, made(i, bb, j))
                nc.scalar.copy(item(bb, j)[0], item_psum(bb, j)).then_inc(pj_hi, 1)

            with act.Fori(0, B // 2) as i:
                for u in STEPS:
                    bb = shared(u)
                    if bb is not None:
                        act.wait_ge(c_loaded[bb], 16 * i + 16)
                        if bb == 1:
                            act.wait_ge(pj_lo, made(i, 0, 5))
                        nc.scalar.copy(ctx_hi[:], ctx_raw[:, bb]).then_inc(c_hi, 1)
                        for j in range(6):
                            high(i, bb, j)
                    if u + 1 < PAIR:
                        high(i, (u + 1) // HEADS, 6 + (u + 1) % HEADS)
                    if 0 <= u < PAIR:
                        act.wait_ge(s_bias, PAIR * i + u + 1)
                        for t in range(2):
                            e = nc.scalar.activation(prob[:, u % 2, t], prob[:, u % 2, t], ACT.Exp, bias=nbias[:, u % 2, t:t + 1],
                                                     scale=SCALE, accum_out=rsum[:, u % 2, t:t + 1])
                        e.then_inc(e_done, 1)
                    if 0 <= u - 1 < PAIR:
                        act.wait_ge(t_ready, PAIR * i + u)
                        nc.scalar.copy(pt_hi[:, (u - 1) % 2], ptb[:].rearrange("p (k s) -> p k s", k=2)).then_inc(pt_hid, 1)
                    if 0 <= u - 2 < PAIR:
                        act.wait_ge(av_ready, PAIR * i + u - 1)
                        nc.scalar.copy(ot_hi[:, (u - 2) % 2], avb[:, 0:S]).then_inc(ot_hid, 1)
                    if u - 3 in (HEADS - 1, PAIR - 1):
                        bb = (u - 3) // HEADS
                        act.wait_ge(o_free, 2 * i + bb + 3)
                        act.dma_start(x_out[bass.ds((2 * i + bb) * S, S), :].rearrange("(t p) d -> p t d", p=P),
                                      xo_sb[:, bb]).then_inc(x_stored[bb], 16)
            for bb in range(2):
                act.wait_ge(x_stored[bb], 16 * (B // 2) + 16)

        @block.gpsimd
        def _(pool):
            pool.dma_start(ident[:], identity).then_inc(id_done, 16)
            with pool.Fori(0, B // 2) as i:
                for u in range(PAIR):
                    pool.wait_ge(r_done, PAIR * i + u + 1)
                    pool.nop(nofuse=True)
                    for t in range(2):
                        p = nc.gpsimd.tensor_scalar(prob[:, u % 2, t], prob[:, u % 2, t], rinv[:, u % 2, t:t + 1], None, ALU.mult)
                    p.then_inc(p_done, 1)

        @block.vector
        def _(dve):
            def low(out, raw_in, hi):
                return nc.vector.tensor_tensor(out, raw_in, hi.bitcast(F32), ALU.subtract)

            nc.vector.memset(nbias[:], 0.0).then_inc(o_free, 2)
            for bb in range(2):
                nc.vector.memset(rsum[:, bb], 1.0).then_inc(x_stored[bb], 16)
            for n in range(len(pieces)):
                dve.wait_ge(w_hi, n + 1)
                low(pieces[n][2], raw(n), pieces[n][1]).then_inc(w_lo, 1)
            dve.wait_ge(m_loaded, 16)
            dve.wait_ge(g_done, 1)

            def low_item(i, bb, j):
                dve.wait_ge(pj_hi, made(i, bb, j))
                low(item(bb, j)[1], item_psum(bb, j), item(bb, j)[0]).then_inc(pj_lo, 1)

            LINKS = 3 + ROOT_LINKS

            def normalize(i, bb):
                at = LINKS * (2 * i + bb)
                dve.wait_ge(x_loaded[bb], 32 * i + 32)
                for t in range(2):
                    l = nc.vector.bn_stats(stats[:, t], x_sb[:, bb, t])
                l.then_inc(chain, 1)
                dve.wait_ge(chain, at + 1)
                dve.nop(nofuse=True)
                for t in range(2):
                    l = nc.vector.bn_aggr(mv[:, t], stats[:, t])
                l.then_inc(chain, 1)
                inverse_root(dve, nc.vector, chain, at + 2, mv[:, :, 1], LN_EPS, root, rstd[:])
                for t in range(2):
                    l = nc.vector.tensor_scalar(xn[:, t], x_sb[:, bb, t], mv[:, t, 0:1], rstd[:, t:t + 1], ALU.subtract, ALU.mult)
                l.then_inc(xn_done, 1)
                nc.vector.tensor_scalar(maskb[:, bb], mask_u8[:, bass.ds((2 * i + bb) * S, S)], -1.0, -MASKED, ALU.add, ALU.mult).then_inc(chain, 1)
                dve.wait_ge(chain, at + LINKS)

            with dve.Fori(0, B // 2) as i:
                for u in STEPS:
                    if 0 <= u - 1 < PAIR:
                        v = u - 1
                        dve.wait_ge(e_done, PAIR * i + v + 1)
                        nc.vector.tensor_scalar(rsafe[:, v % 2], rsum[:, v % 2], TINY, None, ALU.max).then_inc(r_half, 1)
                        dve.wait_ge(r_half, PAIR * i + v + 1)
                        nc.vector.reciprocal(rinv[:, v % 2], rsafe[:, v % 2]).then_inc(r_done, 1)
                    bb = shared(u)
                    if bb is not None:
                        normalize(i, bb)
                        dve.wait_ge(c_hi, 2 * i + bb + 1)
                        low(ctx_lo[:], ctx_raw[:, bb], ctx_hi[:]).then_inc(c_lo, 1)
                        for j in range(6):
                            low_item(i, bb, j)
                    if u + 1 < PAIR:
                        low_item(i, (u + 1) // HEADS, 6 + (u + 1) % HEADS)
                    if 0 <= u < PAIR:
                        dve.wait_ge(s_ready, PAIR * i + u + 1)
                        dve.nop(nofuse=True)
                        out = sc[u % 2][:].rearrange("p (t s) -> p t s", t=2)
                        for t in range(2):
                            m = nc.vector.tensor_tensor_reduce(prob[:, u % 2, t], out[:, t], maskb[:, u // HEADS], 1.0, NEG_INF, ALU.add, ALU.max,
                                                               mx[:, u % 2, t:t + 1])
                        m.then_inc(s_max, 1)
                        dve.wait_ge(s_max, PAIR * i + u + 1)
                        nc.vector.tensor_scalar(nbias[:, u % 2], mx[:, u % 2], MASKED / 2, -SCALE, ALU.max, ALU.mult).then_inc(s_bias, 1)
                    if 0 <= u - 1 < PAIR:
                        dve.wait_ge(pt_hid, PAIR * i + u)
                        low(pt_lo[:, (u - 1) % 2], ptb[:].rearrange("p (k s) -> p k s", k=2), pt_hi[:, (u - 1) % 2]).then_inc(pt_lod, 1)
                    if 0 <= u - 2 < PAIR:
                        dve.wait_ge(ot_hid, PAIR * i + u - 1)
                        low(ot_lo[:, (u - 2) % 2], avb[:, 0:S], ot_hi[:, (u - 2) % 2]).then_inc(ot_lod, 1)
                    if u - 3 in (HEADS - 1, PAIR - 1):
                        bb = (u - 3) // HEADS
                        dve.wait_ge(o_ready, 2 * i + bb + 1)
                        dve.wait_ge(x_stored[bb], 16 * i + 16)
                        for t in range(2):
                            o = nc.vector.scalar_tensor_tensor(xo_sb[:, bb, t], ob[t][:], gate_t[:, 0:1], xr_sb[:, bb, t], ALU.mult, ALU.add)
                        o.then_inc(o_free, 1)
    clear(nc, used)


def route(nc, x_in, xn_out, slot_tokens, tile_table, logits_w, router_scale, expert_scale, gate, identity, earlier, iotas, pairs, empty_list, weights, tag):
    QT = 4
    TURNS = TOK // (QT * P)
    FC = D // P
    used = []
    with ExitStack() as ctx:
        def sb(name, shape, dt=F32):
            return ctx.enter_context(nc.sbuf_tensor(tag + name, shape, dt))

        def bank(name):
            return ctx.enter_context(nc.psum_tensor(tag + name, [P, 512], F32))

        def sem(name):
            used.append(nc.alloc_semaphore(tag + name))
            return used[-1]

        ident, before, ones = sb("ident", [P, P]), sb("before", [P, P]), sb("ones", [P, P])
        iota = sb("iota", [P, 3 * E + 1])
        expert_no, list_start, upto, tile_no = iota[:, 0:E], iota[:, E:2 * E], iota[:, 2 * E:3 * E], iota[:, 3 * E:3 * E + 1]
        pair_no = sb("pair_no", [P, TOK * TOPK // P], I32)
        wr_raw, wr, rscale = sb("wr_raw", [P, FC, E]), sb("wr", [P, FC, E]), sb("rscale", [P, FC])
        escale, gate_t = sb("escale", [P, E]), sb("gate_t", [P, 1])
        empty, blank = sb("empty", [P, SLOTS // P], I32), sb("blank", [P, D])
        x_sb, xn = sb("x_sb", [P, 2, QT, D]), sb("xn", [P, 2, QT, D])
        stats, mv = sb("stats", [P, QT, 6]), sb("mv", [P, QT, 2])
        rstd, var2, r2 = sb("rstd", [P, QT]), sb("var2", [P, QT]), sb("r2", [P, QT])
        root = [sb(f"root{n}", [P, QT]) for n in range(3)]
        xt = sb("xt", [P, 2, FC, P])
        logits, best, best_no = sb("logits", [P, QT, E]), sb("best", [P, QT, 8]), sb("best_no", [P, QT, 8], U32)
        no_f, gap, odds, share = sb("no_f", [P, QT, 2]), sb("gap", [P, QT]), sb("odds", [P, QT]), sb("share", [P, QT, 2])
        hot, picked, total = sb("hot", [P, QT, 2, E]), sb("picked", [P, QT, E]), sb("total", [P, E])
        rank, scratch = sb("rank", [P, QT, E]), sb("scratch", [P, QT, 2, E])
        pos_f, scale_of = sb("pos_f", [P, QT, 2]), sb("scale_of", [P, QT, 2])
        pair, pos_here = sb("pair", [P, 2, QT, 2], I32), sb("pos_here", [P, 2, QT, 2], I32)
        count, count_i, tiles, tiles_rep = sb("count", [P, 1]), sb("count_i", [P, 1], I32), sb("tiles", [P, 1]), sb("tiles_rep", [P, P])
        credit = sb("credit", [P, 4])
        cum, below, start = sb("cum", [P, E]), sb("below", [P, E]), sb("start", [P, E])
        tab_f, tab_i = sb("tab_f", [P, 4]), sb("tab_i", [P, 2], I32)

        tb = [bank("tb0"), bank("tb1")]
        lb, rb, cb = bank("lb"), bank("rb"), bank("cb")

        c_loaded, blank_done, cleared, x_loaded = sem("c_loaded"), sem("blank_done"), sem("cleared"), [sem("x_loaded0"), sem("x_loaded1")]
        gate_done, wr_done = sem("gate_done"), sem("wr_done")
        link_done, xn_done, xn_stored = sem("link_done"), sem("xn_done"), [sem("xn_stored0"), sem("xn_stored1")]
        t_ready, t_done, l_ready = sem("t_ready"), sem("t_done"), sem("l_ready")
        gap_done, odds_done, picked_done, rank_ready, pos_done = sem("gap_done"), sem("odds_done"), sem("picked_done"), sem("rank_ready"), sem("pos_done")
        listed, list_free, count_ready, tiles_done, cum_ready, tab_link, tab_done, tab_stored = (
            sem("listed"), sem("list_free"), sem("count_ready"), sem("tiles_done"), sem("cum_ready"), sem("tab_link"), sem("tab_done"), sem("tab_stored"))

        block = ctx.enter_context(nc.Block())
        LISTED = 16 * 2 * QT

        def rows(i):
            return bass.ds(i * QT * P, QT * P)

        @block.sync
        def _(sp):
            for dst, src in ((ident[:], identity), (before[:], earlier), (iota[:], iotas), (wr_raw[:], logits_w), (rscale[:], router_scale),
                             (escale[:], expert_scale), (gate_t[:], gate), (pair_no[:], pairs), (empty[:], empty_list)):
                sp.dma_start(dst, src).then_inc(c_loaded, 16)
            sp.wait_ge(c_loaded, 16 * 9)
            sp.dma_start(slot_tokens.rearrange("(p s) o -> p (s o)", p=P), empty[:]).then_inc(cleared, 16)
            sp.wait_ge(blank_done, 1)
            sp.dma_start(xn_out[TOK:TOK + P, :], blank[:]).then_inc(cleared, 16)
            with sp.Fori(0, TURNS // 2) as i:
                for b in range(2):
                    sp.wait_ge(xn_done, 2 * i + b + 1)
                    sp.nop(nofuse=True)
                    sp.dma_start(x_sb[:, b], x_in[rows(2 * i + b), :].rearrange("(t p) d -> p t d", p=P)).then_inc(x_loaded[b], 16)
            sp.wait_ge(tab_done, 1)
            sp.dma_start(tile_table, tab_i[:]).then_inc(tab_stored, 16)
            sp.wait_ge(tab_stored, 16)

        @block.tensor
        def _(pe):
            def logits_of(turn, t):
                pe.wait_ge(t_done, QT * turn + t + 3)
                for c in range(FC):
                    mm = nc.tensor.matmul(lb[:, t * E:(t + 1) * E], xt[:, t % 2, c], wr[:, c], start=(c == 0), stop=(c == FC - 1))
                if t == QT - 1:
                    mm.then_inc(l_ready, 1)

            pe.wait_ge(c_loaded, 16 * 9)
            pe.wait_ge(wr_done, 1)
            with pe.Fori(0, TURNS // 2) as i:
                for b in range(2):
                    turn = 2 * i + b
                    pe.wait_ge(xn_done, turn + 3)
                    for t in range(QT):
                        pe.wait_ge(t_done, QT * turn + t + 1)
                        for c in range(FC):
                            mm = nc.tensor.transpose(tb[t % 2][:, c * P:(c + 1) * P], xn[:, b, t, c * P:(c + 1) * P], ident[:])
                        mm.then_inc(t_ready, 1)
                        if t >= 1:
                            logits_of(turn, t - 1)
                    logits_of(turn, QT - 1)
                    pe.wait_ge(picked_done, turn + 1)
                    for t in range(QT):
                        out = rb[:, t * E:(t + 1) * E]
                        nc.tensor.matmul(out, before[:], picked[:, t], start=True, stop=False)
                        for u in range(t):
                            nc.tensor.matmul(out, ones[:], picked[:, u], start=False, stop=False)
                        mm = nc.tensor.matmul(out, ones[:], total[:], start=False, stop=True)
                    mm.then_inc(rank_ready, 1)
            pe.wait_ge(pos_done, TURNS + 1)
            nc.tensor.matmul(cb[0:E, 0:1], total[:], ones[:, 0:1], start=True, stop=True).then_inc(count_ready, 1)
            pe.wait_ge(tiles_done, 1)
            nc.tensor.matmul(cb[:, E:2 * E], tiles_rep[0:E, :], upto[0:E, :], start=True, stop=True).then_inc(cum_ready, 1)

        @block.scalar
        def _(act):
            act.wait_ge(c_loaded, 16 * 9)
            nc.scalar.activation(gate_t[:], gate_t[:], ACT.Tanh).then_inc(gate_done, 1)
            with act.Fori(0, TURNS // 2) as i:
                for b in range(2):
                    turn = 2 * i + b
                    act.wait_ge(xn_done, turn + 3)
                    act.dma_start(xn_out[rows(turn), :].rearrange("(t p) d -> p t d", p=P), xn[:, b]).then_inc(xn_stored[b], 16)
                    for t in range(QT):
                        act.wait_ge(t_ready, QT * turn + t + 1)
                        nc.scalar.copy(xt[:, t % 2], tb[t % 2][:].rearrange("p (c s) -> p c s", c=FC)).then_inc(t_done, 1)
                    act.wait_ge(gap_done, turn + 1)
                    nc.scalar.activation(odds[:], gap[:], ACT.Exp).then_inc(odds_done, 1)
            for b in range(2):
                act.wait_ge(xn_stored[b], 16 * (TURNS // 2) + 16)

        @block.gpsimd
        def _(pool):
            nc.gpsimd.memset(blank[:], 0.0).then_inc(blank_done, 1)
            pool.wait_ge(cleared, 32)
            with pool.Fori(0, TURNS // 2) as i:
                for b in range(2):
                    turn = 2 * i + b
                    for t in range(QT):
                        for k in range(2):
                            if (t, k) == (0, 0):
                                pool.wait_ge(pos_done, turn + 2)
                                pool.nop(nofuse=True)
                            pool.indirect_dma_start(out=slot_tokens, out_offset=bass.IndirectOffsetOnAxis(ap=pos_here[:, b, t, k:k + 1], axis=0),
                                                    in_=pair[:, b, t, k:k + 1], in_offset=None).then_inc(listed, 16)
                    pool.wait_ge(listed, LISTED * (turn + 1))
                    pool.nop(nofuse=True).then_inc(list_free, 1)

        LINKS = 24 + 2 * ROOT_LINKS

        @block.vector
        def _(dve):
            V = nc.vector
            V.memset(total[:], 0.0).then_inc(xn_done, 2)
            V.memset(ones[:], 1.0).then_inc(t_done, 2)
            V.memset(credit[:, 0:1], 0.0).then_inc(xn_stored[0], 16)
            V.memset(credit[:, 1:2], 0.0).then_inc(xn_stored[1], 16)
            V.memset(credit[:, 2:3], 0.0).then_inc(pos_done, 1)
            V.memset(credit[:, 3:4], 0.0).then_inc(list_free, 2)
            dve.wait_ge(c_loaded, 16 * 9)
            for c in range(FC):
                w = V.tensor_scalar(wr[:, c], wr_raw[:, c], rscale[:, c:c + 1], float(D) ** -0.5, ALU.mult, ALU.mult)
            w.then_inc(wr_done, 1)
            dve.wait_ge(gate_done, 1)

            with dve.Fori(0, TURNS // 2) as i:
                for b in range(2):
                    turn = 2 * i + b
                    done = [0]

                    def link(op):
                        op.then_inc(link_done, 1)
                        done[0] += 1
                        dve.wait_ge(link_done, LINKS * turn + done[0])
                        dve.nop(nofuse=True)

                    dve.wait_ge(x_loaded[b], 16 * i + 16)
                    for t in range(QT):
                        op = V.bn_stats(stats[:, t], x_sb[:, b, t])
                    link(op)
                    for t in range(QT):
                        op = V.bn_aggr(mv[:, t], stats[:, t])
                    link(op)
                    inverse_root(dve, V, link_done, LINKS * turn + done[0], mv[:, :, 1], LN_EPS, root, rstd[:])
                    done[0] += ROOT_LINKS
                    dve.wait_ge(xn_stored[b], 16 * i + 16)
                    for t in range(QT):
                        op = V.tensor_scalar(xn[:, b, t], x_sb[:, b, t], mv[:, t, 0:1], rstd[:, t:t + 1], ALU.subtract, ALU.mult)
                    op.then_inc(xn_done, 1)
                    link(V.tensor_tensor(var2[:], mv[:, :, 1], rstd[:], ALU.mult))
                    link(V.tensor_tensor(var2[:], var2[:], rstd[:], ALU.mult))
                    inverse_root(dve, V, link_done, LINKS * turn + done[0], var2[:], ROUTER_EPS, root, r2[:])
                    done[0] += ROOT_LINKS
                    dve.wait_ge(l_ready, turn + 1)
                    for t in range(QT):
                        op = V.tensor_scalar(logits[:, t], lb[:, t * E:(t + 1) * E], r2[:, t:t + 1], None, ALU.mult)
                    link(op)
                    for t in range(QT):
                        op = V.max(best[:, t], logits[:, t])
                    link(op)
                    V.tensor_tensor(gap[:], best[:, :, 1], best[:, :, 0], ALU.subtract).then_inc(gap_done, 1)
                    for t in range(QT):
                        op = V.max_index(best_no[:, t], best[:, t], logits[:, t])
                    link(op)
                    link(V.tensor_copy(no_f[:], best_no[:, :, 0:2]))
                    for t in range(QT):
                        for k in range(2):
                            op = V.tensor_scalar(hot[:, t, k], expert_no, no_f[:, t, k:k + 1], None, ALU.is_equal)
                    link(op)
                    V.tensor_tensor(picked[:], hot[:, :, 0], hot[:, :, 1], ALU.add).then_inc(picked_done, 1)
                    dve.wait_ge(odds_done, turn + 1)
                    link(V.tensor_scalar(gap[:], odds[:], 1.0, None, ALU.add))
                    link(V.reciprocal(share[:, :, 0], gap[:]))
                    link(V.tensor_tensor(share[:, :, 1], share[:, :, 0], odds[:], ALU.mult))
                    for t in range(QT):
                        for k in range(2):
                            op = V.tensor_tensor(scratch[:, t, k], hot[:, t, k], escale[:], ALU.mult)
                    link(op)
                    link(V.tensor_reduce(scale_of[:], scratch[:], AX.X, ALU.add))
                    link(V.tensor_tensor(share[:], share[:], scale_of[:], ALU.mult))
                    op = V.tensor_scalar(weights[:, bass.ds(turn * 2 * QT, 2 * QT)], share[:].rearrange("p t k -> p (t k)"), gate_t[:, 0:1], None, ALU.mult)
                    link(op)
                    dve.wait_ge(rank_ready, turn + 1)
                    for t in range(QT):
                        op = V.tensor_tensor(rank[:, t], rb[:, t * E:(t + 1) * E], list_start, ALU.add)
                    link(op)
                    for t in range(QT):
                        for k in range(2):
                            op = V.tensor_tensor(scratch[:, t, k], hot[:, t, k], rank[:, t], ALU.mult)
                    link(op)
                    link(V.tensor_reduce(pos_f[:], scratch[:], AX.X, ALU.add))
                    for t in range(QT):
                        link(V.tensor_tensor(total[:], total[:], picked[:, t], ALU.add))
                    dve.wait_ge(list_free, turn + 1)
                    link(V.tensor_copy(pos_here[:, b], pos_f[:]))
                    V.tensor_copy(pair[:, b].rearrange("p t k -> p (t k)"), pair_no[:, bass.ds(turn * 2 * QT, 2 * QT)]).then_inc(pos_done, 1)
                    assert done[0] == LINKS, done[0]
            dve.wait_ge(count_ready, 1)
            made = [0]

            def last(op):
                op.then_inc(tab_link, 1)
                made[0] += 1
                dve.wait_ge(tab_link, made[0])

            last(V.tensor_scalar(count[0:E, :], cb[0:E, 0:1], float(TILE - 1), None, ALU.add))
            last(V.tensor_copy(count_i[0:E, :], count[0:E, :]))
            last(V.tensor_scalar(count_i[0:E, :], count_i[0:E, :], TILE.bit_length() - 1, None, ALU.logical_shift_right))
            last(V.tensor_copy(tiles[0:E, :], count_i[0:E, :]))
            V.tensor_scalar(tiles_rep[0:E, :], ones[0:E, :], tiles[0:E, :], None, ALU.mult).then_inc(tiles_done, 1)
            dve.wait_ge(cum_ready, 1)
            last(V.tensor_copy(cum[:], cb[:, E:2 * E]))
            last(V.tensor_scalar(below[:], cum[:], tile_no, None, ALU.is_le))
            last(V.tensor_tensor(start[:], cum[:], below[:], ALU.mult))
            last(V.tensor_reduce(tab_f[:, 0:1], below[:], AX.X, ALU.add))
            last(V.tensor_reduce(tab_f[:, 1:2], start[:], AX.X, ALU.max))
            last(V.tensor_tensor(tab_f[:, 2:3], tile_no, tab_f[:, 1:2], ALU.subtract))
            last(V.tensor_scalar(tab_f[:, 2:3], tab_f[:, 2:3], float(TILE), None, ALU.mult))
            last(V.tensor_scalar(tab_f[:, 3:4], tab_f[:, 0:1], float(TOK), tab_f[:, 2:3], ALU.mult, ALU.add))
            last(V.tensor_scalar(tab_f[:, 0:1], tab_f[:, 0:1], float(E - 1), None, ALU.min))
            last(V.tensor_copy(tab_i[:, 0:1], tab_f[:, 0:1]))
            V.tensor_copy(tab_i[:, 1:2], tab_f[:, 3:4]).then_inc(tab_done, 1)
    clear(nc, used)


def experts(nc, xn_rows, slot_tokens, tile_table, w_gate, w_out, y_rows, identity, tag):
    FC, HC, TT = D // P, H0 // P, TILE // P
    WCOL = 2 * H0 + D
    TURNS = (TILES + 1) // 2
    used = []
    with ExitStack() as ctx:
        def sb(name, shape, dt=F32):
            return ctx.enter_context(nc.sbuf_tensor(tag + name, shape, dt))

        def bank(name):
            return ctx.enter_context(nc.psum_tensor(tag + name, [P, 512], F32))

        def sem(name):
            used.append(nc.alloc_semaphore(tag + name))
            return used[-1]

        ident = sb("ident", [P, P])
        table = sb("table", [1, 2 * P], I32)
        pairs, ids, rows = sb("pairs", [P, 2, TT], I32), sb("ids", [P, 2, TT], I32), sb("rows", [P, 2, TT], I32)
        xg = sb("xg", [P, 2, TT, D])
        xt_hi, xt_lo = sb("xt_hi", [P, 2, FC, TILE], F32R), sb("xt_lo", [P, 2, FC, TILE], F32R)
        w_raw = sb("w_raw", [P, 2, FC, WCOL])
        w_hi, w_lo = sb("w_hi", [P, 2, FC, WCOL], F32R), sb("w_lo", [P, 2, FC, WCOL], F32R)
        gelu = sb("gelu", [P, 2, TILE])
        act_f = sb("act_f", [P, HC, TILE])
        act_hi, act_lo = sb("act_hi", [P, HC, TILE], F32R), sb("act_lo", [P, HC, TILE], F32R)
        y_sb = sb("y_sb", [P, 2, TT, D])
        credit = sb("credit", [P, 8])
        zeros = sb("zeros", [P, TILE])

        tb = [bank("tb0"), bank("tb1")]
        gb = [bank(f"gb{h}") for h in range(HC)]
        ob = [bank(f"ob{t}") for t in range(TT)]

        id_loaded, tab_loaded = sem("id_loaded"), sem("tab_loaded")
        pairs_loaded, x_loaded, w_loaded = ([sem(f"{n}{b}") for b in range(2)] for n in ("pairs_loaded", "x_loaded", "w_loaded"))
        t_ready, xt_hid, xt_lod = sem("t_ready"), sem("xt_hid"), sem("xt_lod")
        w_hid, w_lod = sem("w_hid"), sem("w_lod")
        g_ready, gelu_done, act_done, act_hid, act_lod = sem("g_ready"), sem("gelu_done"), sem("act_done"), sem("act_hid"), sem("act_lod")
        y_ready, y_done, y_stored, y_free = sem("y_ready"), sem("y_done"), sem("y_stored"), sem("y_free")
        ids_done, rows_done = sem("ids_done"), sem("rows_done")

        def piece(w, b, q):
            return w[:, b, q]

        block = ctx.enter_context(nc.Block())

        @block.sync
        def _(sp):
            sp.dma_start(ident[:], identity).then_inc(id_loaded, 16)
            sp.dma_start(table[:], tile_table.rearrange("t c -> (t c)").unsqueeze(0)).then_inc(tab_loaded, 16)
            sp.wait_ge(tab_loaded, 16)

            def fetch(n, b):
                e = sp.value_load(table[0:1, bass.ds(2 * n, 1)], min_val=0, max_val=E - 1)
                place = sp.value_load(table[0:1, bass.ds(2 * n + 1, 1)], min_val=0, max_val=SLOTS - TILE)
                sp.wait_ge(w_lod, FC * (n + 1))
                sp.nop(nofuse=True)
                sp.dma_start(w_raw[:, b, :, 0:2 * H0], w_gate[bass.ds(e, 1)].rearrange("o (c p) n -> p (o c) n", p=P)).then_inc(w_loaded[b], 16)
                sp.dma_start(w_raw[:, b, :, 2 * H0:], w_out[bass.ds(e, 1)].rearrange("o (c p) n -> p (o c) n", p=P)).then_inc(w_loaded[b], 16)
                sp.wait_ge(rows_done, n + 1)
                sp.nop(nofuse=True)
                sp.dma_start(pairs[:, b], slot_tokens[bass.ds(place, TILE), :].rearrange("(p t) o -> p (t o)", p=P)).then_inc(pairs_loaded[b], 16)

            fetch(0, 0)
            fetch(1, 1)
            with sp.Fori(0, TURNS) as i:
                fetch(2 * i + 2, 0)
                fetch(2 * i + 3, 1)
            for b in range(2):
                sp.wait_ge(pairs_loaded[b], 16 * (TURNS + 1))
                sp.wait_ge(w_loaded[b], 32 * (TURNS + 1))

        @block.gpsimd
        def _(pool):
            def gather(n, b):
                pool.wait_ge(ids_done, n + 1)
                pool.nop(nofuse=True)
                pool.wait_ge(t_ready, 2 * (n + 1))
                pool.nop(nofuse=True)
                for t in range(TT):
                    pool.indirect_dma_start(out=xg[:, b, t], out_offset=None, in_=xn_rows,
                                            in_offset=bass.IndirectOffsetOnAxis(ap=ids[:, b, t:t + 1], axis=0)).then_inc(x_loaded[b], 16)

            def scatter(n, b):
                pool.wait_ge(rows_done, n + 3)
                pool.nop(nofuse=True)
                pool.wait_ge(y_done, n + 2)
                pool.nop(nofuse=True)
                for t in range(TT):
                    pool.indirect_dma_start(out=y_rows, out_offset=bass.IndirectOffsetOnAxis(ap=rows[:, b, t:t + 1], axis=0),
                                            in_=y_sb[:, b, t], in_offset=None).then_inc(y_stored, 16)
                pool.wait_ge(y_stored, 32 * (n + 1))
                pool.nop(nofuse=True).then_inc(y_free, 1)

            def split(n):
                for h in range(HC):
                    pool.wait_ge(act_done, HC * (n + 1) + h + 1)
                    if h == 0:
                        pool.wait_ge(y_ready, n + 1)
                    nc.gpsimd.tensor_tensor(act_hi[:, h], act_f[:, h], zeros[:], ALU.add).then_inc(act_hid, 1)
                    pool.wait_ge(act_hid, HC * n + h + 1)
                    nc.gpsimd.tensor_tensor(act_lo[:, h], act_f[:, h], act_hi[:, h].bitcast(F32), ALU.subtract).then_inc(act_lod, 1)

            nc.gpsimd.memset(zeros[:], 0.0).then_inc(t_ready, 4)
            nc.gpsimd.memset(credit[:, 7:8], 0.0).then_inc(act_lod, HC)
            pool.wait_ge(t_ready, 4)
            gather(0, 0)
            gather(1, 1)
            with pool.Fori(0, TURNS) as i:
                for b in range(2):
                    split(2 * i + b)
                    gather(2 * i + b + 2, b)
                    scatter(2 * i + b, b)
            for b in range(2):
                pool.wait_ge(x_loaded[b], 32 * (TURNS + 1))

        @block.tensor
        def _(pe):
            def three(out, a_hi, a_lo, b_hi, b_lo, start, stop):
                nc.tensor.matmul(out, a_hi, b_hi, start=start, stop=False)
                nc.tensor.matmul(out, a_hi, b_lo, start=False, stop=False)
                return nc.tensor.matmul(out, a_lo, b_hi, start=False, stop=stop)

            def turn(n, b, count):
                pe.wait_ge(x_loaded[b], 32 * count)
                for j in range(2):
                    pe.wait_ge(xt_lod, 2 * n + j + 1)
                    out = tb[j][:].rearrange("p (c s) -> p c s", c=2)
                    for c in range(2):
                        for t in range(TT):
                            mm = nc.tensor.transpose(out[:, c, t * P:(t + 1) * P], xg[:, b, t, (2 * j + c) * P:(2 * j + c + 1) * P], ident[:])
                    mm.then_inc(t_ready, 1)

            def gate_up(n, b):
                pe.wait_ge(xt_lod, 2 * n + 4)
                pe.wait_ge(w_lod, FC * (n + 3))
                for h in range(HC):
                    pe.wait_ge(act_done, HC * n + h + 1)
                    for k in range(2):
                        out = gb[h][:, k * TILE:(k + 1) * TILE]
                        w = k * H0 + h * P
                        for c in range(FC):
                            mm = three(out, w_hi[:, b, c, w:w + P], w_lo[:, b, c, w:w + P], xt_hi[:, b, c], xt_lo[:, b, c], c == 0, c == FC - 1)
                    mm.then_inc(g_ready, 1)

            def down(n, b):
                pe.wait_ge(y_done, n + 1)
                pe.wait_ge(act_lod, HC * (n + 2))
                for t in range(TT):
                    for h in range(HC):
                        mm = three(ob[t][:], act_hi[:, h, t * P:(t + 1) * P], act_lo[:, h, t * P:(t + 1) * P],
                                   w_hi[:, b, h, 2 * H0:], w_lo[:, b, h, 2 * H0:], h == 0, h == HC - 1)
                mm.then_inc(y_ready, 1)

            pe.wait_ge(id_loaded, 16)
            turn(0, 0, 1)
            with pe.Fori(0, TURNS) as i:
                gate_up(2 * i, 0)
                turn(2 * i + 1, 1, i + 1)
                down(2 * i, 0)
                gate_up(2 * i + 1, 1)
                turn(2 * i + 2, 0, i + 2)
                down(2 * i + 1, 1)

        @block.scalar
        def _(act):
            def w_high(n, b, q, count):
                act.wait_ge(w_loaded[b], 32 * count)
                nc.scalar.copy(piece(w_hi, b, q), piece(w_raw, b, q)).then_inc(w_hid, 1)

            def turned(n, b):
                for j in range(2):
                    act.wait_ge(t_ready, 2 * n + j + 5)
                    nc.scalar.copy(xt_hi[:, b, 2 * j:2 * j + 2], tb[j][:].rearrange("p (c s) -> p c s", c=2)).then_inc(xt_hid, 1)

            def tile(n, b, count):
                for h in range(HC):
                    act.wait_ge(g_ready, HC * n + h + 1)
                    act.wait_ge(act_done, HC * n + h + 3)
                    nc.scalar.activation(gelu[:, h % 2], gb[h][:, 0:TILE], ACT.Gelu_apprx_tanh).then_inc(gelu_done, 1)
                    w_high(n + 1, 1 - b, h, count + b)
                turned(n + 1, 1 - b)
                act.wait_ge(y_ready, n + 2)
                act.wait_ge(y_free, n + 1)
                for t in range(TT):
                    y = nc.scalar.copy(y_sb[:, b, t], ob[t][:])
                y.then_inc(y_done, 1)

            for q in range(FC):
                w_high(0, 0, q, 1)
            turned(0, 0)
            with act.Fori(0, TURNS) as i:
                tile(2 * i, 0, i + 1)
                tile(2 * i + 1, 1, i + 1)

        @block.vector
        def _(dve):
            def low(out, raw, hi):
                return nc.vector.tensor_tensor(out, raw, hi.bitcast(F32), ALU.subtract)

            def w_low(n, b, q):
                dve.wait_ge(w_hid, FC * n + q + 1)
                low(piece(w_lo, b, q), piece(w_raw, b, q), piece(w_hi, b, q)).then_inc(w_lod, 1)

            def turned(n, b):
                for j in range(2):
                    dve.wait_ge(xt_hid, 2 * n + j + 1)
                    low(xt_lo[:, b, 2 * j:2 * j + 2], tb[j][:].rearrange("p (c s) -> p c s", c=2), xt_hi[:, b, 2 * j:2 * j + 2]).then_inc(xt_lod, 1)

            def tokens(n, b, count):
                dve.wait_ge(pairs_loaded[b], 16 * count)
                dve.wait_ge(t_ready, 2 * n + 2)
                nc.vector.tensor_scalar(ids[:, b], pairs[:, b], 1, None, ALU.arith_shift_right).then_inc(ids_done, 1)

            def tile(n, b, count):
                for h in range(HC):
                    dve.wait_ge(gelu_done, HC * n + h + 1)
                    dve.wait_ge(act_lod, HC * n + h + 1)
                    nc.vector.tensor_tensor(act_f[:, h], gb[h][:, TILE:], gelu[:, h % 2], ALU.mult).then_inc(act_done, 1)
                    w_low(n + 1, 1 - b, h)
                    if h == 1:
                        dve.wait_ge(y_free, n + 1)
                        nc.vector.tensor_copy(rows[:, b], pairs[:, b]).then_inc(rows_done, 1)
                turned(n + 1, 1 - b)
                tokens(n + 2, b, count + 1)

            nc.vector.memset(credit[:, 0:1], 0.0).then_inc(w_lod, 2 * FC)
            nc.vector.memset(credit[:, 1:2], 0.0).then_inc(act_done, HC)
            nc.vector.memset(credit[:, 2:3], 0.0).then_inc(xt_lod, 2)
            nc.vector.memset(credit[:, 3:4], 0.0).then_inc(y_done, 1)
            nc.vector.memset(credit[:, 4:5], 0.0).then_inc(y_ready, 1)
            nc.vector.memset(credit[:, 5:6], 0.0).then_inc(y_free, 2)
            nc.vector.memset(credit[:, 6:7], 0.0).then_inc(rows_done, 2)
            tokens(0, 0, 1)
            tokens(1, 1, 1)
            for q in range(FC):
                w_low(0, 0, q)
            turned(0, 0)
            with dve.Fori(0, TURNS) as i:
                tile(2 * i, 0, i + 1)
                tile(2 * i + 1, 1, i + 1)
    clear(nc, used)


def gated_normed_attention(nc, x_in, y_rows, weights, x_out, ctx_t, gate, wq, wkv, wkv_dca, wo, bq, bkv, ln_w, ln_b, bo, identity, tag):
    FC, CC, HD = D // P, DC // P, D // NHEAD1
    SCALE = HD ** -0.5
    PAIR = 2 * NHEAD1
    HG = P // HD
    GROUPS = NHEAD1 // HG
    LINKS = 9 + 2 * ROOT_LINKS
    ST = 3 * HD
    used = []
    with ExitStack() as ctx:
        def sb(name, shape, dt=F32):
            return ctx.enter_context(nc.sbuf_tensor(tag + name, shape, dt))

        def bank(name):
            return ctx.enter_context(nc.psum_tensor(tag + name, [P, 512], F32))

        def sem(name):
            used.append(nc.alloc_semaphore(tag + name))
            return used[-1]

        wq_hi, wq_lo = sb("wq_hi", [P, FC, D], F32R), sb("wq_lo", [P, FC, D], F32R)
        wkv_hi, wkv_lo = sb("wkv_hi", [P, CC, 2 * D], F32R), sb("wkv_lo", [P, CC, 2 * D], F32R)
        wd_hi, wd_lo = sb("wd_hi", [P, CC, 2 * D], F32R), sb("wd_lo", [P, CC, 2 * D], F32R)
        wo_hi, wo_lo = sb("wo_hi", [P, FC, D], F32R), sb("wo_lo", [P, FC, D], F32R)
        ident = sb("ident", [P, P])
        bq_sb, bkv_sb, bo_sb = sb("bq_sb", [P, D]), sb("bkv_sb", [P, 2, 2 * D]), sb("bo_sb", [P, D])
        lnw_sb, lnb_sb = sb("lnw_sb", [P, 4, HD]), sb("lnb_sb", [P, 4, HD])
        gate_t = sb("gate_t", [P, 1])
        x_sb = sb("x_sb", [P, 2, 2, D])
        y_sb = sb("y_sb", [P, 2, 2, D])
        w_here = sb("w_here", [P, 4])
        stats, mv, rstd = sb("stats", [P, 2, 6]), sb("mv", [P, 2, 2]), sb("rstd", [P, 2])
        root = [sb(f"root{n}", [P, 2]) for n in range(3)]
        xt_hi, xt_lo = sb("xt_hi", [P, FC, S], F32R), sb("xt_lo", [P, FC, S], F32R)
        ctx_raw = sb("ctx_raw", [P, CC, S])
        ctx_hi, ctx_lo = sb("ctx_hi", [P, CC, S], F32R), sb("ctx_lo", [P, CC, S], F32R)
        dca_hi, dca_lo = sb("dca_hi", [P, CC, P], F32R), sb("dca_lo", [P, CC, P], F32R)
        nrm = sb("nrm", [P, 2, 4, D])
        sq = sb("sq", [P, 4, D])
        xn = sq[:, 0:2]
        hsum, hmean, hvar, hrstd = sb("hsum", [P, 4 * NHEAD1]), sb("hmean", [P, 4 * NHEAD1]), sb("hvar", [P, 4 * NHEAD1]), sb("hrstd", [P, 4 * NHEAD1])
        hroot = [sb(f"hroot{n}", [P, 4 * NHEAD1]) for n in range(3)]
        v_raw = sb("v_raw", [P, 2, D])
        v_hi, v_lo = sb("v_hi", [P, 2, NHEAD1, P], F32R), sb("v_lo", [P, 2, NHEAD1, P], F32R)
        stack = sb("stack", [P, 2, 4, HG, ST])
        qk = sb("qk", [ST, 2, 2 * S], F32R)
        prob = sb("prob", [P, 2, 2, S])
        mx, nbias = sb("mx", [P, 2, 2, 2]), sb("nbias", [P, 2, 2, 2])
        rsum, rinv = sb("rsum", [P, 2, 2, 2]), sb("rinv", [P, 2, 2, 2])
        pt_hi, pt_lo = sb("pt_hi", [P, 2, 2, S], F32R), sb("pt_lo", [P, 2, 2, S], F32R)
        ot_hi, ot_lo = sb("ot_hi", [P, 2, S], F32R), sb("ot_lo", [P, 2, S], F32R)
        credit = sb("credit", [P, 4])

        pjb, qkb = bank("pjb"), bank("qkb")
        sc = [bank("sc0"), bank("sc1")]
        ptb, avb = bank("ptb"), bank("avb")
        ob = [bank("ob0"), bank("ob1")]

        c_loaded, w_loaded, w_hid, w_lod = sem("c_loaded"), [sem("w_loaded0"), sem("w_loaded1")], sem("w_hid"), sem("w_lod")
        gate_done, zeroed = sem("gate_done"), sem("zeroed")
        x_loaded, x_stored, ctx_loaded, y_loaded = [sem("x_loaded0"), sem("x_loaded1")], [sem("x_stored0"), sem("x_stored1")], sem("ctx_loaded"), sem("y_loaded")
        y_used, link_done, xn_done, ctx_hid, ctx_lod = sem("y_used"), sem("link_done"), sem("xn_done"), sem("ctx_hid"), sem("ctx_lod")
        pj_ready, pj_hid, pj_taken = sem("pj_ready"), sem("pj_hid"), sem("pj_taken")
        mean_done, cent_done, sq_done, nrm_link, nrm_done = (
            sem("mean_done"), sem("cent_done"), sem("sq_done"), sem("nrm_link"), sem("nrm_done"))
        st_hid, st_done, v_hid, v_done = sem("st_hid"), sem("st_done"), sem("v_hid"), sem("v_done")
        qk_ready, qk_done = sem("qk_ready"), sem("qk_done")
        s_ready, s_max, s_bias, e_done, r_done, p_done = sem("s_ready"), sem("s_max"), sem("s_bias"), sem("e_done"), sem("r_done"), sem("p_done")
        t_ready, pt_hid, pt_lod = sem("t_ready"), sem("pt_hid"), sem("pt_lod")
        av_ready, ot_hid, ot_lod = sem("av_ready"), sem("ot_hid"), sem("ot_lod")
        o_ready, o_free = sem("o_ready"), sem("o_free")

        pieces = [(wq, wq_hi[:], wq_lo[:]), (wkv, wkv_hi[:], wkv_lo[:]), (wkv_dca, wd_hi[:], wd_lo[:]), (wo, wo_hi[:], wo_lo[:])]
        consts = [(ident[:], identity), (bq_sb[:], bq), (bkv_sb[:], bkv), (bo_sb[:], bo), (lnw_sb[:], ln_w), (lnb_sb[:], ln_b), (gate_t[:], gate)]

        def raw(n):
            a, b = pieces[n][0].shape[1:]
            return nrm[:, n % 2].rearrange("p r d -> p (r d)").rearrange("p (a b) -> p a b", a=a)

        STEPS = range(-1, PAIR + 3)
        N1 = NHEAD1
        AT = {}
        for bb, when in ((0, dict(comb=-1, turn=-1, proj=-1, var=-1, v01=-1, v23=2)),
                         (1, dict(comb=1, turn=3, proj=5, var=9, v01=12, v23=N1 + 3))):
            for what, u in when.items():
                AT.setdefault(u, []).append((what, bb))
            for g in range(GROUPS):
                u = bb * N1 + g * HG - 2
                AT.setdefault(max(u, -1), []).append((g, bb))

        def due(u, what):
            return [bb for w, bb in AT.get(u, []) if w == what]

        def stacks(u):
            return [(bb, w) for w, bb in AT.get(u, []) if isinstance(w, int)]

        def diag(v, g2, h):
            return v[:, :, 2 * g2 * HG:2 * (g2 + 1) * HG].rearrange("p k (g h) c -> p k g h c", h=HG)[:, :, :, h, h * HD:(h + 1) * HD]

        def v_cols(g2, h):
            return v_raw[:, :, 2 * g2 * P:2 * (g2 + 1) * P].rearrange("p k (g c) -> p k g c", c=P)[:, :, :, h * HD:(h + 1) * HD]

        def group_cols(bb, g):
            return nrm[:, bb, :, g * P:(g + 1) * P].rearrange("p r (h c) -> p r h c", h=HG)

        def per_head(x):
            return x[:].unsqueeze(2).to_broadcast([P, 4 * N1, HD])

        block = ctx.enter_context(nc.Block())

        @block.sync
        def _(sp):
            for dst, src in consts:
                sp.dma_start(dst, src).then_inc(c_loaded, 16)
            for n, (src, _, _) in enumerate(pieces):
                if n >= 2:
                    sp.wait_ge(w_lod, n - 1)
                sp.dma_start(raw(n), src).then_inc(w_loaded[n % 2], 16)
            with sp.Fori(0, B // 2) as i:
                for bb in range(2):
                    b = 2 * i + bb
                    sp.wait_ge(x_stored[bb], 16 * i + 16)
                    sp.nop(nofuse=True)
                    sp.dma_start(x_sb[:, bb], x_in[bass.ds(b * S, S), :].rearrange("(t p) d -> p t d", p=P)).then_inc(x_loaded[bb], 16)
                    sp.wait_ge(y_used, b + 1)
                    sp.nop(nofuse=True)
                    sp.dma_start(y_sb[:], y_rows[bass.ds(TOPK * S * b, TOPK * S), :].rearrange("(t p k) d -> p t k d", t=2, k=TOPK)).then_inc(y_loaded, 16)
                    sp.wait_ge(ctx_lod, b + 1)
                    sp.nop(nofuse=True)
                    sp.dma_start(ctx_raw[:], ctx_t[bass.ds(b, 1)].rearrange("o (c p) s -> p (o c) s", p=P)).then_inc(ctx_loaded, 16)

        @block.tensor
        def _(pe):
            def three(out, a_hi, a_lo, b_hi, b_lo, start, stop):
                nc.tensor.matmul(out, a_hi, b_hi, start=start, stop=False)
                nc.tensor.matmul(out, a_hi, b_lo, start=False, stop=False)
                return nc.tensor.matmul(out, a_lo, b_hi, start=False, stop=stop)

            def turn_x(b):
                pe.wait_ge(xn_done, b + 1)
                for j in range(2):
                    pe.wait_ge(pj_taken, 8 * b + j + 1)
                    out = pjb[:].rearrange("p (c s) -> p c s", c=2)
                    for c in range(2):
                        for t in range(2):
                            mm = nc.tensor.transpose(out[:, c, t * P:(t + 1) * P], xn[:, t, (2 * j + c) * P:(2 * j + c + 1) * P], ident[:])
                    mm.then_inc(pj_ready, 1)

            def projections(b):
                for j in range(2, 8):
                    pe.wait_ge(pj_taken, 8 * b + j + 1)
                    t = (j % 2) * P
                    if j < 4:
                        for c in range(FC):
                            mm = three(pjb[:], xt_hi[:, c, t:t + P], xt_lo[:, c, t:t + P], wq_hi[:, c], wq_lo[:, c], c == 0, c == FC - 1)
                    else:
                        w = slice((j - 4) // 2 * D, ((j - 4) // 2 + 1) * D)
                        if j == 4:
                            pe.wait_ge(ctx_lod, b + 2)
                        for c in range(CC):
                            mm = three(pjb[:], ctx_hi[:, c, t:t + P], ctx_lo[:, c, t:t + P], wkv_hi[:, c, w], wkv_lo[:, c, w],
                                       c == 0, c == CC - 1 and t > 0)
                        if t == 0:
                            for c in range(CC):
                                mm = three(pjb[:], dca_hi[:, c], dca_lo[:, c], wd_hi[:, c, w], wd_lo[:, c, w], False, c == CC - 1)
                    mm.then_inc(pj_ready, 1)

            def turn_qk(i, u):
                bb, h = divmod(u, N1)
                pe.wait_ge(st_done, GROUPS * (2 * i + bb) + h // HG + 1)
                pe.wait_ge(qk_done, PAIR * i + u + 1)
                for r in range(4):
                    mm = nc.tensor.transpose(qkb[0:ST, r * P:(r + 1) * P], stack[:, (h // HG) % 2, r, h % HG], ident[:])
                mm.then_inc(qk_ready, 1)

            def scores(i, u):
                pe.wait_ge(qk_done, PAIR * i + u + 2)
                if u >= 2:
                    pe.wait_ge(e_done, PAIR * i + u - 1)
                for t in range(2):
                    mm = nc.tensor.matmul(sc[u % 2][:, t * S:(t + 1) * S], qk[:, u % 2, t * P:(t + 1) * P], qk[:, u % 2, S:], start=True, stop=True)
                mm.then_inc(s_ready, 1)

            def turn_p(i, u):
                pe.wait_ge(p_done, PAIR * i + u + 1)
                if u >= 1:
                    pe.wait_ge(pt_lod, PAIR * i + u)
                out = ptb[:].rearrange("p (k s) -> p k s", k=2)
                for k in range(2):
                    for t in range(2):
                        mm = nc.tensor.transpose(out[:, k, t * P:(t + 1) * P], prob[:, u % 2, t, k * P:(k + 1) * P], ident[:])
                mm.then_inc(t_ready, 1)

            def values(i, u):
                bb, h = divmod(u, N1)
                pe.wait_ge(pt_lod, PAIR * i + u + 1)
                if h % HG == 0:
                    pe.wait_ge(v_done, 2 * (2 * i + bb) + h // (2 * HG) + 1)
                    pe.wait_ge(ot_lod, GROUPS * (2 * i + bb) + h // HG + 1)
                for k in range(2):
                    mm = three(avb[:, 0:S], v_hi[:, k, h], v_lo[:, k, h], pt_hi[:, u % 2, k], pt_lo[:, u % 2, k],
                               h % HG == 0 and k == 0, h % HG == HG - 1 and k == 1)
                mm.then_inc(av_ready, 1)

            def project(i, bb, g):
                pe.wait_ge(ot_lod, GROUPS * (2 * i + bb) + g + 2)
                if g == 0:
                    pe.wait_ge(o_free, 2 * i + bb + 1)
                for t in range(2):
                    mm = three(ob[t][:], ot_hi[:, g % 2, t * P:(t + 1) * P], ot_lo[:, g % 2, t * P:(t + 1) * P], wo_hi[:, g], wo_lo[:, g],
                               g == 0, g == GROUPS - 1)
                if g == GROUPS - 1:
                    mm.then_inc(o_ready, 1)

            pe.wait_ge(c_loaded, 16 * len(consts))
            pe.wait_ge(w_lod, len(pieces))
            pe.wait_ge(zeroed, 3)
            with pe.Fori(0, B // 2) as i:
                for u in STEPS:
                    for bb in due(u, "turn"):
                        turn_x(2 * i + bb)
                    for bb in due(u, "proj"):
                        projections(2 * i + bb)
                    if u + 1 < PAIR:
                        turn_qk(i, u + 1)
                    if 0 <= u < PAIR:
                        scores(i, u)
                    if 0 <= u - 1 < PAIR:
                        turn_p(i, u - 1)
                    if 0 <= u - 2 < PAIR:
                        values(i, u - 2)
                    if 0 <= u - 3 < PAIR and (u - 3) % HG == HG - 1:
                        project(i, (u - 3) // N1, (u - 3) % N1 // HG)

        @block.scalar
        def _(act):
            act.wait_ge(c_loaded, 16 * len(consts))
            nc.scalar.activation(gate_t[:], gate_t[:], ACT.Tanh).then_inc(gate_done, 1)
            for n in range(len(pieces)):
                act.wait_ge(w_loaded[n % 2], 16 * (n // 2 + 1))
                nc.scalar.copy(pieces[n][1], raw(n)).then_inc(w_hid, 1)
            act.wait_ge(zeroed, 3)
            with act.Fori(0, B // 2) as i:
                for u in STEPS:
                    for bb in due(u, "turn"):
                        b = 2 * i + bb
                        act.wait_ge(ctx_loaded, 16 * b + 16)
                        act.wait_ge(pj_taken, 8 * b + 1)
                        nc.scalar.copy(ctx_hi[:, :, DCA:], ctx_raw[:, :, DCA:])
                        nc.scalar.copy(dca_hi[:, :, 0:DCA], ctx_raw[:, :, 0:DCA]).then_inc(ctx_hid, 1)
                        for j in range(2):
                            act.wait_ge(pj_ready, 8 * b + j + 1)
                            nc.scalar.copy(xt_hi[:, 2 * j:2 * j + 2], pjb[:].rearrange("p (c s) -> p c s", c=2)).then_inc(pj_hid, 1)
                    for bb in due(u, "var"):
                        act.wait_ge(cent_done, 2 * i + bb + 1)
                        nc.scalar.activation(sq[:], nrm[:, bb], ACT.Square).then_inc(sq_done, 1)
                    for what, g2 in (("v01", 0), ("v23", 1)):
                        for bb in due(u, what):
                            act.wait_ge(pj_taken, 8 * (2 * i + bb) + 9)
                            if bb == 1:
                                act.wait_ge(av_ready, PAIR * i + N1 - (1 - g2) * 2 * HG)
                            for h in range(HG):
                                v = nc.scalar.copy(diag(v_hi, g2, h), v_cols(g2, h))
                            v.then_inc(v_hid, 1)
                    for bb, g in stacks(u):
                        n = GROUPS * (2 * i + bb) + g
                        act.wait_ge(nrm_done, 2 * i + bb + 1)
                        if (bb, g) not in ((0, 0), (0, 1)):
                            act.wait_ge(qk_ready, PAIR * i + bb * N1 + (g - 1) * HG)
                        out = stack[:, g % 2]
                        nc.scalar.copy(out[:, :, :, 0:HD].bitcast(F32R), group_cols(bb, g))
                        nc.scalar.copy(out[:, 0:2, :, HD:2 * HD].bitcast(F32R), group_cols(bb, g)[:, 0:2])
                        nc.scalar.copy(out[:, 2:4, :, 2 * HD:].bitcast(F32R), group_cols(bb, g)[:, 2:4]).then_inc(st_hid, 1)
                    if u + 1 < PAIR:
                        act.wait_ge(qk_ready, PAIR * i + u + 2)
                        nc.scalar.copy(qk[:, (u + 1) % 2], qkb[0:ST, :]).then_inc(qk_done, 1)
                    if 0 <= u < PAIR:
                        act.wait_ge(s_bias, PAIR * i + u + 1)
                        s = sc[u % 2][:].rearrange("p (t s) -> p t s", t=2)
                        for k, keys in ((0, slice(0, DCA)), (1, slice(DCA, S))):
                            for t in range(2):
                                e = nc.scalar.activation(prob[:, u % 2, t, keys], s[:, t, keys], ACT.Exp, bias=nbias[:, u % 2, k, t:t + 1],
                                                         scale=SCALE, accum_out=rsum[:, u % 2, k, t:t + 1])
                        e.then_inc(e_done, 1)
                    if 0 <= u - 1 < PAIR:
                        act.wait_ge(t_ready, PAIR * i + u)
                        nc.scalar.copy(pt_hi[:, (u - 1) % 2], ptb[:].rearrange("p (k s) -> p k s", k=2)).then_inc(pt_hid, 1)
                    if 0 <= u - 2 < PAIR and (u - 2) % HG == HG - 1:
                        act.wait_ge(av_ready, PAIR * i + u - 1)
                        nc.scalar.copy(ot_hi[:, (u - 2) // HG % 2], avb[:, 0:S]).then_inc(ot_hid, 1)
                    if u - 3 in (N1 - 1, PAIR - 1):
                        bb = (u - 3) // N1
                        act.wait_ge(o_free, 2 * i + bb + 2)
                        act.dma_start(x_out[bass.ds((2 * i + bb) * S, S), :].rearrange("(t p) d -> p t d", p=P), x_sb[:, bb]).then_inc(x_stored[bb], 16)
            for bb in range(2):
                act.wait_ge(x_stored[bb], 16 * (B // 2) + 16)

        @block.gpsimd
        def _(pool):
            T = nc.gpsimd.tensor_tensor
            with pool.Fori(0, B // 2) as i:
                for u in STEPS:
                    for bb in due(u, "proj"):
                        b = 2 * i + bb
                        x = nrm[:, bb].rearrange("p r (h c) -> p (r h) c", h=N1)
                        pool.wait_ge(mean_done, b + 1)
                        T(x, x, per_head(hmean), ALU.subtract).then_inc(cent_done, 1)
                    for bb in due(u, "var"):
                        b = 2 * i + bb
                        x = nrm[:, bb].rearrange("p r (h c) -> p (r h) c", h=N1)
                        pool.wait_ge(link_done, LINKS * (b + 1))
                        T(x, x, per_head(hrstd), ALU.mult).then_inc(nrm_link, 1)
                        for r in range(4):
                            y = nrm[:, bb, r].rearrange("p (h c) -> p h c", h=N1)
                            pool.wait_ge(nrm_link, 5 * b + r + 1)
                            T(y, y, lnw_sb[:, r].unsqueeze(1).to_broadcast([P, N1, HD]), ALU.mult).then_inc(nrm_link, 1)
                        pool.wait_ge(nrm_link, 5 * b + 5)
                        for r in range(4):
                            y = nrm[:, bb, r].rearrange("p (h c) -> p h c", h=N1)
                            l = T(y, y, lnb_sb[:, r].unsqueeze(1).to_broadcast([P, N1, HD]), ALU.add)
                        l.then_inc(nrm_done, 1)
                    if 0 <= u < PAIR:
                        pool.wait_ge(r_done, PAIR * i + u + 1)
                        p = prob[:, u % 2]
                        T(p[:, :, 0:DCA], p[:, :, 0:DCA], rinv[:, u % 2, 0].unsqueeze(2).to_broadcast([P, 2, DCA]), ALU.mult)
                        T(p[:, :, DCA:], p[:, :, DCA:], rinv[:, u % 2, 1].unsqueeze(2).to_broadcast([P, 2, S - DCA]), ALU.mult).then_inc(p_done, 1)

        @block.vector
        def _(dve):
            V = nc.vector
            def low(out, raw_in, hi):
                return V.tensor_tensor(out, raw_in, hi.bitcast(F32), ALU.subtract)

            V.memset(credit[:, 0:1], 0.0).then_inc(x_stored[0], 16)
            V.memset(credit[:, 1:2], 0.0).then_inc(x_stored[1], 16)
            V.memset(credit[:, 2:3], 0.0).then_inc(ctx_lod, 1)
            V.memset(credit[:, 3:4], 0.0).then_inc(pj_taken, 1)
            V.memset(hsum[:], 0.0).then_inc(qk_done, 1)
            V.memset(hvar[:], 0.0).then_inc(ot_lod, 1)
            V.memset(hmean[:], 0.0).then_inc(o_free, 1)
            V.memset(v_hi[:].bitcast(F32), 0.0).then_inc(zeroed, 1)
            V.memset(v_lo[:].bitcast(F32), 0.0)
            V.memset(ctx_hi[:].bitcast(F32), 0.0)
            V.memset(ctx_lo[:].bitcast(F32), 0.0).then_inc(zeroed, 1)
            V.memset(dca_hi[:].bitcast(F32), 0.0)
            V.memset(dca_lo[:].bitcast(F32), 0.0).then_inc(zeroed, 1)
            V.memset(rstd[:], 0.0).then_inc(y_used, 1)
            dve.wait_ge(c_loaded, 16 * len(consts))
            dve.wait_ge(gate_done, 1)
            V.tensor_scalar(bo_sb[:], bo_sb[:], gate_t[:, 0:1], None, ALU.mult).then_inc(zeroed, 1)
            for n in range(len(pieces)):
                dve.wait_ge(w_hid, n + 1)
                low(pieces[n][2], raw(n), pieces[n][1]).then_inc(w_lod, 1)
            dve.wait_ge(zeroed, 4)

            def link(op, at):
                op.then_inc(link_done, 1)
                dve.wait_ge(link_done, at)
                return at

            def combine(i, bb):
                b = 2 * i + bb
                at = LINKS * b
                dve.wait_ge(x_loaded[bb], 16 * i + 16)
                dve.wait_ge(y_loaded, 16 * b + 16)
                V.tensor_copy(w_here[:], weights[:, bass.ds(4 * b, 4)]).then_inc(link_done, 1)
                dve.wait_ge(link_done, at + 1)
                for k in range(TOPK):
                    for t in range(2):
                        l = V.scalar_tensor_tensor(x_sb[:, bb, t], y_sb[:, t, k], w_here[:, 2 * t + k:2 * t + k + 1], x_sb[:, bb, t], ALU.mult, ALU.add)
                    link(l, at + 2 + k)
                dve.nop(nofuse=True).then_inc(y_used, 1)
                for t in range(2):
                    l = V.bn_stats(stats[:, t], x_sb[:, bb, t])
                link(l, at + 4)
                dve.nop(nofuse=True)
                for t in range(2):
                    l = V.bn_aggr(mv[:, t], stats[:, t])
                link(l, at + 5)
                inverse_root(dve, V, link_done, at + 5, mv[:, :, 1], LN_EPS, root, rstd[:])
                for t in range(2):
                    l = V.tensor_scalar(xn[:, t], x_sb[:, bb, t], mv[:, t, 0:1], rstd[:, t:t + 1], ALU.subtract, ALU.mult)
                l.then_inc(xn_done, 1)
                for t in range(2):
                    l = V.tensor_tensor(x_sb[:, bb, t], x_sb[:, bb, t], bo_sb[:], ALU.add)
                link(l, at + 6 + ROOT_LINKS)

            def take(i, bb):
                b = 2 * i + bb
                at = LINKS * b + 6 + ROOT_LINKS
                for j in range(2, 8):
                    dve.wait_ge(pj_ready, 8 * b + j + 1)
                    if j < 4:
                        V.tensor_tensor(nrm[:, bb, j - 2], pjb[:], bq_sb[:], ALU.add).then_inc(pj_taken, 1)
                    elif j < 6:
                        V.tensor_tensor(nrm[:, bb, j - 2], pjb[:], bkv_sb[:, j - 4, 0:D], ALU.add).then_inc(pj_taken, 1)
                    else:
                        V.tensor_tensor(v_raw[:, j - 6], pjb[:], bkv_sb[:, j - 6, D:], ALU.add).then_inc(pj_taken, 1)
                dve.wait_ge(pj_taken, 8 * b + 9)
                link(V.tensor_reduce(hsum[:], nrm[:, bb].rearrange("p r (h c) -> p (r h) c", h=N1), AX.X, ALU.add), at + 1)
                V.tensor_scalar(hmean[:], hsum[:], 1.0 / HD, None, ALU.mult).then_inc(mean_done, 1)

            def variance(i, bb):
                b = 2 * i + bb
                at = LINKS * b + 7 + ROOT_LINKS
                dve.wait_ge(sq_done, b + 1)
                link(V.tensor_reduce(hsum[:], sq[:].rearrange("p r (h c) -> p (r h) c", h=N1), AX.X, ALU.add), at + 1)
                link(V.tensor_scalar(hvar[:], hsum[:], 1.0 / HD, None, ALU.mult), at + 2)
                inverse_root(dve, V, link_done, at + 2, hvar[:], HEAD_EPS, hroot, hrstd[:])

            with dve.Fori(0, B // 2) as i:
                for u in STEPS:
                    if 0 <= u - 1 < PAIR:
                        v = u - 1
                        dve.wait_ge(e_done, PAIR * i + v + 1)
                        V.reciprocal(rinv[:, v % 2], rsum[:, v % 2]).then_inc(r_done, 1)
                    for bb in due(u, "comb"):
                        combine(i, bb)
                    for bb in due(u, "turn"):
                        b = 2 * i + bb
                        dve.wait_ge(ctx_hid, b + 1)
                        low(ctx_lo[:, :, DCA:], ctx_raw[:, :, DCA:], ctx_hi[:, :, DCA:])
                        low(dca_lo[:, :, 0:DCA], ctx_raw[:, :, 0:DCA], dca_hi[:, :, 0:DCA]).then_inc(ctx_lod, 1)
                        for j in range(2):
                            dve.wait_ge(pj_hid, 2 * b + j + 1)
                            low(xt_lo[:, 2 * j:2 * j + 2], pjb[:].rearrange("p (c s) -> p c s", c=2), xt_hi[:, 2 * j:2 * j + 2]).then_inc(pj_taken, 1)
                    for bb in due(u, "proj"):
                        take(i, bb)
                    for bb in due(u, "var"):
                        variance(i, bb)
                    for what, g2 in (("v01", 0), ("v23", 1)):
                        for bb in due(u, what):
                            dve.wait_ge(v_hid, 2 * (2 * i + bb) + g2 + 1)
                            for h in range(HG):
                                l = low(diag(v_lo, g2, h), v_cols(g2, h), diag(v_hi, g2, h))
                            l.then_inc(v_done, 1)
                    for bb, g in stacks(u):
                        n = GROUPS * (2 * i + bb) + g
                        out = stack[:, g % 2]
                        dve.wait_ge(st_hid, n + 1)
                        V.tensor_tensor(out[:, 0:2, :, 2 * HD:], group_cols(bb, g)[:, 0:2], out[:, 0:2, :, 0:HD], ALU.subtract)
                        V.tensor_tensor(out[:, 2:4, :, HD:2 * HD], group_cols(bb, g)[:, 2:4], out[:, 2:4, :, 0:HD], ALU.subtract).then_inc(st_done, 1)
                    if 0 <= u < PAIR:
                        dve.wait_ge(s_ready, PAIR * i + u + 1)
                        s = sc[u % 2][:].rearrange("p (t s) -> p t s", t=2)
                        V.tensor_reduce(mx[:, u % 2, 0], s[:, :, 0:DCA], AX.X, ALU.max)
                        V.tensor_reduce(mx[:, u % 2, 1], s[:, :, DCA:], AX.X, ALU.max).then_inc(s_max, 1)
                        dve.wait_ge(s_max, PAIR * i + u + 1)
                        V.tensor_scalar(nbias[:, u % 2], mx[:, u % 2], -SCALE, None, ALU.mult).then_inc(s_bias, 1)
                    if 0 <= u - 1 < PAIR:
                        dve.wait_ge(pt_hid, PAIR * i + u)
                        low(pt_lo[:, (u - 1) % 2], ptb[:].rearrange("p (k s) -> p k s", k=2), pt_hi[:, (u - 1) % 2]).then_inc(pt_lod, 1)
                    if 0 <= u - 2 < PAIR and (u - 2) % HG == HG - 1:
                        n = (u - 2) // HG
                        dve.wait_ge(ot_hid, 2 * GROUPS * i + n + 1)
                        low(ot_lo[:, n % 2], avb[:, 0:S], ot_hi[:, n % 2]).then_inc(ot_lod, 1)
                    if u - 3 in (N1 - 1, PAIR - 1):
                        bb = (u - 3) // N1
                        dve.wait_ge(o_ready, 2 * i + bb + 1)
                        for t in range(2):
                            o = V.scalar_tensor_tensor(x_sb[:, bb, t], ob[t][:], gate_t[:, 0:1], x_sb[:, bb, t], ALU.mult, ALU.add)
                        o.then_inc(o_free, 1)
    clear(nc, used)


def feed_forward(nc, x_in, x_out, w1, b1, w2, b2, gate, identity, tag):
    CH = 512
    FC, TC, HC = D // P, CH // P, H1 // P
    CHUNKS = TOK // CH
    used = []
    with ExitStack() as ctx:
        def sb(name, shape, dt=F32):
            return ctx.enter_context(nc.sbuf_tensor(tag + name, shape, dt))

        def bank(name):
            return ctx.enter_context(nc.psum_tensor(tag + name, [P, 512], F32))

        def sem(name):
            used.append(nc.alloc_semaphore(tag + name))
            return used[-1]

        w1_hi, w1_lo = sb("w1_hi", [P, FC, H1], F32R), sb("w1_lo", [P, FC, H1], F32R)
        w2_hi, w2_lo = sb("w2_hi", [P, HC, D], F32R), sb("w2_lo", [P, HC, D], F32R)
        ident, b1_sb, b2_sb, gate_t = sb("ident", [P, P]), sb("b1_sb", [P, HC]), sb("b2_sb", [P, D]), sb("gate_t", [P, 1])
        x_sb = sb("x_sb", [P, 2, TC, D])
        xn = sb("xn", [P, TC, D])
        stats, mv, rstd = sb("stats", [P, TC, 6]), sb("mv", [P, TC, 2]), sb("rstd", [P, TC])
        root = [sb(f"root{n}", [P, TC]) for n in range(3)]
        xt_hi, xt_lo = sb("xt_hi", [P, FC, CH], F32R), sb("xt_lo", [P, FC, CH], F32R)
        h_f = sb("h_f", [P, 2, CH])
        h_hi, h_lo = sb("h_hi", [P, 2, CH], F32R), sb("h_lo", [P, 2, CH], F32R)
        credit = sb("credit", [P, 6])

        tb = [bank("tb0"), bank("tb1")]
        hb = [bank("hb0"), bank("hb1")]
        ob = [bank(f"ob{t}") for t in range(TC)]

        c_loaded, w_loaded, w_hid, w_lod = sem("c_loaded"), [sem("w_loaded0"), sem("w_loaded1")], sem("w_hid"), sem("w_lod")
        gate_done, bias_done, link_done = sem("gate_done"), sem("bias_done"), sem("link_done")
        x_loaded, x_stored = [sem("x_loaded0"), sem("x_loaded1")], [sem("x_stored0"), sem("x_stored1")]
        xn_done, t_ready, xt_hid, xt_lod = sem("xn_done"), sem("t_ready"), sem("xt_hid"), sem("xt_lod")
        h_ready, gelu_done, h_hid, h_lod = sem("h_ready"), sem("gelu_done"), sem("h_hid"), sem("h_lod")
        o_ready, o_done = sem("o_ready"), sem("o_done")

        consts = [(ident[:], identity), (b1_sb[:], b1), (b2_sb[:], b2), (gate_t[:], gate)]
        pieces = [(w1[:, c:c + 1], w1_hi[:, c:c + 1], w1_lo[:, c:c + 1]) for c in range(FC)]
        pieces += [(w2[:, h:h + 4], w2_hi[:, h:h + 4], w2_lo[:, h:h + 4]) for h in range(0, HC, 4)]

        def raw(n):
            a = pieces[n][0].shape[1]
            return x_sb[:, n % 2].rearrange("p t d -> p (t d)").rearrange("p (a b) -> p a b", a=a)

        block = ctx.enter_context(nc.Block())

        @block.sync
        def _(sp):
            for dst, src in consts:
                sp.dma_start(dst, src).then_inc(c_loaded, 16)
            for n, (src, _, _) in enumerate(pieces):
                if n >= 2:
                    sp.wait_ge(w_lod, n - 1)
                sp.dma_start(raw(n), src).then_inc(w_loaded[n % 2], 16)
            sp.wait_ge(w_lod, len(pieces))
            with sp.Fori(0, CHUNKS // 2) as i:
                for b in range(2):
                    sp.wait_ge(x_stored[b], 16 * i + 16)
                    sp.nop(nofuse=True)
                    sp.dma_start(x_sb[:, b], x_in[bass.ds((2 * i + b) * CH, CH), :].rearrange("(t p) d -> p t d", p=P)).then_inc(x_loaded[b], 16)

        @block.tensor
        def _(pe):
            def three(out, a_hi, a_lo, b_hi, b_lo, start, stop):
                nc.tensor.matmul(out, a_hi, b_hi, start=start, stop=False)
                nc.tensor.matmul(out, a_hi, b_lo, start=False, stop=False)
                return nc.tensor.matmul(out, a_lo, b_hi, start=False, stop=stop)

            def hidden(n, j):
                pe.wait_ge(gelu_done, HC * n + j + 1)
                for c in range(FC):
                    mm = three(hb[j % 2][:], w1_hi[:, c, j * P:(j + 1) * P], w1_lo[:, c, j * P:(j + 1) * P], xt_hi[:, c], xt_lo[:, c], c == 0, c == FC - 1)
                mm.then_inc(h_ready, 1)

            def out(n, j):
                pe.wait_ge(h_lod, HC * n + j + 1)
                if j == 0:
                    pe.wait_ge(o_done, n + 1)
                for t in range(TC):
                    mm = three(ob[t][:], h_hi[:, j % 2, t * P:(t + 1) * P], h_lo[:, j % 2, t * P:(t + 1) * P], w2_hi[:, j], w2_lo[:, j], j == 0, j == HC - 1)
                if j == HC - 1:
                    mm.then_inc(o_ready, 1)

            pe.wait_ge(c_loaded, 16 * len(consts))
            pe.wait_ge(w_lod, len(pieces))
            with pe.Fori(0, CHUNKS // 2) as i:
                for b in range(2):
                    n = 2 * i + b
                    pe.wait_ge(xn_done, n + 1)
                    for c in range(FC):
                        pe.wait_ge(xt_lod, FC * n + c + 1)
                        for t in range(TC):
                            mm = nc.tensor.transpose(tb[c % 2][:, t * P:(t + 1) * P], xn[:, t, c * P:(c + 1) * P], ident[:])
                        mm.then_inc(t_ready, 1)
                    pe.wait_ge(xt_lod, FC * n + FC + 2)
                    hidden(n, 0)
                    for j in range(HC):
                        if j + 1 < HC:
                            hidden(n, j + 1)
                        out(n, j)

        @block.scalar
        def _(act):
            act.wait_ge(c_loaded, 16 * len(consts))
            nc.scalar.activation(gate_t[:], gate_t[:], ACT.Tanh).then_inc(gate_done, 1)
            for n in range(len(pieces)):
                act.wait_ge(w_loaded[n % 2], 16 * (n // 2 + 1))
                nc.scalar.copy(pieces[n][1], raw(n)).then_inc(w_hid, 1)
            with act.Fori(0, CHUNKS // 2) as i:
                for b in range(2):
                    n = 2 * i + b
                    for c in range(FC):
                        act.wait_ge(t_ready, FC * n + c + 1)
                        nc.scalar.copy(xt_hi[:, c], tb[c % 2][:]).then_inc(xt_hid, 1)
                    for j in range(HC):
                        act.wait_ge(h_ready, HC * n + j + 1)
                        if b > 0 or j >= 2:
                            act.wait_ge(h_lod, HC * n + j - 1)
                        nc.scalar.activation(h_f[:, j % 2], hb[j % 2][:], ACT.Gelu, bias=b1_sb[:, j:j + 1]).then_inc(gelu_done, 1)
                        act.wait_ge(gelu_done, HC * n + j + 3)
                        nc.scalar.copy(h_hi[:, j % 2], h_f[:, j % 2]).then_inc(h_hid, 1)
                    act.wait_ge(o_done, n + 2)
                    act.dma_start(x_out[bass.ds(n * CH, CH), :].rearrange("(t p) d -> p t d", p=P), x_sb[:, b]).then_inc(x_stored[b], 16)
            for b in range(2):
                act.wait_ge(x_stored[b], 16 * (CHUNKS // 2) + 16)

        @block.vector
        def _(dve):
            V = nc.vector
            LINKS = 2 + ROOT_LINKS + 1

            def low(out, raw_in, hi):
                return V.tensor_tensor(out, raw_in, hi.bitcast(F32), ALU.subtract)

            V.memset(credit[:, 0:1], 0.0).then_inc(x_stored[0], 16)
            V.memset(credit[:, 1:2], 0.0).then_inc(x_stored[1], 16)
            V.memset(credit[:, 2:3], 0.0).then_inc(gelu_done, 2)
            V.memset(credit[:, 3:4], 0.0).then_inc(xt_lod, 2)
            V.memset(credit[:, 4:5], 0.0).then_inc(o_done, 1)
            for n in range(len(pieces)):
                dve.wait_ge(w_hid, n + 1)
                low(pieces[n][2], raw(n), pieces[n][1]).then_inc(w_lod, 1)
            dve.wait_ge(c_loaded, 16 * len(consts))
            dve.wait_ge(gate_done, 1)
            V.tensor_scalar(b2_sb[:], b2_sb[:], gate_t[:, 0:1], None, ALU.mult).then_inc(bias_done, 1)
            dve.wait_ge(bias_done, 1)

            with dve.Fori(0, CHUNKS // 2) as i:
                for b in range(2):
                    n = 2 * i + b
                    at = LINKS * n
                    dve.wait_ge(x_loaded[b], 16 * i + 16)
                    for t in range(TC):
                        l = V.bn_stats(stats[:, t], x_sb[:, b, t])
                    l.then_inc(link_done, 1)
                    dve.wait_ge(link_done, at + 1)
                    dve.nop(nofuse=True)
                    for t in range(TC):
                        l = V.bn_aggr(mv[:, t], stats[:, t])
                    l.then_inc(link_done, 1)
                    inverse_root(dve, V, link_done, at + 2, mv[:, :, 1], LN_EPS, root, rstd[:])
                    for t in range(TC):
                        l = V.tensor_scalar(xn[:, t], x_sb[:, b, t], mv[:, t, 0:1], rstd[:, t:t + 1], ALU.subtract, ALU.mult)
                    l.then_inc(xn_done, 1)
                    for t in range(TC):
                        l = V.tensor_tensor(x_sb[:, b, t], x_sb[:, b, t], b2_sb[:], ALU.add)
                    l.then_inc(link_done, 1)
                    dve.wait_ge(link_done, at + LINKS)
                    for c in range(FC):
                        dve.wait_ge(xt_hid, FC * n + c + 1)
                        low(xt_lo[:, c], tb[c % 2][:], xt_hi[:, c]).then_inc(xt_lod, 1)
                    for j in range(HC):
                        dve.wait_ge(h_hid, HC * n + j + 1)
                        low(h_lo[:, j % 2], h_f[:, j % 2], h_hi[:, j % 2]).then_inc(h_lod, 1)
                    dve.wait_ge(o_ready, n + 1)
                    for t in range(TC):
                        o = V.scalar_tensor_tensor(x_sb[:, b, t], ob[t][:], gate_t[:, 0:1], x_sb[:, b, t], ALU.mult, ALU.add)
                    o.then_inc(o_done, 1)
    clear(nc, used)


def program(nc, a, out):
    def dram(name, shape, dt=F32):
        return nc.dram_tensor(name, shape, dt, kind="Internal").ap()

    def by_row(w):
        return w.rearrange("(c p) n -> p c n", p=P)

    x_half, x1, x3 = dram("x_half", [TOK, D]), dram("x1", [TOK, D]), dram("x3", [TOK, D])
    xn_rows, y_rows = dram("xn_rows", [TOK + P, D]), dram("y_rows", [TOPK * TOK + TILE, D])
    slot_tokens, tile_table = dram("slot_tokens", [SLOTS, 1], I32), dram("tile_table", [P, 2], I32)
    for half, (x_res, x_out) in enumerate(((a["x"], x_half), (x_half, x1))):
        gated_cross_attention(nc, half, a["x"], x_res, x_out, a["ctx_t"], a["mask"], a["g_xattn0"], by_row(a["wq0"]), by_row(a["wk0"]), by_row(a["wv0"]),
                              by_row(a["wo0"]), a["identity"], f"a{half}_")
    with ExitStack() as ctx:
        weights = ctx.enter_context(nc.sbuf_tensor("weights", [P, TOPK * TOK // P], F32))
        route(nc, x1, xn_rows, slot_tokens, tile_table, a["router_w"], a["router_scale"], a["expert_scale"], a["g_ffn0"], a["identity"], a["earlier"],
              a["iotas"], a["pairs"], a["empty_list"], weights, "r_")
        experts(nc, xn_rows, slot_tokens, tile_table, a["w_gate"], a["w_out"], y_rows, a["identity"], "e_")
        gated_normed_attention(nc, x1, y_rows, weights, x3, a["ctx_t"], a["g_xattn1"], by_row(a["wq1"]), by_row(a["wkv1"]), by_row(a["wkv_dca"]),
                               by_row(a["wo1"]), a["bq1"], a["bkv1"], a["ln_w"], a["ln_b"], a["bo1"], a["identity"], "d_")
    feed_forward(nc, x3, out, by_row(a["w1"]), a["b1"], by_row(a["w2"]), a["b2"], a["g_ffn1"], a["identity"], "f_")


def kernel(**inputs):
    import concourse.bacc as bacc
    from concourse.bass_utils import run_bass_kernel_spmd

    def all_rows(v):
        return np.broadcast_to(v, (P,) + np.shape(v))

    def columns(v, n):
        return np.reshape(v, (n, P)).T

    def k_then_v(v):
        hd = D // NHEAD1
        return np.reshape(v, v.shape[:-1] + (NHEAD1, 2, hd)).swapaxes(-3, -2).reshape(v.shape)

    i = {name: np.asarray(v) for name, v in inputs.items()}
    keys = np.r_[S - DCA:S, 0:S - DCA]
    bkv = np.array(all_rows(all_rows(k_then_v(np.concatenate([i["L1_xattn_bk"], i["L1_xattn_bv"]])))[0:2]))
    bkv[0:DCA, 0] = i["L1_xattn_bkv_dca"]
    ln = {}
    for n in "wb":
        ln[n] = np.stack([i[f"L1_xattn_{x}_{n}"] for x in ("qn", "qn", "kn", "kn")])
        ln[n] = np.array(all_rows(ln[n]))
        ln[n][0:DCA, 2] = i[f"L1_xattn_kn_dca_{n}"]
    iotas = np.zeros((P, 3 * E + 1), np.float32)
    iotas[:, 0:E], iotas[:, E:2 * E] = np.arange(E), np.arange(E) * TOK
    iotas[0:E, 2 * E:3 * E] = np.triu(np.ones((E, E)))
    iotas[:, 3 * E] = np.arange(P)
    arrays = {
        "x": i["x"].reshape(TOK, D), "ctx_t": i["ctx_1024"][:, keys].swapaxes(1, 2),
        "mask": np.ascontiguousarray(all_rows(i["mask_BxS2_bf1"][:, keys].reshape(-1))).view(np.uint8),
        "g_xattn0": all_rows(i["g_xattn"][0:1]), "g_xattn1": all_rows(i["g_xattn"][1:2]),
        "g_ffn0": all_rows(i["g_ffn"][0:1]), "g_ffn1": all_rows(i["g_ffn"][1:2]),
        "wq0": i["L0_xattn_Wq"], "wk0": i["L0_xattn_Wk"], "wv0": i["L0_xattn_Wv"], "wo0": i["L0_xattn_Wo"],
        "router_w": i["L0_ffn_router_logits"].reshape(D // P, P, E).swapaxes(0, 1), "router_scale": columns(i["L0_ffn_router_scale"], D // P),
        "expert_scale": all_rows(i["L0_ffn_per_expert_scale"]),
        "w_gate": i["L0_ffn_gating_einsum"].transpose(0, 3, 1, 2).reshape(E, D, 2 * H0), "w_out": i["L0_ffn_linear"],
        "wq1": i["L1_xattn_Wq"], "wkv1": k_then_v(np.concatenate([i["L1_xattn_Wk"], i["L1_xattn_Wv"]], axis=1)), "wkv_dca": i["L1_xattn_Wkv_dca"],
        "wo1": i["L1_xattn_Wo"], "bq1": all_rows(i["L1_xattn_bq"]), "bkv1": bkv, "ln_w": ln["w"], "ln_b": ln["b"], "bo1": all_rows(i["L1_xattn_bo"]),
        "w1": i["L1_ffn_proj1"].T, "b1": columns(i["L1_ffn_proj1_bias"], H1 // P), "w2": i["L1_ffn_proj2"].T, "b2": all_rows(i["L1_ffn_proj2_bias"]),
        "identity": np.eye(P, dtype=np.float32), "earlier": np.triu(np.ones((P, P), np.float32), 1), "iotas": iotas,
        "pairs": np.arange(TOPK * TOK, dtype=np.int32).reshape(TOK // P, P, TOPK).swapaxes(0, 1).reshape(P, -1),
        "empty_list": (TOPK * TOK + np.arange(SLOTS, dtype=np.int32) % TILE).reshape(P, -1),
    }
    arrays = {f"in_{name}": np.ascontiguousarray(v) for name, v in arrays.items()}
    nc = bacc.Bacc("TRN2", target_bir_lowering=False, num_devices=1)
    aps = {name[3:]: nc.dram_tensor(name, v.shape, mybir.dt.from_np(v.dtype), kind="ExternalInput").ap() for name, v in arrays.items()}
    out = nc.dram_tensor("out_x", [TOK, D], F32, kind="ExternalOutput").ap()
    program(nc, aps, out)
    r = run_bass_kernel_spmd(nc, [arrays], core_ids=[0])
    return r.results[0]["out_x"].reshape(B, S, D)
```

```python
from contextlib import ExitStack

import numpy as np

import concourse.bass as bass
from concourse import mybir

F32, F32R, U8, U32, I32 = mybir.dt.float32, mybir.dt.float32r, mybir.dt.uint8, mybir.dt.uint32, mybir.dt.int32
ALU = mybir.AluOpType
ACT = mybir.ActivationFunctionType
AX = mybir.AxisListType
P = 128
B, S, D, DC = 16, 256, 512, 256
TOK = B * S
NHEAD0, DH0 = 16, 128
LN_EPS = 1e-5
E, H0, TOPK = 8, 512, 2
ROUTER_EPS = 1e-6
NHEAD1, DCA = 16, 16
HEAD_EPS = 1e-6
H1 = 2048
TILE = 256
TILES = TOK * TOPK // TILE + E - 1
SLOTS = E * TOK + 2 * E * TILE
MASKED = -1.0e30
TINY = 1.0e-30
NEG_INF = -3.0e38

ROOT_MAGIC = 1597463007.0
ROOT_TURNS = 3
ROOT_LINKS = 3 + 3 * ROOT_TURNS


def inverse_root(eng, ops, chain, at, var, eps, tmp, y, half=None):
    v, w, t = (x[:] for x in tmp)
    if half != 1:
        eng.wait_ge(chain, at)
        ops.tensor_scalar(v, var, eps, None, ALU.add).then_inc(chain, 1)
        eng.wait_ge(chain, at + 1)
        ops.tensor_scalar(w, v, -0.5, None, ALU.mult).then_inc(chain, 1)
        ops.tensor_scalar(y.bitcast(I32), v.bitcast(I32), -0.5, ROOT_MAGIC, ALU.mult, ALU.add).then_inc(chain, 1)
    for n in {None: range(ROOT_TURNS), 0: range(1), 1: range(1, ROOT_TURNS)}[half]:
        eng.wait_ge(chain, at + 3 + 3 * n)
        ops.tensor_tensor(t, y, y, ALU.mult).then_inc(chain, 1)
        eng.wait_ge(chain, at + 4 + 3 * n)
        ops.tensor_tensor(t, t, w, ALU.mult).then_inc(chain, 1)
        eng.wait_ge(chain, at + 5 + 3 * n)
        ops.scalar_tensor_tensor(y, t, 1.5, y, ALU.add, ALU.mult).then_inc(chain, 1)
    if half != 0:
        eng.wait_ge(chain, at + ROOT_LINKS)


def clear(nc, semaphores):
    nc.clear_and_free_semaphores(semaphores)
    nc.all_engine_barrier()


def gated_cross_attention(nc, half, x_ln, x_res, x_out, ctx_t, mask, gate, wq, wk, wv, wo, identity, tag):
    HEADS = NHEAD0 // 2
    GROUPS = HEADS // 2
    C0 = half * HEADS * DH0
    G0 = half * GROUPS * DH0
    SCALE = 1.0 / float(np.sqrt(DH0))
    PAIR = 2 * HEADS
    SHARED = 6
    LINKS = 3 + ROOT_LINKS
    FC, CC = D // P, DC // P

    used = []
    with ExitStack() as ctx:
        def sb(name, shape, dt=F32):
            return ctx.enter_context(nc.sbuf_tensor(tag + name, shape, dt))

        def bank(name):
            return ctx.enter_context(nc.psum_tensor(tag + name, [P, 512], F32))

        def sem(name):
            used.append(nc.alloc_semaphore(tag + name))
            return used[-1]

        wq_hi, wq_lo = sb("wq_hi", [P, FC, HEADS * DH0], F32R), sb("wq_lo", [P, FC, HEADS * DH0], F32R)
        wk_hi, wk_lo = sb("wk_hi", [P, CC, GROUPS * DH0], F32R), sb("wk_lo", [P, CC, GROUPS * DH0], F32R)
        wv_hi, wv_lo = sb("wv_hi", [P, CC, GROUPS * DH0], F32R), sb("wv_lo", [P, CC, GROUPS * DH0], F32R)
        wo_hi, wo_lo = sb("wo_hi", [P, HEADS, D], F32R), sb("wo_lo", [P, HEADS, D], F32R)
        ident = sb("ident", [P, P])
        mask_u8 = sb("mask_u8", [P, B * S], U8)
        maskb = sb("maskb", [P, 2, S])
        gate_t = sb("gate_t", [P, 1])
        x_sb = sb("x_sb", [P, 2, 2, D])
        xr_sb = sb("xr_sb", [P, 2, 2, D])
        xo_sb = sb("xo_sb", [P, 2, 2, D])
        xn = sb("xn", [P, 2, D])
        stats = sb("stats", [P, 2, 6])
        mv = sb("mv", [P, 2, 2])
        credit = sb("credit", [P, 6])
        rstd = sb("rstd", [P, 2])
        root = [sb(f"root{n}", [P, 2]) for n in range(3)]
        ctx_raw = sb("ctx_raw", [P, 2, CC, S])
        ctx_hi, ctx_lo = sb("ctx_hi", [P, CC, S], F32R), sb("ctx_lo", [P, CC, S], F32R)
        xt_hi, xt_lo = sb("xt_hi", [P, 2, FC, S], F32R), sb("xt_lo", [P, 2, FC, S], F32R)
        k_hi, k_lo = sb("k_hi", [P, 2, GROUPS, S], F32R), sb("k_lo", [P, 2, GROUPS, S], F32R)
        v_hi, v_lo = sb("v_hi", [P, 2, 2, GROUPS * DH0], F32R), sb("v_lo", [P, 2, 2, GROUPS * DH0], F32R)
        q_hi, q_lo = sb("q_hi", [P, 2, S], F32R), sb("q_lo", [P, 2, S], F32R)
        prob = sb("prob", [P, 4, 2, S])
        mx = sb("mx", [P, 2, 2])
        nbias = sb("nbias", [P, 2, 2])
        rsum = sb("rsum", [P, 2, 2])
        rinv = sb("rinv", [P, 2, 2])
        rsafe = sb("rsafe", [P, 2, 2])
        pt_hi, pt_lo = sb("pt_hi", [P, 2, 2, S], F32R), sb("pt_lo", [P, 2, 2, S], F32R)
        ot_hi, ot_lo = sb("ot_hi", [P, 2, S], F32R), sb("ot_lo", [P, 2, S], F32R)

        pj = [bank("pj0"), bank("pj1")]
        sc = [bank("sc0"), bank("sc1")]
        ptb, avb = bank("ptb"), bank("avb")
        ob = [bank("ob0"), bank("ob1")]

        w_loaded = [sem("w_loaded0"), sem("w_loaded1")]
        w_hi, w_lo = sem("w_hi"), sem("w_lo")
        m_loaded, g_loaded, g_done, id_done = sem("m_loaded"), sem("g_loaded"), sem("g_done"), sem("id_done")
        x_loaded, xr_loaded = [sem("x_loaded0"), sem("x_loaded1")], [sem("xr_loaded0"), sem("xr_loaded1")]
        c_loaded = [sem("c_loaded0"), sem("c_loaded1")]
        chain = sem("chain")
        xn_done, c_hi, c_lo = sem("xn_done"), sem("c_hi"), sem("c_lo")
        pj_ready, pj_hi, pj_lo = sem("pj_ready"), sem("pj_hi"), sem("pj_lo")
        s_ready, s_max, s_bias, e_done, r_half, r_done, p_done = (
            sem("s_ready"), sem("s_max"), sem("s_bias"), sem("e_done"), sem("r_half"), sem("r_done"), sem("p_done"))
        t_ready, pt_hid, pt_lod = sem("t_ready"), sem("pt_hid"), sem("pt_lod")
        av_ready, ot_hid, ot_lod = sem("av_ready"), sem("ot_hid"), sem("ot_lod")
        o_ready, o_free, x_stored = sem("o_ready"), sem("o_free"), [sem("x_stored0"), sem("x_stored1")]

        pieces = [(wk[:, :, G0:G0 + GROUPS * DH0], wk_hi[:], wk_lo[:]), (wv[:, :, G0:G0 + GROUPS * DH0], wv_hi[:], wv_lo[:])]
        for c in range(0, FC, 2):
            pieces.append((wq[:, c:c + 2, C0:C0 + HEADS * DH0], wq_hi[:, c:c + 2], wq_lo[:, c:c + 2]))
        for h in range(0, HEADS, 4):
            pieces.append((wo[:, half * HEADS + h:half * HEADS + h + 4], wo_hi[:, h:h + 4], wo_lo[:, h:h + 4]))

        def raw(n):
            a, b = pieces[n][0].shape[1:]
            return (prob, xo_sb)[n % 2][:].rearrange("p a b c -> p (a b c)")[:, 0:a * b].rearrange("p (a b) -> p a b", a=a)

        WHEN = {}

        def plan(n, *what):
            WHEN.setdefault(n, []).append(what)

        for n in range(3):
            plan(n - 9, "norm", n)
        plan(-8, "ctx", 0)
        for j in range(SHARED):
            plan(j - SHARED, "shared", j)
        FIRST, AHEAD = min(WHEN), 5

        def due(u, last, what):
            batches = range(2) if u < AHEAD or last else range(4)
            return [(bb, n) for bb in batches for w, n in WHEN.get(u - HEADS * bb, []) if w == what]

        def here(u, last):
            return 0 <= u < PAIR or (u >= PAIR and not last)

        def all_steps(eng, step):
            for u in range(FIRST, AHEAD):
                step(0, u, False)
            with eng.Fori(0, B // 2 - 1) as i:
                for u in range(AHEAD, PAIR + AHEAD):
                    step(i, u, False)
            for u in range(AHEAD, PAIR + AHEAD):
                step(B // 2 - 1, u, True)

        def place(i, bb, j):
            before = HEADS * bb + SHARED * bb
            if j >= SHARED:
                h = j - SHARED
                behind_last = isinstance(i, int) and 2 * i + bb == B - 1
                return before + h + (SHARED - 1 if h == 0 else SHARED if behind_last else SHARED + max(0, h + SHARED - HEADS - 1))
            units = j + 2 - SHARED
            return before + j + (max(0, units) if bb == 0 else units)

        def made(i, bb, j):
            return 2 * (HEADS + SHARED) * i + place(i, bb, j) + 1

        def item(bb, j):
            if j < 2:
                return xt_hi[:, bb % 2, 2 * j:2 * j + 2], xt_lo[:, bb % 2, 2 * j:2 * j + 2]
            if j < 4:
                g = 2 * (j - 2)
                return k_hi[:, bb % 2, g:g + 2], k_lo[:, bb % 2, g:g + 2]
            if j < 6:
                return v_hi[:, bb % 2, j - 4], v_lo[:, bb % 2, j - 4]
            return q_hi[:, j % 2], q_lo[:, j % 2]

        def item_psum(i, bb, j):
            b = pj[place(i, bb, j) % 2]
            if j < 4:
                return b[:].rearrange("p (a s) -> p a s", a=2)
            return b[:] if j < 6 else b[:, 0:S]

        block = ctx.enter_context(nc.Block())

        @block.sync
        def _(sp):
            sp.dma_start(gate_t[:], gate).then_inc(g_loaded, 16)
            sp.dma_start(mask_u8[:], mask).then_inc(m_loaded, 16)
            for n, (src, _, _) in enumerate(pieces):
                if n >= 2:
                    sp.wait_ge(w_lo, n - 1)
                sp.dma_start(raw(n), src).then_inc(w_loaded[n % 2], 16)
            with sp.Fori(0, B // 2) as i:
                for bb in range(2):
                    b = 2 * i + bb
                    rows = bass.ds(b * S, S)
                    sp.wait_ge(xn_done, b + 1)
                    sp.dma_start(x_sb[:, bb], x_ln[rows, :].rearrange("(t p) d -> p t d", p=P)).then_inc(x_loaded[bb], 16)
                    sp.wait_ge(c_lo, b + 1)
                    sp.dma_start(ctx_raw[:, bb], ctx_t[bass.ds(b, 1)].rearrange("o (c p) s -> p (o c) s", p=P)).then_inc(c_loaded[bb], 16)
                    sp.wait_ge(o_free, b + 1)
                    sp.dma_start(xr_sb[:, bb], x_res[rows, :].rearrange("(t p) d -> p t d", p=P)).then_inc(xr_loaded[bb], 16)

        @block.tensor
        def _(pe):
            def three(out, a_hi, a_lo, b_hi, b_lo, start, stop):
                nc.tensor.matmul(out, a_hi, b_hi, start=start, stop=False)
                nc.tensor.matmul(out, a_hi, b_lo, start=False, stop=False)
                return nc.tensor.matmul(out, a_lo, b_hi, start=False, stop=stop)

            def shared(i, bb, j):
                if place(i, bb, j) >= 2:
                    pe.wait_ge(pj_lo, made(i, bb, j) - 2)
                out = item_psum(i, bb, j)
                if j < 2:
                    pe.wait_ge(xn_done, 2 * i + bb + 3)
                    for c in range(2):
                        for t in range(2):
                            mm = nc.tensor.transpose(out[:, c, t * P:(t + 1) * P], xn[:, t, (2 * j + c) * P:(2 * j + c + 1) * P], ident[:])
                elif j < 4:
                    if j == 2:
                        pe.wait_ge(c_lo, 2 * i + bb + 3)
                    for a in range(2):
                        g = (2 * (j - 2) + a) * DH0
                        for c in range(CC):
                            mm = three(out[:, a], wk_hi[:, c, g:g + DH0], wk_lo[:, c, g:g + DH0],
                                       ctx_hi[:, c], ctx_lo[:, c], c == 0, c == CC - 1)
                else:
                    t = (j - 4) * P
                    for c in range(CC):
                        mm = three(out, ctx_hi[:, c, t:t + P], ctx_lo[:, c, t:t + P], wv_hi[:, c], wv_lo[:, c], c == 0, c == CC - 1)
                mm.then_inc(pj_ready, 1)

            def query(i, u):
                bb, h = divmod(u, HEADS)
                pe.wait_ge(pj_lo, made(i, bb, SHARED + h) - 2)
                if h == 0:
                    pe.wait_ge(pj_lo, made(i, bb, 1))
                for c in range(FC):
                    mm = three(item_psum(i, bb, SHARED + h), wq_hi[:, c, h * DH0:(h + 1) * DH0], wq_lo[:, c, h * DH0:(h + 1) * DH0],
                               xt_hi[:, bb % 2, c], xt_lo[:, bb % 2, c], c == 0, c == FC - 1)
                mm.then_inc(pj_ready, 1)

            def scores(i, u):
                bb, h = divmod(u, HEADS)
                pe.wait_ge(pj_lo, made(i, bb, SHARED + h))
                pe.wait_ge(s_max, PAIR * i + u + 1)
                out = sc[u % 2][:].rearrange("p (t s) -> p t s", t=2)
                for t in range(2):
                    mm = three(out[:, t], q_hi[:, h % 2, t * P:(t + 1) * P], q_lo[:, h % 2, t * P:(t + 1) * P],
                               k_hi[:, bb % 2, h // 2], k_lo[:, bb % 2, h // 2], True, True)
                mm.then_inc(s_ready, 1)

            def turn(i, u):
                pe.wait_ge(p_done, PAIR * i + u + 1)
                pe.wait_ge(pt_lod, PAIR * i + u + 1)
                out = ptb[:].rearrange("p (k s) -> p k s", k=2)
                for k in range(2):
                    for t in range(2):
                        mm = nc.tensor.transpose(out[:, k, t * P:(t + 1) * P], prob[:, u % 4, t, k * P:(k + 1) * P], ident[:])
                mm.then_inc(t_ready, 1)

            def values(i, u):
                bb, h = divmod(u, HEADS)
                g = (h // 2) * DH0
                pe.wait_ge(pt_lod, PAIR * i + u + 2)
                if h == 0:
                    pe.wait_ge(pj_lo, made(i, bb, 5))
                pe.wait_ge(ot_lod, PAIR * i + u + 1)
                for k in range(2):
                    mm = three(avb[:, 0:S], v_hi[:, bb % 2, k, g:g + DH0], v_lo[:, bb % 2, k, g:g + DH0],
                               pt_hi[:, u % 2, k], pt_lo[:, u % 2, k], k == 0, k == 1)
                mm.then_inc(av_ready, 1)

            def project(i, u):
                bb, h = divmod(u, HEADS)
                pe.wait_ge(ot_lod, PAIR * i + u + 2)
                if h == 0:
                    pe.wait_ge(o_free, 2 * i + bb + 2)
                for t in range(2):
                    mm = three(ob[t][:], ot_hi[:, u % 2, t * P:(t + 1) * P], ot_lo[:, u % 2, t * P:(t + 1) * P],
                               wo_hi[:, h], wo_lo[:, h], h == 0, h == HEADS - 1)
                if h == HEADS - 1:
                    mm.then_inc(o_ready, 1)

            pe.wait_ge(id_done, 16)
            pe.wait_ge(w_lo, len(pieces))

            def step(i, u, last):
                if here(u + 1, last):
                    query(i, u + 1)
                if here(u, last):
                    scores(i, u)
                if here(u - 4, last):
                    values(i, u - 4)
                if here(u - 5, last):
                    project(i, u - 5)
                for bb, j in due(u, last, "shared"):
                    shared(i, bb, j)
                if here(u - 2, last):
                    turn(i, u - 2)

            all_steps(pe, step)

        @block.scalar
        def _(act):
            act.wait_ge(g_loaded, 16)
            nc.scalar.activation(gate_t[:], gate_t[:], ACT.Tanh).then_inc(g_done, 1)
            for n in range(len(pieces)):
                act.wait_ge(w_loaded[n % 2], 16 * (n // 2 + 1))
                nc.scalar.copy(pieces[n][1], raw(n)).then_inc(w_hi, 1)

            def high(i, bb, j):
                act.wait_ge(pj_ready, made(i, bb, j))
                nc.scalar.copy(item(bb, j)[0], item_psum(i, bb, j)).then_inc(pj_hi, 1)

            def step(i, u, last):
                if here(u - 3, last):
                    act.wait_ge(t_ready, PAIR * i + u - 2)
                    nc.scalar.copy(pt_hi[:, (u - 3) % 2], ptb[:].rearrange("p (k s) -> p k s", k=2)).then_inc(pt_hid, 1)
                if here(u + 1, last):
                    high(i, (u + 1) // HEADS, SHARED + (u + 1) % HEADS)
                if here(u, last):
                    act.wait_ge(s_bias, PAIR * i + u + 1)
                    for t in range(2):
                        e = nc.scalar.activation(prob[:, u % 4, t], prob[:, u % 4, t], ACT.Exp, bias=nbias[:, u % 2, t:t + 1],
                                                 scale=SCALE, accum_out=rsum[:, u % 2, t:t + 1])
                    e.then_inc(e_done, 1)
                if here(u - 4, last):
                    act.wait_ge(av_ready, PAIR * i + u - 3)
                    nc.scalar.copy(ot_hi[:, (u - 4) % 2], avb[:, 0:S]).then_inc(ot_hid, 1)
                for bb, j in due(u, last, "shared"):
                    high(i, bb, j)
                for bb, _ in due(u, last, "ctx"):
                    act.wait_ge(c_loaded[bb % 2], 16 * (i + bb // 2) + 16)
                    if bb > 0:
                        act.wait_ge(pj_lo, made(i, bb - 1, SHARED - 1))
                    nc.scalar.copy(ctx_hi[:], ctx_raw[:, bb % 2]).then_inc(c_hi, 1)
                if here(u - 5, last) and (u - 5) % HEADS == HEADS - 1:
                    bb = (u - 5) // HEADS
                    act.wait_ge(o_free, 2 * i + bb + 3)
                    act.dma_start(x_out[bass.ds((2 * i + bb) * S, S), :].rearrange("(t p) d -> p t d", p=P),
                                  xo_sb[:, bb]).then_inc(x_stored[bb], 16)

            all_steps(act, step)
            for bb in range(2):
                act.wait_ge(x_stored[bb], 16 * (B // 2) + 16)

        @block.gpsimd
        def _(pool):
            pool.dma_start(ident[:], identity).then_inc(id_done, 16)

            def step(i, u, last):
                if here(u, last):
                    pool.wait_ge(r_done, PAIR * i + u + 1)
                    pool.nop(nofuse=True)
                    for t in range(2):
                        p = nc.gpsimd.tensor_scalar(prob[:, u % 4, t], prob[:, u % 4, t], rinv[:, u % 2, t:t + 1], None, ALU.mult)
                    p.then_inc(p_done, 1)

            all_steps(pool, step)

        @block.vector
        def _(dve):
            def low(out, raw_in, hi):
                return nc.vector.tensor_tensor(out, raw_in, hi.bitcast(F32), ALU.subtract)

            for n, (what, count) in enumerate([(o_free, 2), (xn_done, 2), (c_lo, 2), (s_max, 2), (pt_lod, 1), (ot_lod, 1)]):
                nc.vector.memset(credit[:, n:n + 1], 0.0).then_inc(what, count)
            for bb in range(2):
                nc.vector.memset(rsum[:, bb], 1.0).then_inc(x_stored[bb], 16)
            for n in range(len(pieces)):
                dve.wait_ge(w_hi, n + 1)
                low(pieces[n][2], raw(n), pieces[n][1]).then_inc(w_lo, 1)
            dve.wait_ge(w_lo, len(pieces))
            dve.wait_ge(m_loaded, 16)
            dve.wait_ge(g_done, 1)

            def low_item(i, bb, j):
                dve.wait_ge(pj_hi, made(i, bb, j))
                low(item(bb, j)[1], item_psum(i, bb, j), item(bb, j)[0]).then_inc(pj_lo, 1)

            def normalize(i, bb, n):
                at = LINKS * (2 * i + bb)
                if n == 0:
                    dve.wait_ge(x_loaded[bb % 2], 16 * (i + bb // 2) + 16)
                    for t in range(2):
                        l = nc.vector.bn_stats(stats[:, t], x_sb[:, bb % 2, t])
                    l.then_inc(chain, 1)
                    dve.wait_ge(chain, at + 1)
                    dve.nop(nofuse=True)
                    for t in range(2):
                        l = nc.vector.bn_aggr(mv[:, t], stats[:, t])
                    l.then_inc(chain, 1)
                    nc.vector.tensor_scalar(maskb[:, bb % 2], mask_u8[:, bass.ds((2 * i + bb) * S, S)], -1.0, -MASKED, ALU.add, ALU.mult).then_inc(chain, 1)
                else:
                    inverse_root(dve, nc.vector, chain, at + 3, mv[:, :, 1], LN_EPS, root, rstd[:], n - 1)
                if n == 2:
                    for t in range(2):
                        l = nc.vector.tensor_scalar(xn[:, t], x_sb[:, bb % 2, t], mv[:, t, 0:1], rstd[:, t:t + 1], ALU.subtract, ALU.mult)
                    l.then_inc(xn_done, 1)

            def step(i, u, last):
                if here(u - 3, last):
                    dve.wait_ge(pt_hid, PAIR * i + u - 2)
                    low(pt_lo[:, (u - 3) % 2], ptb[:].rearrange("p (k s) -> p k s", k=2), pt_hi[:, (u - 3) % 2]).then_inc(pt_lod, 1)
                if here(u + 1, last):
                    low_item(i, (u + 1) // HEADS, SHARED + (u + 1) % HEADS)
                if here(u, last):
                    dve.wait_ge(s_ready, PAIR * i + u + 1)
                    dve.nop(nofuse=True)
                    out = sc[u % 2][:].rearrange("p (t s) -> p t s", t=2)
                    for t in range(2):
                        m = nc.vector.tensor_tensor_reduce(prob[:, u % 4, t], out[:, t], maskb[:, u // HEADS % 2], 1.0, NEG_INF, ALU.add, ALU.max,
                                                           mx[:, u % 2, t:t + 1])
                    m.then_inc(s_max, 1)
                    dve.wait_ge(s_max, PAIR * i + u + 3)
                    nc.vector.tensor_scalar(nbias[:, u % 2], mx[:, u % 2], MASKED / 2, -SCALE, ALU.max, ALU.mult).then_inc(s_bias, 1)
                if here(u - 1, last):
                    v = u - 1
                    dve.wait_ge(e_done, PAIR * i + v + 1)
                    nc.vector.tensor_scalar(rsafe[:, v % 2], rsum[:, v % 2], TINY, None, ALU.max).then_inc(r_half, 1)
                    dve.wait_ge(r_half, PAIR * i + v + 1)
                    nc.vector.reciprocal(rinv[:, v % 2], rsafe[:, v % 2]).then_inc(r_done, 1)
                if here(u - 4, last):
                    dve.wait_ge(ot_hid, PAIR * i + u - 3)
                    low(ot_lo[:, (u - 4) % 2], avb[:, 0:S], ot_hi[:, (u - 4) % 2]).then_inc(ot_lod, 1)
                if here(u - 5, last) and (u - 5) % HEADS == HEADS - 1:
                    bb = (u - 5) // HEADS
                    dve.wait_ge(o_ready, 2 * i + bb + 1)
                    dve.wait_ge(xr_loaded[bb], 16 * i + 16)
                    dve.wait_ge(x_stored[bb], 16 * i + 16)
                    for t in range(2):
                        o = nc.vector.scalar_tensor_tensor(xo_sb[:, bb, t], ob[t][:], gate_t[:, 0:1], xr_sb[:, bb, t], ALU.mult, ALU.add)
                    o.then_inc(o_free, 1)
                for bb, j in due(u, last, "shared"):
                    low_item(i, bb, j)
                for bb, n in due(u, last, "norm"):
                    normalize(i, bb, n)
                for bb, _ in due(u, last, "ctx"):
                    dve.wait_ge(c_hi, 2 * i + bb + 1)
                    low(ctx_lo[:], ctx_raw[:, bb % 2], ctx_hi[:]).then_inc(c_lo, 1)

            all_steps(dve, step)
    clear(nc, used)

def route(nc, x_in, xn_out, slot_tokens, tile_table, logits_w, router_scale, expert_scale, gate, identity, earlier, iotas, pairs, empty_list, weights, tag):
    QT = 8
    TURNS = TOK // (QT * P)
    FC = D // P
    used = []
    with ExitStack() as ctx:
        def sb(name, shape, dt=F32):
            return ctx.enter_context(nc.sbuf_tensor(tag + name, shape, dt))

        def bank(name):
            return ctx.enter_context(nc.psum_tensor(tag + name, [P, 512], F32))

        def sem(name):
            used.append(nc.alloc_semaphore(tag + name))
            return used[-1]

        ident, before, ones = sb("ident", [P, P]), sb("before", [P, P]), sb("ones", [P, P])
        iota = sb("iota", [P, 3 * E + 1])
        expert_no, list_start, upto, tile_no = iota[:, 0:E], iota[:, E:2 * E], iota[:, 2 * E:3 * E], iota[:, 3 * E:3 * E + 1]
        pair_no = sb("pair_no", [P, TOK * TOPK // P], I32)
        wr_raw, wr, rscale = sb("wr_raw", [P, FC, E]), sb("wr", [P, FC, E]), sb("rscale", [P, FC])
        escale, gate_t = sb("escale", [P, E]), sb("gate_t", [P, 1])
        empty, blank = sb("empty", [P, SLOTS // P], I32), sb("blank", [P, D])
        x_sb, xn = sb("x_sb", [P, 2, QT, D]), sb("xn", [P, 2, QT, D])
        stats, mv = sb("stats", [P, QT, 6]), sb("mv", [P, QT, 2])
        rstd, var2, r2 = sb("rstd", [P, QT]), sb("var2", [P, QT]), sb("r2", [P, QT])
        root = [sb(f"root{n}", [P, QT]) for n in range(3)]
        xt = sb("xt", [P, 2, FC, P])
        logits, best, best_no = sb("logits", [P, QT, E]), sb("best", [P, QT, 8]), sb("best_no", [P, QT, 8], U32)
        no_f, gap, odds, share = sb("no_f", [P, QT, 2]), sb("gap", [P, QT]), sb("odds", [P, QT]), sb("share", [P, QT, 2])
        hot, picked, total, here = sb("hot", [P, QT, 2, E]), sb("picked", [P, QT, E]), sb("total", [P, E]), sb("here", [P, E])
        rank, scratch = sb("rank", [P, QT, E]), sb("scratch", [P, QT, 2, E])
        pos_f, scale_of = sb("pos_f", [P, QT, 2]), sb("scale_of", [P, QT, 2])
        pair, pos_here = sb("pair", [P, 2, QT, 2], I32), sb("pos_here", [P, 2, QT, 2], I32)
        count, count_i, tiles, tiles_rep = sb("count", [P, 1]), sb("count_i", [P, 1], I32), sb("tiles", [P, 1]), sb("tiles_rep", [P, P])
        credit = sb("credit", [P, 4])
        cum, below, start = sb("cum", [P, E]), sb("below", [P, E]), sb("start", [P, E])
        tab_f, tab_i = sb("tab_f", [P, 4]), sb("tab_i", [P, 2], I32)

        tb = [bank("tb0"), bank("tb1")]
        lb, rb, cb = bank("lb"), bank("rb"), bank("cb")

        c_loaded, blank_done, cleared, x_loaded = sem("c_loaded"), sem("blank_done"), sem("cleared"), [sem("x_loaded0"), sem("x_loaded1")]
        gate_done, wr_done = sem("gate_done"), sem("wr_done")
        link_done, xn_done, xn_stored = sem("link_done"), sem("xn_done"), [sem("xn_stored0"), sem("xn_stored1")]
        t_ready, t_done, l_ready = sem("t_ready"), sem("t_done"), sem("l_ready")
        gap_done, odds_done, picked_done, rank_ready, pos_done = sem("gap_done"), sem("odds_done"), sem("picked_done"), sem("rank_ready"), sem("pos_done")
        listed, list_free, count_ready, tiles_done, cum_ready, tab_link, tab_done, tab_stored = (
            sem("listed"), sem("list_free"), sem("count_ready"), sem("tiles_done"), sem("cum_ready"), sem("tab_link"), sem("tab_done"), sem("tab_stored"))

        block = ctx.enter_context(nc.Block())
        LISTED = 16 * 2 * QT

        def pair_rows(x):
            return x[:].rearrange("p t k e -> p (t k) e")

        def rows(i):
            return bass.ds(i * QT * P, QT * P)

        @block.sync
        def _(sp):
            for dst, src in ((ident[:], identity), (before[:], earlier), (iota[:], iotas), (wr_raw[:], logits_w), (rscale[:], router_scale),
                             (escale[:], expert_scale), (gate_t[:], gate), (pair_no[:], pairs), (empty[:], empty_list)):
                sp.dma_start(dst, src).then_inc(c_loaded, 16)
            sp.wait_ge(c_loaded, 16 * 9)
            sp.dma_start(slot_tokens.rearrange("(p s) o -> p (s o)", p=P), empty[:]).then_inc(cleared, 16)
            sp.wait_ge(blank_done, 1)
            sp.dma_start(xn_out[TOK:TOK + P, :], blank[:]).then_inc(cleared, 16)
            with sp.Fori(0, TURNS // 2) as i:
                for b in range(2):
                    sp.wait_ge(xn_done, 2 * i + b + 1)
                    sp.nop(nofuse=True)
                    sp.dma_start(x_sb[:, b], x_in[rows(2 * i + b), :].rearrange("(t p) d -> p t d", p=P)).then_inc(x_loaded[b], 16)
            sp.wait_ge(tab_done, 1)
            sp.dma_start(tile_table, tab_i[:]).then_inc(tab_stored, 16)
            sp.wait_ge(tab_stored, 16)

        @block.tensor
        def _(pe):
            def logits_of(turn, t):
                pe.wait_ge(t_done, QT * turn + t + 3)
                for c in range(FC):
                    mm = nc.tensor.matmul(lb[:, t * E:(t + 1) * E], xt[:, t % 2, c], wr[:, c], start=(c == 0), stop=(c == FC - 1))
                if t == QT - 1:
                    mm.then_inc(l_ready, 1)

            pe.wait_ge(c_loaded, 16 * 9)
            pe.wait_ge(wr_done, 1)
            with pe.Fori(0, TURNS // 2) as i:
                for b in range(2):
                    turn = 2 * i + b
                    pe.wait_ge(xn_done, turn + 3)
                    for t in range(QT):
                        pe.wait_ge(t_done, QT * turn + t + 1)
                        for c in range(FC):
                            mm = nc.tensor.transpose(tb[t % 2][:, c * P:(c + 1) * P], xn[:, b, t, c * P:(c + 1) * P], ident[:])
                        mm.then_inc(t_ready, 1)
                        if t >= 1:
                            logits_of(turn, t - 1)
                    logits_of(turn, QT - 1)
                    pe.wait_ge(picked_done, turn + 1)
                    nc.tensor.matmul(rb[:, 0:QT * E], before[:], picked[:].rearrange("p t e -> p (t e)"), start=True, stop=False)
                    for t in range(QT - 1):
                        later = rb[:, (t + 1) * E:QT * E].rearrange("p (t e) -> p t e", e=E)
                        nc.tensor.matmul(later, ones[:], picked[:, t:t + 1].to_broadcast([P, QT - 1 - t, E]), start=False, stop=False)
                    mm = nc.tensor.matmul(rb[:, 0:QT * E].rearrange("p (t e) -> p t e", e=E), ones[:], total[:].unsqueeze(1).to_broadcast([P, QT, E]),
                                          start=False, stop=True)
                    mm.then_inc(rank_ready, 1)
            pe.wait_ge(pos_done, TURNS + 1)
            nc.tensor.matmul(cb[0:E, 0:1], total[:], ones[:, 0:1], start=True, stop=True).then_inc(count_ready, 1)
            pe.wait_ge(tiles_done, 1)
            nc.tensor.matmul(cb[:, E:2 * E], tiles_rep[0:E, :], upto[0:E, :], start=True, stop=True).then_inc(cum_ready, 1)

        @block.scalar
        def _(act):
            act.wait_ge(c_loaded, 16 * 9)
            nc.scalar.activation(gate_t[:], gate_t[:], ACT.Tanh).then_inc(gate_done, 1)
            with act.Fori(0, TURNS // 2) as i:
                for b in range(2):
                    turn = 2 * i + b
                    act.wait_ge(xn_done, turn + 3)
                    act.dma_start(xn_out[rows(turn), :].rearrange("(t p) d -> p t d", p=P), xn[:, b]).then_inc(xn_stored[b], 16)
                    for t in range(QT):
                        act.wait_ge(t_ready, QT * turn + t + 1)
                        nc.scalar.copy(xt[:, t % 2], tb[t % 2][:].rearrange("p (c s) -> p c s", c=FC)).then_inc(t_done, 1)
                    act.wait_ge(gap_done, turn + 1)
                    nc.scalar.activation(odds[:], gap[:], ACT.Exp).then_inc(odds_done, 1)
            for b in range(2):
                act.wait_ge(xn_stored[b], 16 * (TURNS // 2) + 16)

        @block.gpsimd
        def _(pool):
            nc.gpsimd.memset(blank[:], 0.0).then_inc(blank_done, 1)
            pool.wait_ge(cleared, 32)
            with pool.Fori(0, TURNS // 2) as i:
                for b in range(2):
                    turn = 2 * i + b
                    for t in range(QT):
                        for k in range(2):
                            if (t, k) == (0, 0):
                                pool.wait_ge(pos_done, turn + 2)
                                pool.nop(nofuse=True)
                            pool.indirect_dma_start(out=slot_tokens, out_offset=bass.IndirectOffsetOnAxis(ap=pos_here[:, b, t, k:k + 1], axis=0),
                                                    in_=pair[:, b, t, k:k + 1], in_offset=None).then_inc(listed, 16)
                    pool.wait_ge(listed, LISTED * (turn + 1))
                    pool.nop(nofuse=True).then_inc(list_free, 1)

        LINKS = 22 + 2 * ROOT_LINKS

        @block.vector
        def _(dve):
            V = nc.vector
            V.memset(total[:], 0.0).then_inc(xn_done, 2)
            V.memset(ones[:], 1.0).then_inc(t_done, 2)
            V.memset(credit[:, 0:1], 0.0).then_inc(xn_stored[0], 16)
            V.memset(credit[:, 1:2], 0.0).then_inc(xn_stored[1], 16)
            V.memset(credit[:, 2:3], 0.0).then_inc(pos_done, 1)
            V.memset(credit[:, 3:4], 0.0).then_inc(list_free, 2)
            dve.wait_ge(c_loaded, 16 * 9)
            for c in range(FC):
                w = V.tensor_scalar(wr[:, c], wr_raw[:, c], rscale[:, c:c + 1], float(D) ** -0.5, ALU.mult, ALU.mult)
            w.then_inc(wr_done, 1)
            dve.wait_ge(gate_done, 1)

            with dve.Fori(0, TURNS // 2) as i:
                for b in range(2):
                    turn = 2 * i + b
                    done = [0]

                    def link(op):
                        op.then_inc(link_done, 1)
                        done[0] += 1
                        dve.wait_ge(link_done, LINKS * turn + done[0])
                        dve.nop(nofuse=True)

                    dve.wait_ge(x_loaded[b], 16 * i + 16)
                    for t in range(QT):
                        op = V.bn_stats(stats[:, t], x_sb[:, b, t])
                    link(op)
                    for t in range(QT):
                        op = V.bn_aggr(mv[:, t], stats[:, t])
                    link(op)
                    inverse_root(dve, V, link_done, LINKS * turn + done[0], mv[:, :, 1], LN_EPS, root, rstd[:])
                    done[0] += ROOT_LINKS
                    dve.wait_ge(xn_stored[b], 16 * i + 16)
                    for t in range(QT):
                        op = V.tensor_scalar(xn[:, b, t], x_sb[:, b, t], mv[:, t, 0:1], rstd[:, t:t + 1], ALU.subtract, ALU.mult)
                    op.then_inc(xn_done, 1)
                    link(V.tensor_tensor(var2[:], mv[:, :, 1], rstd[:], ALU.mult))
                    link(V.tensor_tensor(var2[:], var2[:], rstd[:], ALU.mult))
                    inverse_root(dve, V, link_done, LINKS * turn + done[0], var2[:], ROUTER_EPS, root, r2[:])
                    done[0] += ROOT_LINKS
                    dve.wait_ge(l_ready, turn + 1)
                    for t in range(QT):
                        op = V.tensor_scalar(logits[:, t], lb[:, t * E:(t + 1) * E], r2[:, t:t + 1], None, ALU.mult)
                    link(op)
                    for t in range(QT):
                        op = V.max(best[:, t], logits[:, t])
                    link(op)
                    V.tensor_tensor(gap[:], best[:, :, 1], best[:, :, 0], ALU.subtract).then_inc(gap_done, 1)
                    for t in range(QT):
                        op = V.max_index(best_no[:, t], best[:, t], logits[:, t])
                    link(op)
                    link(V.tensor_copy(no_f[:], best_no[:, :, 0:2]))
                    link(V.tensor_tensor(pair_rows(hot), expert_no.unsqueeze(1).to_broadcast([P, 2 * QT, E]),
                                         no_f[:].rearrange("p t k -> p (t k)").unsqueeze(2).to_broadcast([P, 2 * QT, E]), ALU.is_equal))
                    V.tensor_tensor(picked[:], hot[:, :, 0], hot[:, :, 1], ALU.add).then_inc(picked_done, 1)
                    dve.wait_ge(odds_done, turn + 1)
                    link(V.tensor_scalar(gap[:], odds[:], 1.0, None, ALU.add))
                    link(V.reciprocal(share[:, :, 0], gap[:]))
                    link(V.tensor_tensor(share[:, :, 1], share[:, :, 0], odds[:], ALU.mult))
                    link(V.tensor_tensor(pair_rows(scratch), pair_rows(hot), escale[:].unsqueeze(1).to_broadcast([P, 2 * QT, E]), ALU.mult))
                    link(V.tensor_reduce(scale_of[:], scratch[:], AX.X, ALU.add))
                    link(V.tensor_tensor(share[:], share[:], scale_of[:], ALU.mult))
                    op = V.tensor_scalar(weights[:, bass.ds(turn * 2 * QT, 2 * QT)], share[:].rearrange("p t k -> p (t k)"), gate_t[:, 0:1], None, ALU.mult)
                    link(op)
                    dve.wait_ge(rank_ready, turn + 1)
                    link(V.tensor_tensor(rank[:], rb[:, 0:QT * E].rearrange("p (t e) -> p t e", e=E), list_start.unsqueeze(1).to_broadcast([P, QT, E]), ALU.add))
                    link(V.tensor_tensor(scratch[:], hot[:], rank[:].unsqueeze(2).to_broadcast([P, QT, 2, E]), ALU.mult))
                    link(V.tensor_reduce(pos_f[:], scratch[:], AX.X, ALU.add))
                    link(V.tensor_reduce(here[:], picked[:].rearrange("p t e -> p e t"), AX.X, ALU.add))
                    link(V.tensor_tensor(total[:], total[:], here[:], ALU.add))
                    dve.wait_ge(list_free, turn + 1)
                    link(V.tensor_copy(pos_here[:, b], pos_f[:]))
                    V.tensor_copy(pair[:, b].rearrange("p t k -> p (t k)"), pair_no[:, bass.ds(turn * 2 * QT, 2 * QT)]).then_inc(pos_done, 1)
                    assert done[0] == LINKS, done[0]
            dve.wait_ge(count_ready, 1)
            made = [0]

            def last(op):
                op.then_inc(tab_link, 1)
                made[0] += 1
                dve.wait_ge(tab_link, made[0])

            last(V.tensor_scalar(count[0:E, :], cb[0:E, 0:1], float(TILE - 1), None, ALU.add))
            last(V.tensor_copy(count_i[0:E, :], count[0:E, :]))
            last(V.tensor_scalar(count_i[0:E, :], count_i[0:E, :], TILE.bit_length() - 1, None, ALU.logical_shift_right))
            last(V.tensor_copy(tiles[0:E, :], count_i[0:E, :]))
            V.tensor_scalar(tiles_rep[0:E, :], ones[0:E, :], tiles[0:E, :], None, ALU.mult).then_inc(tiles_done, 1)
            dve.wait_ge(cum_ready, 1)
            last(V.tensor_copy(cum[:], cb[:, E:2 * E]))
            last(V.tensor_scalar(below[:], cum[:], tile_no, None, ALU.is_le))
            last(V.tensor_tensor(start[:], cum[:], below[:], ALU.mult))
            last(V.tensor_reduce(tab_f[:, 0:1], below[:], AX.X, ALU.add))
            last(V.tensor_reduce(tab_f[:, 1:2], start[:], AX.X, ALU.max))
            last(V.tensor_tensor(tab_f[:, 2:3], tile_no, tab_f[:, 1:2], ALU.subtract))
            last(V.tensor_scalar(tab_f[:, 2:3], tab_f[:, 2:3], float(TILE), None, ALU.mult))
            last(V.tensor_scalar(tab_f[:, 3:4], tab_f[:, 0:1], float(TOK), tab_f[:, 2:3], ALU.mult, ALU.add))
            last(V.tensor_scalar(tab_f[:, 0:1], tab_f[:, 0:1], float(E - 1), None, ALU.min))
            last(V.tensor_copy(tab_i[:, 0:1], tab_f[:, 0:1]))
            V.tensor_copy(tab_i[:, 1:2], tab_f[:, 3:4]).then_inc(tab_done, 1)
    clear(nc, used)


def experts(nc, xn_rows, slot_tokens, tile_table, w_gate, w_out, y_rows, identity, tag):
    FC, HC, TT = D // P, H0 // P, TILE // P
    WCOL = 2 * H0 + D
    TURNS = TILES // 2
    LAST = 2 * TURNS
    used = []
    with ExitStack() as ctx:
        def sb(name, shape, dt=F32):
            return ctx.enter_context(nc.sbuf_tensor(tag + name, shape, dt))

        def bank(name):
            return ctx.enter_context(nc.psum_tensor(tag + name, [P, 512], F32))

        def sem(name):
            used.append(nc.alloc_semaphore(tag + name))
            return used[-1]

        ident = sb("ident", [P, P])
        table = sb("table", [1, 2 * P], I32)
        pairs, ids, rows = sb("pairs", [P, 2, TT], I32), sb("ids", [P, 2, TT], I32), sb("rows", [P, 2, TT], I32)
        xg = sb("xg", [P, 2, TT, D])
        xt_hi, xt_lo = sb("xt_hi", [P, 2, FC, TILE], F32R), sb("xt_lo", [P, 2, FC, TILE], F32R)
        w_raw = sb("w_raw", [P, 2, FC, WCOL])
        w_hi, w_lo = sb("w_hi", [P, 2, FC, WCOL], F32R), sb("w_lo", [P, 2, FC, WCOL], F32R)
        gelu = sb("gelu", [P, 2, TILE])
        act_f = sb("act_f", [P, HC, TILE])
        act_hi, act_lo = sb("act_hi", [P, 2, HC, TILE], F32R), sb("act_lo", [P, 2, HC, TILE], F32R)
        y_sb = sb("y_sb", [P, 2, TT, D])
        credit = sb("credit", [P, 9])
        zeros = sb("zeros", [P, TILE])

        tb = [bank("tb0"), bank("tb1")]
        gb = [bank(f"gb{h}") for h in range(HC)]
        ob = [bank(f"ob{t}") for t in range(TT)]

        id_loaded, tab_loaded = sem("id_loaded"), sem("tab_loaded")
        pairs_loaded, x_loaded, in_loaded, out_loaded = ([sem(f"{n}{b}") for b in range(2)] for n in ("pairs_loaded", "x_loaded", "in_loaded", "out_loaded"))
        t_ready, xt_hid, xt_lod = sem("t_ready"), sem("xt_hid"), sem("xt_lod")
        in_hid, in_lod, out_hid, out_lod = sem("in_hid"), sem("in_lod"), sem("out_hid"), sem("out_lod")
        g_ready, gelu_done, act_done, act_hid, act_lod = sem("g_ready"), sem("gelu_done"), sem("act_done"), sem("act_hid"), sem("act_lod")
        y_ready, y_done, y_stored, y_free = sem("y_ready"), sem("y_done"), sem("y_stored"), sem("y_free")
        ids_done, rows_done = sem("ids_done"), sem("rows_done")

        IN, OUT = slice(0, 2 * H0), slice(2 * H0, WCOL)

        block = ctx.enter_context(nc.Block())

        @block.sync
        def _(sp):
            sp.dma_start(ident[:], identity).then_inc(id_loaded, 16)
            sp.dma_start(table[:], tile_table.rearrange("t c -> (t c)").unsqueeze(0)).then_inc(tab_loaded, 16)
            sp.wait_ge(tab_loaded, 16)

            def fetch(n, b):
                e = sp.value_load(table[0:1, bass.ds(2 * n, 1)], min_val=0, max_val=E - 1)
                place = sp.value_load(table[0:1, bass.ds(2 * n + 1, 1)], min_val=0, max_val=SLOTS - TILE)
                sp.wait_ge(in_lod, FC * (n + 1))
                sp.nop(nofuse=True)
                sp.dma_start(w_raw[:, b, :, IN], w_gate[bass.ds(e, 1)].rearrange("o (c p) n -> p (o c) n", p=P)).then_inc(in_loaded[b], 16)
                fetch_pairs(n, b, place)
                sp.wait_ge(out_lod, FC * (n + 1))
                sp.nop(nofuse=True)
                sp.dma_start(w_raw[:, b, :, OUT], w_out[bass.ds(e, 1)].rearrange("o (c p) n -> p (o c) n", p=P)).then_inc(out_loaded[b], 16)

            def fetch_pairs(n, b, place):
                sp.wait_ge(rows_done, n + 1)
                sp.nop(nofuse=True)
                sp.dma_start(pairs[:, b], slot_tokens[bass.ds(place, TILE), :].rearrange("(p t) o -> p (t o)", p=P)).then_inc(pairs_loaded[b], 16)

            fetch(0, 0)
            fetch(1, 1)
            with sp.Fori(0, TURNS) as i:
                fetch(2 * i + 2, 0)
                fetch(2 * i + 3, 1)
            fetch_pairs(LAST + 2, 0, sp.value_load(table[0:1, bass.ds(2 * LAST + 5, 1)], min_val=0, max_val=SLOTS - TILE))
            sp.wait_ge(pairs_loaded[0], 16 * (TURNS + 2))
            sp.wait_ge(pairs_loaded[1], 16 * (TURNS + 1))
            for b in range(2):
                sp.wait_ge(in_loaded[b], 16 * (TURNS + 1))
                sp.wait_ge(out_loaded[b], 16 * (TURNS + 1))

        @block.gpsimd
        def _(pool):
            def gather(n, b):
                pool.wait_ge(ids_done, n + 1)
                pool.nop(nofuse=True)
                pool.wait_ge(t_ready, 2 * (n + 1))
                pool.nop(nofuse=True)
                for t in range(TT):
                    pool.indirect_dma_start(out=xg[:, b, t], out_offset=None, in_=xn_rows,
                                            in_offset=bass.IndirectOffsetOnAxis(ap=ids[:, b, t:t + 1], axis=0)).then_inc(x_loaded[b], 16)

            def scatter(n, b):
                pool.wait_ge(rows_done, n + 3)
                pool.nop(nofuse=True)
                pool.wait_ge(y_done, n + 2)
                pool.nop(nofuse=True)
                for t in range(TT):
                    pool.indirect_dma_start(out=y_rows, out_offset=bass.IndirectOffsetOnAxis(ap=rows[:, b, t:t + 1], axis=0),
                                            in_=y_sb[:, b, t], in_offset=None).then_inc(y_stored, 16)
                pool.wait_ge(y_stored, 32 * (n + 1))
                pool.nop(nofuse=True).then_inc(y_free, 1)

            def split(n, b):
                for h in range(HC):
                    pool.wait_ge(act_done, HC * (n + 1) + h + 1)
                    if h == 0:
                        pool.wait_ge(y_ready, n + 1)
                    nc.gpsimd.tensor_tensor(act_hi[:, b, h], act_f[:, h], zeros[:], ALU.add).then_inc(act_hid, 1)
                    pool.wait_ge(act_hid, HC * n + h + 1)
                    nc.gpsimd.tensor_tensor(act_lo[:, b, h], act_f[:, h], act_hi[:, b, h].bitcast(F32), ALU.subtract).then_inc(act_lod, 1)

            nc.gpsimd.memset(zeros[:], 0.0).then_inc(t_ready, 4)
            nc.gpsimd.memset(credit[:, 7:8], 0.0).then_inc(act_lod, HC)
            pool.wait_ge(t_ready, 4)
            gather(0, 0)
            gather(1, 1)
            split(0, 0)
            gather(2, 0)
            with pool.Fori(0, TURNS) as i:
                for b in range(2):
                    n = 2 * i + b
                    split(n + 1, 1 - b)
                    gather(n + 3, 1 - b)
                    scatter(n, b)
            scatter(LAST, 0)
            pool.wait_ge(x_loaded[0], 32 * (TURNS + 2))
            pool.wait_ge(x_loaded[1], 32 * (TURNS + 1))

        @block.tensor
        def _(pe):
            def three(out, a_hi, a_lo, b_hi, b_lo, start, stop):
                nc.tensor.matmul(out, a_hi, b_hi, start=start, stop=False)
                nc.tensor.matmul(out, a_hi, b_lo, start=False, stop=False)
                return nc.tensor.matmul(out, a_lo, b_hi, start=False, stop=stop)

            def turn(n, b, count):
                pe.wait_ge(x_loaded[b], 32 * count)
                for j in range(2):
                    pe.wait_ge(xt_lod, 2 * n + j + 1)
                    out = tb[j][:].rearrange("p (c s) -> p c s", c=2)
                    for c in range(2):
                        for t in range(TT):
                            mm = nc.tensor.transpose(out[:, c, t * P:(t + 1) * P], xg[:, b, t, (2 * j + c) * P:(2 * j + c + 1) * P], ident[:])
                    mm.then_inc(t_ready, 1)

            def gate_up(n, b):
                pe.wait_ge(xt_lod, 2 * n + 4)
                pe.wait_ge(in_lod, FC * (n + 3))
                for h in range(HC):
                    pe.wait_ge(act_done, HC * n + h + 1)
                    for k in range(2):
                        out = gb[h][:, k * TILE:(k + 1) * TILE]
                        w = k * H0 + h * P
                        for c in range(FC):
                            mm = three(out, w_hi[:, b, c, w:w + P], w_lo[:, b, c, w:w + P], xt_hi[:, b, c], xt_lo[:, b, c], c == 0, c == FC - 1)
                    mm.then_inc(g_ready, 1)

            def down(n, b):
                pe.wait_ge(y_done, n + 1)
                pe.wait_ge(act_lod, HC * (n + 2))
                pe.wait_ge(out_lod, FC * (n + 3))
                for t in range(TT):
                    for h in range(HC):
                        mm = three(ob[t][:], act_hi[:, b, h, t * P:(t + 1) * P], act_lo[:, b, h, t * P:(t + 1) * P],
                                   w_hi[:, b, h, OUT], w_lo[:, b, h, OUT], h == 0, h == HC - 1)
                mm.then_inc(y_ready, 1)

            pe.wait_ge(id_loaded, 16)
            turn(0, 0, 1)
            gate_up(0, 0)
            turn(1, 1, 1)
            with pe.Fori(0, TURNS) as i:
                for b in range(2):
                    n = 2 * i + b
                    gate_up(n + 1, 1 - b)
                    turn(n + 2, b, i + 2)
                    down(n, b)
            down(LAST, 0)

        @block.scalar
        def _(act):
            def in_high(n, b, q, count):
                act.wait_ge(in_loaded[b], 16 * count)
                nc.scalar.copy(w_hi[:, b, q, IN], w_raw[:, b, q, IN]).then_inc(in_hid, 1)

            def out_high(n, b, q, count):
                act.wait_ge(out_loaded[b], 16 * count)
                nc.scalar.copy(w_hi[:, b, q, OUT], w_raw[:, b, q, OUT]).then_inc(out_hid, 1)

            def turned(n, b):
                for j in range(2):
                    act.wait_ge(t_ready, 2 * n + j + 5)
                    nc.scalar.copy(xt_hi[:, b, 2 * j:2 * j + 2], tb[j][:].rearrange("p (c s) -> p c s", c=2)).then_inc(xt_hid, 1)

            def tile(n, b, count):
                for h in range(HC):
                    act.wait_ge(g_ready, HC * n + h + 1)
                    act.wait_ge(act_done, HC * n + h + 3)
                    nc.scalar.activation(gelu[:, h % 2], gb[h][:, 0:TILE], ACT.Gelu_apprx_tanh).then_inc(gelu_done, 1)
                    in_high(n + 1, 1 - b, h, count + b)
                    out_high(n, b, h, count)
                turned(n + 1, 1 - b)

            def rows_of_y(n, b):
                act.wait_ge(y_ready, n + 3)
                act.wait_ge(y_free, n + 1)
                for t in range(TT):
                    y = nc.scalar.copy(y_sb[:, b, t], ob[t][:])
                y.then_inc(y_done, 1)

            for q in range(FC):
                in_high(0, 0, q, 1)
            turned(0, 0)
            tile(0, 0, 1)
            with act.Fori(0, TURNS) as i:
                for b in range(2):
                    n = 2 * i + b
                    tile(n + 1, 1 - b, i + 1 + b)
                    rows_of_y(n, b)
            rows_of_y(LAST, 0)

        @block.vector
        def _(dve):
            def low(out, raw, hi):
                return nc.vector.tensor_tensor(out, raw, hi.bitcast(F32), ALU.subtract)

            def in_low(n, b, q):
                dve.wait_ge(in_hid, FC * n + q + 1)
                low(w_lo[:, b, q, IN], w_raw[:, b, q, IN], w_hi[:, b, q, IN]).then_inc(in_lod, 1)

            def out_low(n, b, q):
                dve.wait_ge(out_hid, FC * n + q + 1)
                low(w_lo[:, b, q, OUT], w_raw[:, b, q, OUT], w_hi[:, b, q, OUT]).then_inc(out_lod, 1)

            def turned(n, b):
                for j in range(2):
                    dve.wait_ge(xt_hid, 2 * n + j + 1)
                    low(xt_lo[:, b, 2 * j:2 * j + 2], tb[j][:].rearrange("p (c s) -> p c s", c=2), xt_hi[:, b, 2 * j:2 * j + 2]).then_inc(xt_lod, 1)

            def tokens(n, b, count):
                dve.wait_ge(pairs_loaded[b], 16 * count)
                dve.wait_ge(t_ready, 2 * n + 2)
                nc.vector.tensor_scalar(ids[:, b], pairs[:, b], 1, None, ALU.arith_shift_right).then_inc(ids_done, 1)

            def tile(n, b, count):
                for h in range(HC):
                    dve.wait_ge(gelu_done, HC * n + h + 1)
                    dve.wait_ge(act_lod, HC * n + h + 1)
                    nc.vector.tensor_tensor(act_f[:, h], gb[h][:, TILE:], gelu[:, h % 2], ALU.mult).then_inc(act_done, 1)
                    in_low(n + 1, 1 - b, h)
                    out_low(n, b, h)
                    if h == 2:
                        dve.wait_ge(y_free, n + 1)
                        nc.vector.tensor_copy(rows[:, b], pairs[:, b]).then_inc(rows_done, 1)
                turned(n + 1, 1 - b)
                tokens(n + 2, b, count + 1)

            nc.vector.memset(credit[:, 0:1], 0.0).then_inc(in_lod, 2 * FC)
            nc.vector.memset(credit[:, 8:9], 0.0).then_inc(out_lod, 2 * FC)
            nc.vector.memset(credit[:, 1:2], 0.0).then_inc(act_done, HC)
            nc.vector.memset(credit[:, 2:3], 0.0).then_inc(xt_lod, 2)
            nc.vector.memset(credit[:, 3:4], 0.0).then_inc(y_done, 1)
            nc.vector.memset(credit[:, 4:5], 0.0).then_inc(y_ready, 2)
            nc.vector.memset(credit[:, 5:6], 0.0).then_inc(y_free, 2)
            nc.vector.memset(credit[:, 6:7], 0.0).then_inc(rows_done, 2)
            tokens(0, 0, 1)
            tokens(1, 1, 1)
            for q in range(FC):
                in_low(0, 0, q)
            turned(0, 0)
            tile(0, 0, 1)
            with dve.Fori(0, TURNS) as i:
                for b in range(2):
                    tile(2 * i + b + 1, 1 - b, i + 1 + b)
    clear(nc, used)


def gated_normed_attention(nc, x_in, y_rows, weights, x_out, ctx_t, gate, wq, wkv, wkv_dca, wo, bq, bkv, ln_w, ln_b, bo, identity, tag):
    FC, CC, HD = D // P, DC // P, D // NHEAD1
    SCALE = HD ** -0.5
    N1 = NHEAD1
    PAIR = 2 * N1
    HG = P // HD
    GROUPS = NHEAD1 // HG
    LINKS = 8 + 2 * ROOT_LINKS
    ST = 3 * HD
    used = []
    with ExitStack() as ctx:
        def sb(name, shape, dt=F32):
            return ctx.enter_context(nc.sbuf_tensor(tag + name, shape, dt))

        def bank(name):
            return ctx.enter_context(nc.psum_tensor(tag + name, [P, 512], F32))

        def sem(name):
            used.append(nc.alloc_semaphore(tag + name))
            return used[-1]

        wq_hi, wq_lo = sb("wq_hi", [P, FC, D], F32R), sb("wq_lo", [P, FC, D], F32R)
        wkv_hi, wkv_lo = sb("wkv_hi", [P, CC, 2 * D], F32R), sb("wkv_lo", [P, CC, 2 * D], F32R)
        wd_hi, wd_lo = sb("wd_hi", [P, CC, 2 * D], F32R), sb("wd_lo", [P, CC, 2 * D], F32R)
        wo_hi, wo_lo = sb("wo_hi", [P, FC, D], F32R), sb("wo_lo", [P, FC, D], F32R)
        ident = sb("ident", [P, P])
        bq_sb, bkv_sb, bo_sb = sb("bq_sb", [P, D]), sb("bkv_sb", [P, 2, 2 * D]), sb("bo_sb", [P, D])
        lnw_sb, lnb_sb = sb("lnw_sb", [P, 4, HD]), sb("lnb_sb", [P, 4, HD])
        gate_t = sb("gate_t", [P, 1])
        x2 = sb("x2", [P, 2, D])
        x_sb = sb("x_sb", [P, 2, 2, D])
        y_sb = sb("y_sb", [P, 2, 2, D])
        w_here = sb("w_here", [P, 4])
        stats, mv, rstd = sb("stats", [P, 2, 6]), sb("mv", [P, 2, 2]), sb("rstd", [P, 2])
        root = [sb(f"root{n}", [P, 2]) for n in range(3)]
        xt_hi, xt_lo = sb("xt_hi", [P, FC, S], F32R), sb("xt_lo", [P, FC, S], F32R)
        ctx_raw = sb("ctx_raw", [P, CC, S])
        ctx_hi, ctx_lo = sb("ctx_hi", [P, CC, S], F32R), sb("ctx_lo", [P, CC, S], F32R)
        dca_hi, dca_lo = sb("dca_hi", [P, CC, P], F32R), sb("dca_lo", [P, CC, P], F32R)
        nrm = sb("nrm", [P, 2, 4, D])
        sq = sb("sq", [P, 2, D])
        xn = sq
        hsum, hvar, hrstd = sb("hsum", [P, 4 * NHEAD1]), sb("hvar", [P, 4 * NHEAD1]), sb("hrstd", [P, 4 * NHEAD1])
        hroot = [sb(f"hroot{n}", [P, 4 * NHEAD1]) for n in range(3)]
        col_mean = [x[:].rearrange("p (a h) -> p a h", a=4) for x in [hsum, hvar] + hroot]
        v_raw = sb("v_raw", [P, 2, D])
        v_hi, v_lo = sb("v_hi", [P, 2, NHEAD1, P], F32R), sb("v_lo", [P, 2, NHEAD1, P], F32R)
        stack = sb("stack", [P, 2, 4, HG, ST])
        qk = sb("qk", [ST, 2, 2 * S], F32R)
        prob = sb("prob", [P, 4, 2, S])
        mx, nbias = sb("mx", [P, 2, 2, 2]), sb("nbias", [P, 2, 2, 2])
        rsum, rinv = sb("rsum", [P, 2, 2, 2]), sb("rinv", [P, 4, 2, 2])
        pt_hi, pt_lo = sb("pt_hi", [P, 2, 2, S], F32R), sb("pt_lo", [P, 2, 2, S], F32R)
        ot_hi, ot_lo = sb("ot_hi", [P, 2, S], F32R), sb("ot_lo", [P, 2, S], F32R)
        credit = sb("credit", [P, 11])

        pjb, qkb = bank("pjb"), bank("qkb")
        sc = [bank("sc0"), bank("sc1")]
        ptb, avb = bank("ptb"), bank("avb")
        ob = [bank("ob0"), bank("ob1")]

        c_loaded, w_loaded, w_hid, w_lod = sem("c_loaded"), [sem("w_loaded0"), sem("w_loaded1")], sem("w_hid"), sem("w_lod")
        gate_done, zeroed = sem("gate_done"), sem("zeroed")
        x_loaded, x_used, ctx_loaded, y_loaded = sem("x_loaded"), sem("x_used"), sem("ctx_loaded"), sem("y_loaded")
        x_stored, w_meaned, w_centered = [sem("x_stored0"), sem("x_stored1")], sem("w_meaned"), sem("w_centered")
        y_used, link_done, xn_done, ctx_hid, ctx_lod = sem("y_used"), sem("link_done"), sem("xn_done"), sem("ctx_hid"), sem("ctx_lod")
        pj_ready, pj_hid, pj_taken = sem("pj_ready"), sem("pj_hid"), sem("pj_taken")
        sq_done, nrm_link = sem("sq_done"), sem("nrm_link")
        st_hid, st_done, v_hid, v_done = sem("st_hid"), sem("st_done"), sem("v_hid"), sem("v_done")
        qk_ready, qk_done = sem("qk_ready"), sem("qk_done")
        s_ready, s_max, s_bias, e_done, r_done, p_done = sem("s_ready"), sem("s_max"), sem("s_bias"), sem("e_done"), sem("r_done"), sem("p_done")
        t_ready, pt_hid, pt_lod = sem("t_ready"), sem("pt_hid"), sem("pt_lod")
        av_ready, ot_hid, ot_lod = sem("av_ready"), sem("ot_hid"), sem("ot_lod")
        o_ready, o_free = sem("o_ready"), sem("o_free")

        pieces = [(wq, wq_hi[:], wq_lo[:]), (wkv, wkv_hi[:], wkv_lo[:]), (wkv_dca, wd_hi[:], wd_lo[:]), (wo, wo_hi[:], wo_lo[:])]
        consts = [(ident[:], identity), (bq_sb[:], bq), (bkv_sb[:], bkv), (bo_sb[:], bo), (lnw_sb[:], ln_w), (lnb_sb[:], ln_b), (gate_t[:], gate)]

        def raw(n):
            a, b = pieces[n][0].shape[1:]
            return nrm[:, n % 2].rearrange("p r d -> p (r d)").rearrange("p (a b) -> p a b", a=a)

        WHEN = {}

        def plan(n, *what):
            WHEN.setdefault(n, []).append(what)

        for k in range(TOPK):
            plan(k - 21, "sum", k)
        for n in range(3):
            plan(n - 20, "norm", n)
        for j in range(2):
            plan(j - 17, "turn", j)
            plan(j - 16, "turned", j)
        plan(-10, "res", 0)
        for j in range(2, 8):
            plan(j - 16, "proj", j)
            plan(j - 15, "take", j)
        for half in range(2):
            plan(2 * half - 11, "square", half)
            plan(2 * half - 10, "sumsq", half)
        for n in range(2):
            plan(n - 7, "root", n)
        for g in range(GROUPS):
            for n in range(3):
                plan(HG * g - 6 + n, "piece", (g, n))
            plan(HG * g - 3, "stack", g)
        for h in range(HG):
            plan(h - 4, "v", (0, h))
            plan(h + 3, "v", (1, h))
        FIRST, AHEAD = min(WHEN), 5

        def due(u, last, what):
            batches = range(2) if u < AHEAD or last else range(4)
            return [(bb, n) for bb in batches for w, n in WHEN.get(u - N1 * bb, []) if w == what]

        def here(u, last):
            return 0 <= u < PAIR or (u >= PAIR and not last)

        def all_steps(eng, step):
            for u in range(FIRST, AHEAD):
                step(0, u, False)
            with eng.Fori(0, B // 2 - 1) as i:
                for u in range(AHEAD, PAIR + AHEAD):
                    step(i, u, False)
            for u in range(AHEAD, PAIR + AHEAD):
                step(B // 2 - 1, u, True)

        def diag(v, g2, h):
            return v[:, :, 2 * g2 * HG:2 * (g2 + 1) * HG].rearrange("p k (g h) c -> p k g h c", h=HG)[:, :, :, h, h * HD:(h + 1) * HD]

        def v_cols(g2, h):
            return v_raw[:, :, 2 * g2 * P:2 * (g2 + 1) * P].rearrange("p k (g c) -> p k g c", c=P)[:, :, :, h * HD:(h + 1) * HD]

        def group_cols(bb, g):
            return nrm[:, bb, :, g * P:(g + 1) * P].rearrange("p r (h c) -> p r h c", h=HG)

        def head_cols(w):
            return w.rearrange("p a (h c) -> p a h c", h=N1)

        block = ctx.enter_context(nc.Block())

        @block.sync
        def _(sp):
            for dst, src in consts:
                sp.dma_start(dst, src).then_inc(c_loaded, 16)
            for n, (src, _, _) in enumerate(pieces):
                if n >= 2:
                    sp.wait_ge(w_lod, n - 1)
                sp.dma_start(raw(n), src).then_inc(w_loaded[n % 2], 16)
            with sp.Fori(0, B // 2) as i:
                for bb in range(2):
                    b = 2 * i + bb
                    sp.wait_ge(x_used, b + 1)
                    sp.nop(nofuse=True)
                    sp.dma_start(x2[:], x_in[bass.ds(b * S, S), :].rearrange("(t p) d -> p t d", p=P)).then_inc(x_loaded, 16)
                    sp.wait_ge(y_used, b + 1)
                    sp.nop(nofuse=True)
                    sp.dma_start(y_sb[:], y_rows[bass.ds(TOPK * S * b, TOPK * S), :].rearrange("(t p k) d -> p t k d", t=2, k=TOPK)).then_inc(y_loaded, 16)
                    sp.wait_ge(ctx_lod, b + 1)
                    sp.nop(nofuse=True)
                    sp.dma_start(ctx_raw[:], ctx_t[bass.ds(b, 1)].rearrange("o (c p) s -> p (o c) s", p=P)).then_inc(ctx_loaded, 16)

        @block.tensor
        def _(pe):
            def three(out, a_hi, a_lo, b_hi, b_lo, start, stop):
                nc.tensor.matmul(out, a_hi, b_hi, start=start, stop=False)
                nc.tensor.matmul(out, a_hi, b_lo, start=False, stop=False)
                return nc.tensor.matmul(out, a_lo, b_hi, start=False, stop=stop)

            def turn_x(b, j):
                pe.wait_ge(xn_done, b + 1)
                pe.wait_ge(pj_taken, 8 * b + j + 1)
                out = pjb[:].rearrange("p (c s) -> p c s", c=2)
                for c in range(2):
                    for t in range(2):
                        mm = nc.tensor.transpose(out[:, c, t * P:(t + 1) * P], xn[:, t, (2 * j + c) * P:(2 * j + c + 1) * P], ident[:])
                mm.then_inc(pj_ready, 1)

            def projection(b, j):
                pe.wait_ge(pj_taken, 8 * b + j + 1)
                t = (j % 2) * P
                if j < 4:
                    for c in range(FC):
                        mm = three(pjb[:], xt_hi[:, c, t:t + P], xt_lo[:, c, t:t + P], wq_hi[:, c], wq_lo[:, c], c == 0, c == FC - 1)
                else:
                    w = slice((j - 4) // 2 * D, ((j - 4) // 2 + 1) * D)
                    if j == 4:
                        pe.wait_ge(ctx_lod, b + 2)
                    for c in range(CC):
                        mm = three(pjb[:], ctx_hi[:, c, t:t + P], ctx_lo[:, c, t:t + P], wkv_hi[:, c, w], wkv_lo[:, c, w],
                                   c == 0, c == CC - 1 and t > 0)
                    if t == 0:
                        for c in range(CC):
                            mm = three(pjb[:], dca_hi[:, c], dca_lo[:, c], wd_hi[:, c, w], wd_lo[:, c, w], False, c == CC - 1)
                mm.then_inc(pj_ready, 1)

            def turn_qk(i, u):
                bb, h = divmod(u, N1)
                pe.wait_ge(st_done, GROUPS * (2 * i + bb) + h // HG + 1)
                pe.wait_ge(qk_done, PAIR * i + u + 1)
                for r in range(4):
                    mm = nc.tensor.transpose(qkb[0:ST, r * P:(r + 1) * P], stack[:, (h // HG) % 2, r, h % HG], ident[:])
                mm.then_inc(qk_ready, 1)

            def scores(i, u):
                pe.wait_ge(qk_done, PAIR * i + u + 2)
                pe.wait_ge(e_done, PAIR * i + u + 1)
                for t in range(2):
                    mm = nc.tensor.matmul(sc[u % 2][:, t * S:(t + 1) * S], qk[:, u % 2, t * P:(t + 1) * P], qk[:, u % 2, S:], start=True, stop=True)
                mm.then_inc(s_ready, 1)

            def turn_p(i, u):
                pe.wait_ge(p_done, PAIR * i + u + 1)
                pe.wait_ge(pt_lod, PAIR * i + u + 1)
                out = ptb[:].rearrange("p (k s) -> p k s", k=2)
                for k in range(2):
                    for t in range(2):
                        mm = nc.tensor.transpose(out[:, k, t * P:(t + 1) * P], prob[:, u % 4, t, k * P:(k + 1) * P], ident[:])
                mm.then_inc(t_ready, 1)

            def values(i, u):
                bb, h = divmod(u, N1)
                pe.wait_ge(pt_lod, PAIR * i + u + 2)
                if h % HG == 0:
                    pe.wait_ge(v_done, 2 * HG * (2 * i + bb) + HG * (h // (2 * HG) + 1))
                    pe.wait_ge(ot_lod, GROUPS * (2 * i + bb) + h // HG + 1)
                for k in range(2):
                    mm = three(avb[:, 0:S], v_hi[:, k, h], v_lo[:, k, h], pt_hi[:, u % 2, k], pt_lo[:, u % 2, k],
                               h % HG == 0 and k == 0, h % HG == HG - 1 and k == 1)
                mm.then_inc(av_ready, 1)

            def project(i, bb, g):
                pe.wait_ge(ot_lod, GROUPS * (2 * i + bb) + g + 2)
                if g == 0:
                    pe.wait_ge(o_free, 2 * i + bb + 1)
                for t in range(2):
                    mm = three(ob[t][:], ot_hi[:, g % 2, t * P:(t + 1) * P], ot_lo[:, g % 2, t * P:(t + 1) * P], wo_hi[:, g], wo_lo[:, g],
                               g == 0, g == GROUPS - 1)
                if g == GROUPS - 1:
                    mm.then_inc(o_ready, 1)

            pe.wait_ge(c_loaded, 16 * len(consts))
            pe.wait_ge(w_lod, len(pieces))
            pe.wait_ge(zeroed, 3)

            def step(i, u, last):
                if here(u + 2, last):
                    turn_qk(i, u + 2)
                if here(u + 1, last):
                    scores(i, u + 1)
                if here(u - 4, last):
                    values(i, u - 4)
                if here(u - 5, last) and (u - 5) % HG == HG - 1:
                    project(i, (u - 5) // N1, (u - 5) % N1 // HG)
                if here(u - 2, last):
                    turn_p(i, u - 2)
                for bb, j in due(u, last, "turn"):
                    turn_x(2 * i + bb, j)
                for bb, j in due(u, last, "proj"):
                    projection(2 * i + bb, j)

            all_steps(pe, step)

        @block.scalar
        def _(act):
            act.wait_ge(c_loaded, 16 * len(consts))
            nc.scalar.activation(gate_t[:], gate_t[:], ACT.Tanh).then_inc(gate_done, 1)
            for n in range(len(pieces)):
                if n < 3:
                    act.wait_ge(w_centered, n + 1)
                else:
                    act.wait_ge(w_loaded[n % 2], 16 * (n // 2 + 1))
                nc.scalar.copy(pieces[n][1], raw(n)).then_inc(w_hid, 1)
            act.wait_ge(zeroed, 3)

            def step(i, u, last):
                for bb, j in due(u, last, "turned"):
                    b = 2 * i + bb
                    if j == 0:
                        act.wait_ge(ctx_loaded, 16 * b + 16)
                        act.wait_ge(pj_taken, 8 * b + 1)
                        nc.scalar.copy(ctx_hi[:, :, DCA:], ctx_raw[:, :, DCA:])
                        nc.scalar.copy(dca_hi[:, :, 0:DCA], ctx_raw[:, :, 0:DCA]).then_inc(ctx_hid, 1)
                    act.wait_ge(pj_ready, 8 * b + j + 1)
                    nc.scalar.copy(xt_hi[:, 2 * j:2 * j + 2], pjb[:].rearrange("p (c s) -> p c s", c=2)).then_inc(pj_hid, 1)
                if here(u - 3, last):
                    act.wait_ge(t_ready, PAIR * i + u - 2)
                    nc.scalar.copy(pt_hi[:, (u - 3) % 2], ptb[:].rearrange("p (k s) -> p k s", k=2)).then_inc(pt_hid, 1)
                if here(u + 2, last):
                    act.wait_ge(qk_ready, PAIR * i + u + 3)
                    nc.scalar.copy(qk[:, u % 2], qkb[0:ST, :]).then_inc(qk_done, 1)
                if here(u, last):
                    act.wait_ge(s_bias, PAIR * i + u + 1)
                    s = sc[u % 2][:].rearrange("p (t s) -> p t s", t=2)
                    for k, keys in ((0, slice(0, DCA)), (1, slice(DCA, S))):
                        for t in range(2):
                            e = nc.scalar.activation(prob[:, u % 4, t, keys], s[:, t, keys], ACT.Exp, bias=nbias[:, u % 2, k, t:t + 1],
                                                     scale=SCALE, accum_out=rsum[:, u % 2, k, t:t + 1])
                    e.then_inc(e_done, 1)
                if here(u - 4, last) and (u - 4) % HG == HG - 1:
                    act.wait_ge(av_ready, PAIR * i + u - 2)
                    nc.scalar.copy(ot_hi[:, (u - 4) // HG % 2], avb[:, 0:S]).then_inc(ot_hid, 1)
                for bb, half in due(u, last, "square"):
                    act.wait_ge(pj_taken, 8 * (2 * i + bb) + 5 + 2 * half)
                    if half:
                        act.wait_ge(link_done, LINKS * (2 * i + bb) + 6 + ROOT_LINKS)
                    nc.scalar.activation(sq[:], nrm[:, bb % 2, 2 * half:2 * half + 2], ACT.Square).then_inc(sq_done, 1)
                for bb, (g2, h) in due(u, last, "v"):
                    b = 2 * i + bb
                    act.wait_ge(pj_taken, 8 * b + 9)
                    if u >= AHEAD or bb > 0:
                        act.wait_ge(av_ready, N1 * b - N1 + 2 * HG * (g2 + 1) + 1)
                    nc.scalar.copy(diag(v_hi, g2, h), v_cols(g2, h)).then_inc(v_hid, 1)
                for bb, g in due(u, last, "stack"):
                    b = 2 * i + bb
                    act.wait_ge(nrm_link, 3 * GROUPS * b + 3 * g + 3)
                    if u >= AHEAD:
                        act.wait_ge(qk_ready, N1 * b + (g - 1) * HG)
                    out = stack[:, g % 2]
                    nc.scalar.copy(out[:, :, :, 0:HD].bitcast(F32R), group_cols(bb % 2, g))
                    nc.scalar.copy(out[:, 0:2, :, HD:2 * HD].bitcast(F32R), group_cols(bb % 2, g)[:, 0:2])
                    nc.scalar.copy(out[:, 2:4, :, 2 * HD:].bitcast(F32R), group_cols(bb % 2, g)[:, 2:4]).then_inc(st_hid, 1)
                if here(u - 5, last) and (u - 5) % N1 == N1 - 1:
                    bb = (u - 5) // N1
                    act.wait_ge(o_free, 2 * i + bb + 2)
                    act.dma_start(x_out[bass.ds((2 * i + bb) * S, S), :].rearrange("(t p) d -> p t d", p=P), x_sb[:, bb]).then_inc(x_stored[bb], 16)

            all_steps(act, step)
            for bb in range(2):
                act.wait_ge(x_stored[bb], 16 * (B // 2) + 16)

        @block.gpsimd
        def _(pool):
            T = nc.gpsimd.tensor_tensor

            def step(i, u, last):
                if here(u - 1, last):
                    pool.wait_ge(r_done, PAIR * i + u)
                    p = prob[:, (u - 1) % 4]
                    T(p[:, :, 0:DCA], p[:, :, 0:DCA], rinv[:, (u - 1) % 4, 0].unsqueeze(2).to_broadcast([P, 2, DCA]), ALU.mult)
                    T(p[:, :, DCA:], p[:, :, DCA:], rinv[:, (u - 1) % 4, 1].unsqueeze(2).to_broadcast([P, 2, S - DCA]), ALU.mult).then_inc(p_done, 1)
                for bb, (g, n) in due(u, last, "piece"):
                    b = 2 * i + bb
                    x = group_cols(bb % 2, g)
                    if n == 0:
                        pool.wait_ge(link_done, LINKS * (b + 1))
                        r = hrstd[:].rearrange("p (r h) -> p r h", r=4)[:, :, g * HG:(g + 1) * HG].unsqueeze(3).to_broadcast([P, 4, HG, HD])
                        T(x, x, r, ALU.mult).then_inc(nrm_link, 1)
                    else:
                        pool.wait_ge(nrm_link, 3 * GROUPS * b + 3 * g + n)
                        c, op = ((lnw_sb, ALU.mult), (lnb_sb, ALU.add))[n - 1]
                        T(x, x, c[:].unsqueeze(2).to_broadcast([P, 4, HG, HD]), op).then_inc(nrm_link, 1)

            all_steps(pool, step)

        @block.vector
        def _(dve):
            V = nc.vector
            def low(out, raw_in, hi):
                return V.tensor_tensor(out, raw_in, hi.bitcast(F32), ALU.subtract)

            V.memset(credit[:, 0:1], 0.0).then_inc(x_stored[0], 16)
            V.memset(credit[:, 1:2], 0.0).then_inc(x_stored[1], 16)
            V.memset(credit[:, 2:3], 0.0).then_inc(ctx_lod, 1)
            V.memset(credit[:, 3:4], 0.0).then_inc(pj_taken, 1)
            V.memset(credit[:, 9:10], 0.0).then_inc(qk_done, 1)
            V.memset(credit[:, 10:11], 0.0).then_inc(ot_lod, 1)
            V.memset(credit[:, 4:5], 0.0).then_inc(o_free, 1)
            V.memset(credit[:, 5:6], 0.0).then_inc(x_used, 1)
            V.memset(credit[:, 6:7], 0.0).then_inc(e_done, 2)
            V.memset(credit[:, 7:8], 0.0).then_inc(pt_lod, 1)
            V.memset(credit[:, 8:9], 0.0).then_inc(av_ready, 1)
            V.memset(v_hi[:].bitcast(F32), 0.0).then_inc(zeroed, 1)
            V.memset(v_lo[:].bitcast(F32), 0.0)
            V.memset(ctx_hi[:].bitcast(F32), 0.0)
            V.memset(ctx_lo[:].bitcast(F32), 0.0).then_inc(zeroed, 1)
            V.memset(dca_hi[:].bitcast(F32), 0.0)
            V.memset(dca_lo[:].bitcast(F32), 0.0).then_inc(zeroed, 1)
            V.memset(rstd[:], 0.0).then_inc(y_used, 1)
            dve.wait_ge(c_loaded, 16 * len(consts))
            dve.wait_ge(gate_done, 1)
            V.tensor_scalar(bo_sb[:], bo_sb[:], gate_t[:, 0:1], None, ALU.mult).then_inc(zeroed, 1)

            def center(n, cols):
                m = col_mean[n][:, 0:cols.shape[1]]
                V.tensor_reduce(m, head_cols(cols), AX.X, ALU.add).then_inc(w_meaned, 1)
                dve.wait_ge(w_meaned, 2 * n + 1)
                V.tensor_scalar(m, m, -1.0 / HD, None, ALU.mult).then_inc(w_meaned, 1)
                dve.wait_ge(w_meaned, 2 * n + 2)
                return V.tensor_tensor(head_cols(cols), head_cols(cols), m.unsqueeze(3).to_broadcast([P, cols.shape[1], N1, HD]), ALU.add)

            def split(n):
                dve.wait_ge(w_hid, n + 1)
                low(pieces[n][2], raw(n), pieces[n][1]).then_inc(w_lod, 1)

            for n in range(3):
                dve.wait_ge(w_loaded[n % 2], 16 * (n // 2 + 1))
                center(n, raw(n)[:, :, 0:D]).then_inc(w_centered, 1)
                if n > 0:
                    split(n - 1)
            split(2)
            center(3, bq_sb[:].unsqueeze(1)).then_inc(zeroed, 1)
            center(4, bkv_sb[:, :, 0:D]).then_inc(zeroed, 1)
            split(3)
            dve.wait_ge(zeroed, 6)

            def link(op, at):
                op.then_inc(link_done, 1)
                dve.wait_ge(link_done, at)
                return at

            def add_experts(b, k):
                at = LINKS * b
                if k == 0:
                    dve.wait_ge(x_loaded, 16 * b + 16)
                    dve.wait_ge(y_loaded, 16 * b + 16)
                    V.tensor_copy(w_here[:], weights[:, bass.ds(4 * b, 4)]).then_inc(link_done, 1)
                dve.wait_ge(link_done, at + 1 + k)
                for t in range(2):
                    l = V.scalar_tensor_tensor(x2[:, t], y_sb[:, t, k], w_here[:, 2 * t + k:2 * t + k + 1], x2[:, t], ALU.mult, ALU.add)
                l.then_inc(link_done, 1)
                if k == 1:
                    dve.wait_ge(link_done, at + 3)
                    dve.nop(nofuse=True).then_inc(y_used, 1)

            def normalize(b, n):
                at = LINKS * b + 3
                if n == 0:
                    for t in range(2):
                        l = V.bn_stats(stats[:, t], x2[:, t])
                    link(l, at + 1)
                    dve.nop(nofuse=True)
                    for t in range(2):
                        l = V.bn_aggr(mv[:, t], stats[:, t])
                    l.then_inc(link_done, 1)
                else:
                    inverse_root(dve, V, link_done, at + 2, mv[:, :, 1], LN_EPS, root, rstd[:], n - 1)
                if n == 2:
                    for t in range(2):
                        l = V.tensor_scalar(xn[:, t], x2[:, t], mv[:, t, 0:1], rstd[:, t:t + 1], ALU.subtract, ALU.mult)
                    l.then_inc(xn_done, 1)

            def take(i, bb, j):
                dve.wait_ge(pj_ready, 8 * (2 * i + bb) + j + 1)
                if j == 6 and bb > 0:
                    dve.wait_ge(v_done, 2 * HG * (2 * i + bb))
                if j < 4:
                    V.tensor_tensor(nrm[:, bb % 2, j - 2], pjb[:], bq_sb[:], ALU.add).then_inc(pj_taken, 1)
                elif j < 6:
                    V.tensor_tensor(nrm[:, bb % 2, j - 2], pjb[:], bkv_sb[:, j - 4, 0:D], ALU.add).then_inc(pj_taken, 1)
                else:
                    V.tensor_tensor(v_raw[:, j - 6], pjb[:], bkv_sb[:, j - 6, D:], ALU.add).then_inc(pj_taken, 1)

            def step(i, u, last):
                for bb, j in due(u, last, "take"):
                    take(i, bb, j)
                for bb, j in due(u, last, "turned"):
                    b = 2 * i + bb
                    if j == 0:
                        dve.wait_ge(ctx_hid, b + 1)
                        low(ctx_lo[:, :, DCA:], ctx_raw[:, :, DCA:], ctx_hi[:, :, DCA:])
                        low(dca_lo[:, :, 0:DCA], ctx_raw[:, :, 0:DCA], dca_hi[:, :, 0:DCA]).then_inc(ctx_lod, 1)
                    dve.wait_ge(pj_hid, 2 * b + j + 1)
                    low(xt_lo[:, 2 * j:2 * j + 2], pjb[:].rearrange("p (c s) -> p c s", c=2), xt_hi[:, 2 * j:2 * j + 2]).then_inc(pj_taken, 1)
                if here(u - 1, last):
                    v = u - 1
                    dve.wait_ge(e_done, PAIR * i + v + 3)
                    V.reciprocal(rinv[:, v % 4], rsum[:, v % 2]).then_inc(r_done, 1)
                if here(u - 3, last):
                    v = u - 3
                    dve.wait_ge(pt_hid, PAIR * i + v + 1)
                    low(pt_lo[:, v % 2], ptb[:].rearrange("p (k s) -> p k s", k=2), pt_hi[:, v % 2]).then_inc(pt_lod, 1)
                if here(u + 1, last):
                    v = u + 1
                    dve.wait_ge(s_ready, PAIR * i + v + 1)
                    s = sc[v % 2][:].rearrange("p (t s) -> p t s", t=2)
                    V.tensor_reduce(mx[:, v % 2, 0], s[:, :, 0:DCA], AX.X, ALU.max)
                    V.tensor_reduce(mx[:, v % 2, 1], s[:, :, DCA:], AX.X, ALU.max).then_inc(s_max, 1)
                    dve.wait_ge(s_max, PAIR * i + v + 1)
                    V.tensor_scalar(nbias[:, v % 2], mx[:, v % 2], -SCALE, None, ALU.mult).then_inc(s_bias, 1)
                if here(u - 4, last) and (u - 4) % HG == HG - 1:
                    n = (u - 4) // HG
                    dve.wait_ge(ot_hid, 2 * GROUPS * i + n + 1)
                    low(ot_lo[:, n % 2], avb[:, 0:S], ot_hi[:, n % 2]).then_inc(ot_lod, 1)
                if here(u - 5, last) and (u - 5) % N1 == N1 - 1:
                    bb = (u - 5) // N1
                    dve.wait_ge(o_ready, 2 * i + bb + 1)
                    for t in range(2):
                        o = V.scalar_tensor_tensor(x_sb[:, bb, t], ob[t][:], gate_t[:, 0:1], x_sb[:, bb, t], ALU.mult, ALU.add)
                    o.then_inc(o_free, 1)
                for bb, k in due(u, last, "sum"):
                    add_experts(2 * i + bb, k)
                for bb, n in due(u, last, "norm"):
                    normalize(2 * i + bb, n)
                for bb, _ in due(u, last, "res"):
                    dve.wait_ge(x_stored[bb % 2], 16 * (i + bb // 2) + 16)
                    for t in range(2):
                        l = V.tensor_tensor(x_sb[:, bb % 2, t], x2[:, t], bo_sb[:], ALU.add)
                    l.then_inc(x_used, 1)
                for bb, half in due(u, last, "sumsq"):
                    b = 2 * i + bb
                    dve.wait_ge(sq_done, 2 * b + half + 1)
                    V.tensor_reduce(hsum[:, half * 2 * N1:(half + 1) * 2 * N1], sq[:].rearrange("p r (h c) -> p (r h) c", h=N1),
                                    AX.X, ALU.add).then_inc(link_done, 1)
                for bb, n in due(u, last, "root"):
                    b = 2 * i + bb
                    at = LINKS * b + 7 + ROOT_LINKS
                    if n == 0:
                        dve.wait_ge(link_done, at)
                        link(V.tensor_scalar(hvar[:], hsum[:], 1.0 / HD, None, ALU.mult), at + 1)
                        if u >= AHEAD:
                            dve.wait_ge(nrm_link, 3 * GROUPS * b - 2)
                    inverse_root(dve, V, link_done, at + 1, hvar[:], HEAD_EPS, hroot, hrstd[:], n)
                for bb, (g2, h) in due(u, last, "v"):
                    dve.wait_ge(v_hid, 2 * HG * (2 * i + bb) + HG * g2 + h + 1)
                    low(diag(v_lo, g2, h), v_cols(g2, h), diag(v_hi, g2, h)).then_inc(v_done, 1)
                for bb, g in due(u, last, "stack"):
                    out = stack[:, g % 2]
                    dve.wait_ge(st_hid, GROUPS * (2 * i + bb) + g + 1)
                    V.tensor_tensor(out[:, 0:2, :, 2 * HD:], group_cols(bb % 2, g)[:, 0:2], out[:, 0:2, :, 0:HD], ALU.subtract)
                    V.tensor_tensor(out[:, 2:4, :, HD:2 * HD], group_cols(bb % 2, g)[:, 2:4], out[:, 2:4, :, 0:HD], ALU.subtract).then_inc(st_done, 1)

            all_steps(dve, step)
    clear(nc, used)

def feed_forward(nc, x_in, x_out, w1, b1, w2, b2, gate, identity, tag):
    CH = 512
    FC, TC, HC = D // P, CH // P, H1 // P
    CHUNKS = TOK // CH
    used = []
    with ExitStack() as ctx:
        def sb(name, shape, dt=F32):
            return ctx.enter_context(nc.sbuf_tensor(tag + name, shape, dt))

        def bank(name):
            return ctx.enter_context(nc.psum_tensor(tag + name, [P, 512], F32))

        def sem(name):
            used.append(nc.alloc_semaphore(tag + name))
            return used[-1]

        w1_hi, w1_lo = sb("w1_hi", [P, FC, H1], F32R), sb("w1_lo", [P, FC, H1], F32R)
        w2_hi, w2_lo = sb("w2_hi", [P, HC, D], F32R), sb("w2_lo", [P, HC, D], F32R)
        ident, b1_sb, b2_sb, gate_t = sb("ident", [P, P]), sb("b1_sb", [P, HC]), sb("b2_sb", [P, D]), sb("gate_t", [P, 1])
        x_sb = sb("x_sb", [P, 2, TC, D])
        xn = sb("xn", [P, TC, D])
        stats, mv, rstd = sb("stats", [P, TC, 6]), sb("mv", [P, TC, 2]), sb("rstd", [P, TC])
        root = [sb(f"root{n}", [P, TC]) for n in range(3)]
        xt_hi, xt_lo = sb("xt_hi", [P, 2, FC, CH], F32R), sb("xt_lo", [P, 2, FC, CH], F32R)
        h_f = sb("h_f", [P, 2, CH])
        h_hi, h_lo = sb("h_hi", [P, 2, CH], F32R), sb("h_lo", [P, 2, CH], F32R)
        credit = sb("credit", [P, 6])

        tb = [bank("tb0"), bank("tb1")]
        hb = [bank("hb0"), bank("hb1")]
        ob = [bank(f"ob{t}") for t in range(TC)]

        c_loaded, w_loaded, w_hid, w_lod = sem("c_loaded"), [sem("w_loaded0"), sem("w_loaded1")], sem("w_hid"), sem("w_lod")
        gate_done, bias_done, link_done = sem("gate_done"), sem("bias_done"), sem("link_done")
        x_loaded, x_stored = [sem("x_loaded0"), sem("x_loaded1")], [sem("x_stored0"), sem("x_stored1")]
        xn_done, t_ready, xt_hid, xt_lod = sem("xn_done"), sem("t_ready"), sem("xt_hid"), sem("xt_lod")
        h_ready, gelu_done, h_hid, h_lod = sem("h_ready"), sem("gelu_done"), sem("h_hid"), sem("h_lod")
        o_ready, o_done = sem("o_ready"), sem("o_done")

        consts = [(ident[:], identity), (b1_sb[:], b1), (b2_sb[:], b2), (gate_t[:], gate)]
        pieces = [(w1[:, c:c + 1], w1_hi[:, c:c + 1], w1_lo[:, c:c + 1]) for c in range(FC)]
        pieces += [(w2[:, h:h + 4], w2_hi[:, h:h + 4], w2_lo[:, h:h + 4]) for h in range(0, HC, 4)]

        def raw(n):
            a = pieces[n][0].shape[1]
            return x_sb[:, n % 2].rearrange("p t d -> p (t d)").rearrange("p (a b) -> p a b", a=a)

        NORM = {2: 0, 3: 1, 4: 2, 5: 3, 6: 4}
        TURN = {7 + c: c for c in range(FC)}

        def all_chunks(eng, first, chunk):
            first()
            with eng.Fori(0, CHUNKS // 2 - 1) as i:
                for b in range(2):
                    chunk(i, b, False)
            for b in range(2):
                chunk(CHUNKS // 2 - 1, b, b == 1)

        block = ctx.enter_context(nc.Block())

        @block.sync
        def _(sp):
            for dst, src in consts:
                sp.dma_start(dst, src).then_inc(c_loaded, 16)
            for n, (src, _, _) in enumerate(pieces):
                if n >= 2:
                    sp.wait_ge(w_lod, n - 1)
                sp.dma_start(raw(n), src).then_inc(w_loaded[n % 2], 16)
            sp.wait_ge(w_lod, len(pieces))
            with sp.Fori(0, CHUNKS // 2) as i:
                for b in range(2):
                    sp.wait_ge(x_stored[b], 16 * i + 16)
                    sp.nop(nofuse=True)
                    sp.dma_start(x_sb[:, b], x_in[bass.ds((2 * i + b) * CH, CH), :].rearrange("(t p) d -> p t d", p=P)).then_inc(x_loaded[b], 16)

        @block.tensor
        def _(pe):
            def three(out, a_hi, a_lo, b_hi, b_lo, start, stop):
                nc.tensor.matmul(out, a_hi, b_hi, start=start, stop=False)
                nc.tensor.matmul(out, a_hi, b_lo, start=False, stop=False)
                return nc.tensor.matmul(out, a_lo, b_hi, start=False, stop=stop)

            def turn(n, c):
                pe.wait_ge(xn_done, n + 1)
                pe.wait_ge(xt_lod, FC * n + c + 1)
                for t in range(TC):
                    mm = nc.tensor.transpose(tb[c % 2][:, t * P:(t + 1) * P], xn[:, t, c * P:(c + 1) * P], ident[:])
                mm.then_inc(t_ready, 1)

            def hidden(n, b, j):
                pe.wait_ge(gelu_done, HC * n + j + 1)
                if j == 0:
                    pe.wait_ge(xt_lod, FC * n + FC + 2)
                for c in range(FC):
                    mm = three(hb[j % 2][:], w1_hi[:, c, j * P:(j + 1) * P], w1_lo[:, c, j * P:(j + 1) * P], xt_hi[:, b, c], xt_lo[:, b, c], c == 0, c == FC - 1)
                mm.then_inc(h_ready, 1)

            def out(n, j):
                pe.wait_ge(h_lod, HC * n + j + 3)
                if j == 0:
                    pe.wait_ge(o_done, n + 1)
                for t in range(TC):
                    mm = three(ob[t][:], h_hi[:, j % 2, t * P:(t + 1) * P], h_lo[:, j % 2, t * P:(t + 1) * P], w2_hi[:, j], w2_lo[:, j], j == 0, j == HC - 1)
                if j == HC - 1:
                    mm.then_inc(o_ready, 1)

            pe.wait_ge(c_loaded, 16 * len(consts))
            pe.wait_ge(w_lod, len(pieces))

            def first():
                for c in range(FC):
                    turn(0, c)
                hidden(0, 0, 0)

            def chunk(i, b, last):
                n = 2 * i + b
                for j in range(HC):
                    if j + 1 < HC:
                        hidden(n, b, j + 1)
                    elif not last:
                        hidden(n + 1, 1 - b, 0)
                    out(n, j)
                    if j in TURN and not last:
                        turn(n + 1, TURN[j])

            all_chunks(pe, first, chunk)

        @block.scalar
        def _(act):
            act.wait_ge(c_loaded, 16 * len(consts))
            nc.scalar.activation(gate_t[:], gate_t[:], ACT.Tanh).then_inc(gate_done, 1)
            for n in range(len(pieces)):
                act.wait_ge(w_loaded[n % 2], 16 * (n // 2 + 1))
                nc.scalar.copy(pieces[n][1], raw(n)).then_inc(w_hid, 1)

            def turned(n, b, c):
                act.wait_ge(t_ready, FC * n + c + 1)
                nc.scalar.copy(xt_hi[:, b, c], tb[c % 2][:]).then_inc(xt_hid, 1)

            def first():
                for c in range(FC):
                    turned(0, 0, c)

            def chunk(i, b, last):
                n = 2 * i + b
                for j in range(HC):
                    act.wait_ge(h_ready, HC * n + j + 1)
                    act.wait_ge(h_lod, HC * n + j + 1)
                    nc.scalar.activation(h_f[:, j % 2], hb[j % 2][:], ACT.Gelu, bias=b1_sb[:, j:j + 1]).then_inc(gelu_done, 1)
                    act.wait_ge(gelu_done, HC * n + j + 3)
                    nc.scalar.copy(h_hi[:, j % 2], h_f[:, j % 2]).then_inc(h_hid, 1)
                    if j - 1 in TURN and not last:
                        turned(n + 1, 1 - b, TURN[j - 1])
                act.wait_ge(o_done, n + 2)
                act.dma_start(x_out[bass.ds(n * CH, CH), :].rearrange("(t p) d -> p t d", p=P), x_sb[:, b]).then_inc(x_stored[b], 16)

            all_chunks(act, first, chunk)
            for b in range(2):
                act.wait_ge(x_stored[b], 16 * (CHUNKS // 2) + 16)

        @block.vector
        def _(dve):
            V = nc.vector
            LINKS = 2 + ROOT_LINKS + 1

            def low(out, raw_in, hi):
                return V.tensor_tensor(out, raw_in, hi.bitcast(F32), ALU.subtract)

            V.memset(credit[:, 0:1], 0.0).then_inc(x_stored[0], 16)
            V.memset(credit[:, 1:2], 0.0).then_inc(x_stored[1], 16)
            V.memset(credit[:, 2:3], 0.0).then_inc(gelu_done, 2)
            V.memset(credit[:, 3:4], 0.0).then_inc(xt_lod, 2)
            V.memset(credit[:, 4:5], 0.0).then_inc(o_done, 1)
            V.memset(credit[:, 5:6], 0.0).then_inc(h_lod, 2)
            for n in range(len(pieces)):
                dve.wait_ge(w_hid, n + 1)
                low(pieces[n][2], raw(n), pieces[n][1]).then_inc(w_lod, 1)
            dve.wait_ge(c_loaded, 16 * len(consts))
            dve.wait_ge(gate_done, 1)
            V.tensor_scalar(b2_sb[:], b2_sb[:], gate_t[:, 0:1], None, ALU.mult).then_inc(bias_done, 1)
            dve.wait_ge(bias_done, 1)

            def normalize(i, b, part):
                n = 2 * i + b
                at = LINKS * n
                x = x_sb[:, b % 2]
                if part == 0:
                    dve.wait_ge(x_loaded[b % 2], 16 * (i + b // 2) + 16)
                    for t in range(TC):
                        l = V.bn_stats(stats[:, t], x[:, t])
                    l.then_inc(link_done, 1)
                elif part == 1:
                    dve.wait_ge(link_done, at + 1)
                    dve.nop(nofuse=True)
                    for t in range(TC):
                        l = V.bn_aggr(mv[:, t], stats[:, t])
                    l.then_inc(link_done, 1)
                    inverse_root(dve, V, link_done, at + 2, mv[:, :, 1], LN_EPS, root, rstd[:], 0)
                elif part == 2:
                    inverse_root(dve, V, link_done, at + 2, mv[:, :, 1], LN_EPS, root, rstd[:], 1)
                elif part == 3:
                    for t in range(TC):
                        l = V.tensor_scalar(xn[:, t], x[:, t], mv[:, t, 0:1], rstd[:, t:t + 1], ALU.subtract, ALU.mult)
                    l.then_inc(xn_done, 1)
                else:
                    for t in range(TC):
                        l = V.tensor_tensor(x[:, t], x[:, t], b2_sb[:], ALU.add)
                    l.then_inc(link_done, 1)

            def turned(n, b, c):
                dve.wait_ge(xt_hid, FC * n + c + 1)
                low(xt_lo[:, b, c], tb[c % 2][:], xt_hi[:, b, c]).then_inc(xt_lod, 1)

            def first():
                for part in NORM.values():
                    normalize(0, 0, part)
                for c in range(FC):
                    turned(0, 0, c)

            def chunk(i, b, last):
                n = 2 * i + b
                for j in range(HC):
                    dve.wait_ge(h_hid, HC * n + j + 1)
                    low(h_lo[:, j % 2], h_f[:, j % 2], h_hi[:, j % 2]).then_inc(h_lod, 1)
                    if not last:
                        if j in NORM:
                            normalize(i, b + 1, NORM[j])
                        if j - 1 in TURN:
                            turned(n + 1, 1 - b, TURN[j - 1])
                dve.wait_ge(o_ready, n + 1)
                dve.wait_ge(link_done, LINKS * n + LINKS)
                for t in range(TC):
                    o = V.scalar_tensor_tensor(x_sb[:, b, t], ob[t][:], gate_t[:, 0:1], x_sb[:, b, t], ALU.mult, ALU.add)
                o.then_inc(o_done, 1)

            all_chunks(dve, first, chunk)
    clear(nc, used)

def program(nc, a, out):
    def dram(name, shape, dt=F32):
        return nc.dram_tensor(name, shape, dt, kind="Internal").ap()

    def by_row(w):
        return w.rearrange("(c p) n -> p c n", p=P)

    x_half, x1, x3 = dram("x_half", [TOK, D]), dram("x1", [TOK, D]), dram("x3", [TOK, D])
    xn_rows, y_rows = dram("xn_rows", [TOK + P, D]), dram("y_rows", [TOPK * TOK + TILE, D])
    slot_tokens, tile_table = dram("slot_tokens", [SLOTS, 1], I32), dram("tile_table", [P, 2], I32)
    for half, (x_res, x_out) in enumerate(((a["x"], x_half), (x_half, x1))):
        gated_cross_attention(nc, half, a["x"], x_res, x_out, a["ctx_t"], a["mask"], a["g_xattn0"], by_row(a["wq0"]), by_row(a["wk0"]), by_row(a["wv0"]),
                              by_row(a["wo0"]), a["identity"], f"a{half}_")
    with ExitStack() as ctx:
        weights = ctx.enter_context(nc.sbuf_tensor("weights", [P, TOPK * TOK // P], F32))
        route(nc, x1, xn_rows, slot_tokens, tile_table, a["router_w"], a["router_scale"], a["expert_scale"], a["g_ffn0"], a["identity"], a["earlier"],
              a["iotas"], a["pairs"], a["empty_list"], weights, "r_")
        experts(nc, xn_rows, slot_tokens, tile_table, a["w_gate"], a["w_out"], y_rows, a["identity"], "e_")
        gated_normed_attention(nc, x1, y_rows, weights, x3, a["ctx_t"], a["g_xattn1"], by_row(a["wq1"]), by_row(a["wkv1"]), by_row(a["wkv_dca"]),
                               by_row(a["wo1"]), a["bq1"], a["bkv1"], a["ln_w"], a["ln_b"], a["bo1"], a["identity"], "d_")
    feed_forward(nc, x3, out, by_row(a["w1"]), a["b1"], by_row(a["w2"]), a["b2"], a["g_ffn1"], a["identity"], "f_")


def kernel(**inputs):
    import concourse.bacc as bacc
    from concourse.bass_utils import run_bass_kernel_spmd

    def all_rows(v):
        return np.broadcast_to(v, (P,) + np.shape(v))

    def columns(v, n):
        return np.reshape(v, (n, P)).T

    def k_then_v(v):
        hd = D // NHEAD1
        return np.reshape(v, v.shape[:-1] + (NHEAD1, 2, hd)).swapaxes(-3, -2).reshape(v.shape)

    i = {name: np.asarray(v) for name, v in inputs.items()}
    keys = np.r_[S - DCA:S, 0:S - DCA]
    bkv = np.array(all_rows(all_rows(k_then_v(np.concatenate([i["L1_xattn_bk"], i["L1_xattn_bv"]])))[0:2]))
    bkv[0:DCA, 0] = i["L1_xattn_bkv_dca"]
    ln = {}
    for n in "wb":
        ln[n] = np.stack([i[f"L1_xattn_{x}_{n}"] for x in ("qn", "qn", "kn", "kn")])
        ln[n] = np.array(all_rows(ln[n]))
        ln[n][0:DCA, 2] = i[f"L1_xattn_kn_dca_{n}"]
    iotas = np.zeros((P, 3 * E + 1), np.float32)
    iotas[:, 0:E], iotas[:, E:2 * E] = np.arange(E), np.arange(E) * TOK
    iotas[0:E, 2 * E:3 * E] = np.triu(np.ones((E, E)))
    iotas[:, 3 * E] = np.arange(P)
    arrays = {
        "x": i["x"].reshape(TOK, D), "ctx_t": i["ctx_1024"][:, keys].swapaxes(1, 2),
        "mask": np.ascontiguousarray(all_rows(i["mask_BxS2_bf1"][:, keys].reshape(-1))).view(np.uint8),
        "g_xattn0": all_rows(i["g_xattn"][0:1]), "g_xattn1": all_rows(i["g_xattn"][1:2]),
        "g_ffn0": all_rows(i["g_ffn"][0:1]), "g_ffn1": all_rows(i["g_ffn"][1:2]),
        "wq0": i["L0_xattn_Wq"], "wk0": i["L0_xattn_Wk"], "wv0": i["L0_xattn_Wv"], "wo0": i["L0_xattn_Wo"],
        "router_w": i["L0_ffn_router_logits"].reshape(D // P, P, E).swapaxes(0, 1), "router_scale": columns(i["L0_ffn_router_scale"], D // P),
        "expert_scale": all_rows(i["L0_ffn_per_expert_scale"]),
        "w_gate": i["L0_ffn_gating_einsum"].transpose(0, 3, 1, 2).reshape(E, D, 2 * H0), "w_out": i["L0_ffn_linear"],
        "wq1": i["L1_xattn_Wq"], "wkv1": k_then_v(np.concatenate([i["L1_xattn_Wk"], i["L1_xattn_Wv"]], axis=1)), "wkv_dca": i["L1_xattn_Wkv_dca"],
        "wo1": i["L1_xattn_Wo"], "bq1": all_rows(i["L1_xattn_bq"]), "bkv1": bkv, "ln_w": ln["w"], "ln_b": ln["b"], "bo1": all_rows(i["L1_xattn_bo"]),
        "w1": i["L1_ffn_proj1"].T, "b1": columns(i["L1_ffn_proj1_bias"], H1 // P), "w2": i["L1_ffn_proj2"].T, "b2": all_rows(i["L1_ffn_proj2_bias"]),
        "identity": np.eye(P, dtype=np.float32), "earlier": np.triu(np.ones((P, P), np.float32), 1), "iotas": iotas,
        "pairs": np.arange(TOPK * TOK, dtype=np.int32).reshape(TOK // P, P, TOPK).swapaxes(0, 1).reshape(P, -1),
        "empty_list": (TOPK * TOK + np.arange(SLOTS, dtype=np.int32) % TILE).reshape(P, -1),
    }
    arrays = {f"in_{name}": np.ascontiguousarray(v) for name, v in arrays.items()}
    nc = bacc.Bacc("TRN2", target_bir_lowering=False, num_devices=1)
    aps = {name[3:]: nc.dram_tensor(name, v.shape, mybir.dt.from_np(v.dtype), kind="ExternalInput").ap() for name, v in arrays.items()}
    out = nc.dram_tensor("out_x", [TOK, D], F32, kind="ExternalOutput").ap()
    program(nc, aps, out)
    r = run_bass_kernel_spmd(nc, [arrays], core_ids=[0])
    return r.results[0]["out_x"].reshape(B, S, D)
```

```python
from contextlib import ExitStack

import numpy as np

import concourse.bass as bass
from concourse import mybir

F32, F32R, U8, U32, I32 = mybir.dt.float32, mybir.dt.float32r, mybir.dt.uint8, mybir.dt.uint32, mybir.dt.int32
ALU = mybir.AluOpType
ACT = mybir.ActivationFunctionType
AX = mybir.AxisListType
P = 128
B, S, D, DC = 16, 256, 512, 256
TOK = B * S
NHEAD0, DH0 = 16, 128
LN_EPS = 1e-5
E, H0, TOPK = 8, 512, 2
ROUTER_EPS = 1e-6
NHEAD1, DCA = 16, 16
HEAD_EPS = 1e-6
H1 = 2048
TILE = 256
TILES = TOK * TOPK // TILE + E - 1
SLOTS = E * TOK + 2 * E * TILE
MASKED = -1.0e30
TINY = 1.0e-30
NEG_INF = -3.0e38

ROOT_MAGIC = 1597463007.0
ROOT_TURNS = 3
ROOT_LINKS = 3 + 3 * ROOT_TURNS


def root_link(eng, ops, chain, at, var, eps, tmp, y, n):
    v, w, t = (x[:] for x in tmp)
    eng.wait_ge(chain, at + min(n, 1) if n < 3 else at + n)
    if n == 0:
        op = ops.tensor_scalar(v, var, eps, None, ALU.add)
    elif n == 1:
        op = ops.tensor_scalar(w, v, -0.5, None, ALU.mult)
    elif n == 2:
        op = ops.tensor_scalar(y.bitcast(I32), v.bitcast(I32), -0.5, ROOT_MAGIC, ALU.mult, ALU.add)
    elif n % 3 == 0:
        op = ops.tensor_tensor(t, y, y, ALU.mult)
    elif n % 3 == 1:
        op = ops.tensor_tensor(t, t, w, ALU.mult)
    else:
        op = ops.scalar_tensor_tensor(y, t, 1.5, y, ALU.add, ALU.mult)
    op.then_inc(chain, 1)


def inverse_root(eng, ops, chain, at, var, eps, tmp, y, half=None):
    for n in {None: range(ROOT_LINKS), 0: range(6), 1: range(6, ROOT_LINKS)}[half]:
        root_link(eng, ops, chain, at, var, eps, tmp, y, n)
    if half != 0:
        eng.wait_ge(chain, at + ROOT_LINKS)


def clear(nc, semaphores):
    nc.clear_and_free_semaphores(semaphores)
    nc.all_engine_barrier()


def gated_cross_attention(nc, half, x_ln, x_res, x_out, ctx_t, mask, gate, wq, wk, wv, wo, identity, tag):
    HEADS = NHEAD0 // 2
    GROUPS = HEADS // 2
    C0 = half * HEADS * DH0
    G0 = half * GROUPS * DH0
    SCALE = 1.0 / float(np.sqrt(DH0))
    PAIR = 2 * HEADS
    SHARED = 6
    LINKS = 3 + ROOT_LINKS
    FC, CC = D // P, DC // P

    used = []
    with ExitStack() as ctx:
        def sb(name, shape, dt=F32):
            return ctx.enter_context(nc.sbuf_tensor(tag + name, shape, dt))

        def bank(name):
            return ctx.enter_context(nc.psum_tensor(tag + name, [P, 512], F32))

        def sem(name):
            used.append(nc.alloc_semaphore(tag + name))
            return used[-1]

        wq_hi, wq_lo = sb("wq_hi", [P, FC, HEADS * DH0], F32R), sb("wq_lo", [P, FC, HEADS * DH0], F32R)
        wk_hi, wk_lo = sb("wk_hi", [P, CC, GROUPS * DH0], F32R), sb("wk_lo", [P, CC, GROUPS * DH0], F32R)
        wv_hi, wv_lo = sb("wv_hi", [P, CC, GROUPS * DH0], F32R), sb("wv_lo", [P, CC, GROUPS * DH0], F32R)
        wo_hi, wo_lo = sb("wo_hi", [P, HEADS, D], F32R), sb("wo_lo", [P, HEADS, D], F32R)
        ident = sb("ident", [P, P])
        mask_u8 = sb("mask_u8", [P, B * S], U8)
        maskb = sb("maskb", [P, 2, S])
        gate_t = sb("gate_t", [P, 1])
        x_sb = sb("x_sb", [P, 2, 2, D])
        xr_sb = sb("xr_sb", [P, 2, 2, D])
        xo_sb = sb("xo_sb", [P, 2, 2, D])
        xn = sb("xn", [P, 2, D])
        stats = sb("stats", [P, 2, 6])
        mv = sb("mv", [P, 2, 2])
        credit = sb("credit", [P, 6])
        rstd = sb("rstd", [P, 2])
        root = [sb(f"root{n}", [P, 2]) for n in range(3)]
        ctx_raw = sb("ctx_raw", [P, 2, CC, S])
        ctx_hi, ctx_lo = sb("ctx_hi", [P, CC, S], F32R), sb("ctx_lo", [P, CC, S], F32R)
        xt_hi, xt_lo = sb("xt_hi", [P, 2, FC, S], F32R), sb("xt_lo", [P, 2, FC, S], F32R)
        k_hi, k_lo = sb("k_hi", [P, 2, GROUPS, S], F32R), sb("k_lo", [P, 2, GROUPS, S], F32R)
        v_hi, v_lo = sb("v_hi", [P, 2, 2, GROUPS * DH0], F32R), sb("v_lo", [P, 2, 2, GROUPS * DH0], F32R)
        q_hi, q_lo = sb("q_hi", [P, 2, S], F32R), sb("q_lo", [P, 2, S], F32R)
        prob = sb("prob", [P, 4, 2, S])
        mx = sb("mx", [P, 2, 2])
        nbias = sb("nbias", [P, 2, 2])
        rsum = sb("rsum", [P, 2, 2])
        rinv = sb("rinv", [P, 2, 2])
        rsafe = sb("rsafe", [P, 2, 2])
        pt_hi, pt_lo = sb("pt_hi", [P, 2, 2, S], F32R), sb("pt_lo", [P, 2, 2, S], F32R)
        ot_hi, ot_lo = sb("ot_hi", [P, 2, S], F32R), sb("ot_lo", [P, 2, S], F32R)

        pj = [bank("pj0"), bank("pj1")]
        sc = [bank("sc0"), bank("sc1")]
        ptb, avb = bank("ptb"), bank("avb")
        ob = [bank("ob0"), bank("ob1")]

        w_loaded = [sem(f"w_loaded{n}") for n in range(4)]
        w_hi, w_lo, w_lo_pool = sem("w_hi"), sem("w_lo"), sem("w_lo_pool")
        m_loaded, g_loaded, g_done, id_done = sem("m_loaded"), sem("g_loaded"), sem("g_done"), sem("id_done")
        x_loaded, xr_loaded = [sem("x_loaded0"), sem("x_loaded1")], [sem("xr_loaded0"), sem("xr_loaded1")]
        c_loaded = [sem("c_loaded0"), sem("c_loaded1")]
        chain = sem("chain")
        xn_done, c_hi, c_lo = sem("xn_done"), sem("c_hi"), sem("c_lo")
        pj_ready, pj_hi, pj_lo = sem("pj_ready"), sem("pj_hi"), sem("pj_lo")
        s_ready, s_max, s_bias, e_done, r_half, r_done, p_done = (
            sem("s_ready"), sem("s_max"), sem("s_bias"), sem("e_done"), sem("r_half"), sem("r_done"), sem("p_done"))
        t_ready, pt_hid, pt_lod = sem("t_ready"), sem("pt_hid"), sem("pt_lod")
        av_ready, ot_hid, ot_lod = sem("av_ready"), sem("ot_hid"), sem("ot_lod")
        o_ready, o_free, x_stored = sem("o_ready"), sem("o_free"), [sem("x_stored0"), sem("x_stored1")]

        pieces = [(wk[:, :, G0:G0 + GROUPS * DH0], wk_hi[:], wk_lo[:]), (wv[:, :, G0:G0 + GROUPS * DH0], wv_hi[:], wv_lo[:])]
        for c in range(0, FC, 2):
            pieces.append((wq[:, c:c + 2, C0:C0 + HEADS * DH0], wq_hi[:, c:c + 2], wq_lo[:, c:c + 2]))
        for h in range(0, HEADS, 4):
            pieces.append((wo[:, half * HEADS + h:half * HEADS + h + 4], wo_hi[:, h:h + 4], wo_lo[:, h:h + 4]))

        def raw(n):
            a, b = pieces[n][0].shape[1:]
            room, at = ((prob, 0), (prob, a * b), (xo_sb, 0), (xr_sb, 0), (xo_sb, 0), (xr_sb, 0))[n]
            return room[:].rearrange("p a b c -> p (a b c)")[:, at:at + a * b].rearrange("p (a b) -> p a b", a=a)

        SPLIT = {-7: 2, -6: 3, -2: 4, 0: 5}

        WHEN = {}

        def plan(n, *what):
            WHEN.setdefault(n, []).append(what)

        for n in range(3):
            plan(n - 9, "norm", n)
        plan(-8, "ctx", 0)
        for j in range(SHARED):
            plan(j - SHARED, "shared", j)
        FIRST, AHEAD = min(WHEN), 5

        def due(u, last, what):
            batches = range(2) if u < AHEAD or last else range(4)
            return [(bb, n) for bb in batches for w, n in WHEN.get(u - HEADS * bb, []) if w == what]

        def here(u, last):
            return 0 <= u < PAIR or (u >= PAIR and not last)

        def all_steps(eng, step):
            for u in range(FIRST, AHEAD):
                step(0, u, False)
            with eng.Fori(0, B // 2 - 1) as i:
                for u in range(AHEAD, PAIR + AHEAD):
                    step(i, u, False)
            for u in range(AHEAD, PAIR + AHEAD):
                step(B // 2 - 1, u, True)

        def place(i, bb, j):
            before = HEADS * bb + SHARED * bb
            if j >= SHARED:
                h = j - SHARED
                behind_last = isinstance(i, int) and 2 * i + bb == B - 1
                return before + h + (SHARED - 1 if h == 0 else SHARED if behind_last else SHARED + max(0, h + SHARED - HEADS - 1))
            units = j + 2 - SHARED
            return before + j + (max(0, units) if bb == 0 else units)

        def made(i, bb, j):
            return 2 * (HEADS + SHARED) * i + place(i, bb, j) + 1

        def item(bb, j):
            if j < 2:
                return xt_hi[:, bb % 2, 2 * j:2 * j + 2], xt_lo[:, bb % 2, 2 * j:2 * j + 2]
            if j < 4:
                g = 2 * (j - 2)
                return k_hi[:, bb % 2, g:g + 2], k_lo[:, bb % 2, g:g + 2]
            if j < 6:
                return v_hi[:, bb % 2, j - 4], v_lo[:, bb % 2, j - 4]
            return q_hi[:, j % 2], q_lo[:, j % 2]

        def item_psum(i, bb, j):
            b = pj[place(i, bb, j) % 2]
            if j < 4:
                return b[:].rearrange("p (a s) -> p a s", a=2)
            return b[:] if j < 6 else b[:, 0:S]

        block = ctx.enter_context(nc.Block())

        @block.sync
        def _(sp):
            sp.dma_start(gate_t[:], gate).then_inc(g_loaded, 16)
            def load(n):
                sp.dma_start(raw(n), pieces[n][0]).then_inc(w_loaded[n % 4], 16)

            def rows(b):
                return bass.ds(b * S, S)

            def load_x(b, bb):
                sp.dma_start(x_sb[:, bb], x_ln[rows(b), :].rearrange("(t p) d -> p t d", p=P)).then_inc(x_loaded[bb], 16)

            def load_ctx(b, bb):
                sp.dma_start(ctx_raw[:, bb], ctx_t[bass.ds(b, 1)].rearrange("o (c p) s -> p (o c) s", p=P)).then_inc(c_loaded[bb], 16)

            def load_residual(b, bb):
                sp.dma_start(xr_sb[:, bb], x_res[rows(b), :].rearrange("(t p) d -> p t d", p=P)).then_inc(xr_loaded[bb], 16)

            load_x(0, 0)
            for n in range(2):
                load(n)
            load_ctx(0, 0)
            sp.dma_start(mask_u8[:], mask).then_inc(m_loaded, 16)
            for n in range(2, 4):
                load(n)
            for n in range(4, 6):
                sp.wait_ge(w_lo, n - 1)
                load(n)
            load_x(1, 1)
            load_ctx(1, 1)
            sp.wait_ge(w_lo_pool, 2)
            for b in range(2):
                load_residual(b, b)
            with sp.Fori(1, B // 2) as i:
                for bb in range(2):
                    b = 2 * i + bb
                    sp.wait_ge(xn_done, b + 1)
                    sp.nop(nofuse=True)
                    load_x(b, bb)
                    sp.wait_ge(c_lo, b + 1)
                    sp.nop(nofuse=True)
                    load_ctx(b, bb)
                    sp.wait_ge(o_free, b + 1)
                    sp.nop(nofuse=True)
                    load_residual(b, bb)

        @block.tensor
        def _(pe):
            def three(out, a_hi, a_lo, b_hi, b_lo, start, stop):
                nc.tensor.matmul(out, a_hi, b_hi, start=start, stop=False)
                nc.tensor.matmul(out, a_hi, b_lo, start=False, stop=False)
                return nc.tensor.matmul(out, a_lo, b_hi, start=False, stop=stop)

            def shared(i, u, bb, j):
                if place(i, bb, j) >= 2:
                    pe.wait_ge(pj_lo, made(i, bb, j) - 2)
                out = item_psum(i, bb, j)
                if j < 2:
                    pe.wait_ge(xn_done, 2 * i + bb + 3)
                    for c in range(2):
                        for t in range(2):
                            mm = nc.tensor.transpose(out[:, c, t * P:(t + 1) * P], xn[:, t, (2 * j + c) * P:(2 * j + c + 1) * P], ident[:])
                elif j < 4:
                    if u < 0 and j == 2:
                        pe.wait_ge(w_lo, 2)
                    if j == 2:
                        pe.wait_ge(c_lo, 2 * i + bb + 3)
                    for a in range(2):
                        g = (2 * (j - 2) + a) * DH0
                        for c in range(CC):
                            mm = three(out[:, a], wk_hi[:, c, g:g + DH0], wk_lo[:, c, g:g + DH0],
                                       ctx_hi[:, c], ctx_lo[:, c], c == 0, c == CC - 1)
                else:
                    t = (j - 4) * P
                    for c in range(CC):
                        mm = three(out, ctx_hi[:, c, t:t + P], ctx_lo[:, c, t:t + P], wv_hi[:, c], wv_lo[:, c], c == 0, c == CC - 1)
                mm.then_inc(pj_ready, 1)

            def query(i, u):
                bb, h = divmod(u, HEADS)
                pe.wait_ge(pj_lo, made(i, bb, SHARED + h) - 2)
                if h == 0:
                    pe.wait_ge(pj_lo, made(i, bb, 1))
                for c in range(FC):
                    mm = three(item_psum(i, bb, SHARED + h), wq_hi[:, c, h * DH0:(h + 1) * DH0], wq_lo[:, c, h * DH0:(h + 1) * DH0],
                               xt_hi[:, bb % 2, c], xt_lo[:, bb % 2, c], c == 0, c == FC - 1)
                mm.then_inc(pj_ready, 1)

            def scores(i, u):
                bb, h = divmod(u, HEADS)
                pe.wait_ge(pj_lo, made(i, bb, SHARED + h))
                pe.wait_ge(s_max, PAIR * i + u + 1)
                out = sc[u % 2][:].rearrange("p (t s) -> p t s", t=2)
                for t in range(2):
                    mm = three(out[:, t], q_hi[:, h % 2, t * P:(t + 1) * P], q_lo[:, h % 2, t * P:(t + 1) * P],
                               k_hi[:, bb % 2, h // 2], k_lo[:, bb % 2, h // 2], True, True)
                mm.then_inc(s_ready, 1)

            def turn(i, u):
                pe.wait_ge(p_done, PAIR * i + u + 1)
                pe.wait_ge(pt_lod, PAIR * i + u + 1)
                out = ptb[:].rearrange("p (k s) -> p k s", k=2)
                for k in range(2):
                    for t in range(2):
                        mm = nc.tensor.transpose(out[:, k, t * P:(t + 1) * P], prob[:, u % 4, t, k * P:(k + 1) * P], ident[:])
                mm.then_inc(t_ready, 1)

            def values(i, u):
                bb, h = divmod(u, HEADS)
                g = (h // 2) * DH0
                pe.wait_ge(pt_lod, PAIR * i + u + 2)
                if h == 0:
                    pe.wait_ge(pj_lo, made(i, bb, 5))
                pe.wait_ge(ot_lod, PAIR * i + u + 1)
                for k in range(2):
                    mm = three(avb[:, 0:S], v_hi[:, bb % 2, k, g:g + DH0], v_lo[:, bb % 2, k, g:g + DH0],
                               pt_hi[:, u % 2, k], pt_lo[:, u % 2, k], k == 0, k == 1)
                mm.then_inc(av_ready, 1)

            def project(i, u):
                bb, h = divmod(u, HEADS)
                pe.wait_ge(ot_lod, PAIR * i + u + 2)
                if h == 0:
                    pe.wait_ge(o_free, 2 * i + bb + 2)
                for t in range(2):
                    mm = three(ob[t][:], ot_hi[:, u % 2, t * P:(t + 1) * P], ot_lo[:, u % 2, t * P:(t + 1) * P],
                               wo_hi[:, h], wo_lo[:, h], h == 0, h == HEADS - 1)
                if h == HEADS - 1:
                    mm.then_inc(o_ready, 1)

            pe.wait_ge(id_done, 16)

            def step(i, u, last):
                if u == 4:
                    pe.wait_ge(w_lo_pool, 2)
                if here(u + 1, last):
                    if u < 0:
                        pe.wait_ge(w_lo, 4)
                    query(i, u + 1)
                if here(u, last):
                    scores(i, u)
                if here(u - 4, last):
                    values(i, u - 4)
                if here(u - 5, last):
                    project(i, u - 5)
                for bb, j in due(u, last, "shared"):
                    shared(i, u, bb, j)
                if here(u - 2, last):
                    turn(i, u - 2)

            all_steps(pe, step)

        @block.scalar
        def _(act):
            act.wait_ge(g_loaded, 16)
            nc.scalar.activation(gate_t[:], gate_t[:], ACT.Tanh).then_inc(g_done, 1)

            def split(n):
                act.wait_ge(w_loaded[n % 4], 16 * (n // 4 + 1))
                nc.scalar.copy(pieces[n][1], raw(n)).then_inc(w_hi, 1)

            for n in range(2):
                split(n)

            def high(i, bb, j):
                act.wait_ge(pj_ready, made(i, bb, j))
                nc.scalar.copy(item(bb, j)[0], item_psum(i, bb, j)).then_inc(pj_hi, 1)

            def step(i, u, last):
                if here(u - 3, last):
                    act.wait_ge(t_ready, PAIR * i + u - 2)
                    nc.scalar.copy(pt_hi[:, (u - 3) % 2], ptb[:].rearrange("p (k s) -> p k s", k=2)).then_inc(pt_hid, 1)
                if here(u + 1, last):
                    high(i, (u + 1) // HEADS, SHARED + (u + 1) % HEADS)
                if here(u, last):
                    act.wait_ge(s_bias, PAIR * i + u + 1)
                    for t in range(2):
                        e = nc.scalar.activation(prob[:, u % 4, t], prob[:, u % 4, t], ACT.Exp, bias=nbias[:, u % 2, t:t + 1],
                                                 scale=SCALE, accum_out=rsum[:, u % 2, t:t + 1])
                    e.then_inc(e_done, 1)
                if here(u - 4, last):
                    act.wait_ge(av_ready, PAIR * i + u - 3)
                    nc.scalar.copy(ot_hi[:, (u - 4) % 2], avb[:, 0:S]).then_inc(ot_hid, 1)
                for bb, j in due(u, last, "shared"):
                    high(i, bb, j)
                for bb, _ in due(u, last, "ctx"):
                    act.wait_ge(c_loaded[bb % 2], 16 * (i + bb // 2) + 16)
                    if bb > 0:
                        act.wait_ge(pj_lo, made(i, bb - 1, SHARED - 1))
                    nc.scalar.copy(ctx_hi[:], ctx_raw[:, bb % 2]).then_inc(c_hi, 1)
                if u in SPLIT:
                    split(SPLIT[u])
                if here(u - 5, last) and (u - 5) % HEADS == HEADS - 1:
                    bb = (u - 5) // HEADS
                    act.wait_ge(o_free, 2 * i + bb + 3)
                    act.dma_start(x_out[bass.ds((2 * i + bb) * S, S), :].rearrange("(t p) d -> p t d", p=P),
                                  xo_sb[:, bb]).then_inc(x_stored[bb], 16)

            all_steps(act, step)
            for bb in range(2):
                act.wait_ge(x_stored[bb], 16 * (B // 2) + 16)

        @block.gpsimd
        def _(pool):
            pool.dma_start(ident[:], identity).then_inc(id_done, 16)
            for n in range(4, 6):
                pool.wait_ge(w_hi, n + 1)
                nc.gpsimd.tensor_tensor(pieces[n][2], raw(n), pieces[n][1].bitcast(F32), ALU.subtract).then_inc(w_lo_pool, 1)

            def step(i, u, last):
                if here(u, last):
                    pool.wait_ge(r_done, PAIR * i + u + 1)
                    pool.nop(nofuse=True)
                    for t in range(2):
                        p = nc.gpsimd.tensor_scalar(prob[:, u % 4, t], prob[:, u % 4, t], rinv[:, u % 2, t:t + 1], None, ALU.mult)
                    p.then_inc(p_done, 1)

            all_steps(pool, step)

        @block.vector
        def _(dve):
            def low(out, raw_in, hi):
                return nc.vector.tensor_tensor(out, raw_in, hi.bitcast(F32), ALU.subtract)

            for n, (what, count) in enumerate([(o_free, 2), (xn_done, 2), (c_lo, 2), (s_max, 2), (pt_lod, 1), (ot_lod, 1)]):
                nc.vector.memset(credit[:, n:n + 1], 0.0).then_inc(what, count)
            for bb in range(2):
                nc.vector.memset(rsum[:, bb], 1.0).then_inc(x_stored[bb], 16)

            def split(n):
                dve.wait_ge(w_hi, n + 1)
                low(pieces[n][2], raw(n), pieces[n][1]).then_inc(w_lo, 1)

            dve.wait_ge(g_done, 1)

            def low_item(i, bb, j):
                dve.wait_ge(pj_hi, made(i, bb, j))
                low(item(bb, j)[1], item_psum(i, bb, j), item(bb, j)[0]).then_inc(pj_lo, 1)

            def normalize(i, u, bb, n):
                at = LINKS * (2 * i + bb)
                if n == 0:
                    dve.wait_ge(x_loaded[bb % 2], 16 * (i + bb // 2) + 16)
                    for t in range(2):
                        l = nc.vector.bn_stats(stats[:, t], x_sb[:, bb % 2, t])
                    l.then_inc(chain, 1)
                    dve.wait_ge(chain, at + 1)
                    dve.nop(nofuse=True)
                    for t in range(2):
                        l = nc.vector.bn_aggr(mv[:, t], stats[:, t])
                    l.then_inc(chain, 1)
                    if u == FIRST:
                        dve.wait_ge(m_loaded, 16)
                    nc.vector.tensor_scalar(maskb[:, bb % 2], mask_u8[:, bass.ds((2 * i + bb) * S, S)], -1.0, -MASKED, ALU.add, ALU.mult).then_inc(chain, 1)
                else:
                    inverse_root(dve, nc.vector, chain, at + 3, mv[:, :, 1], LN_EPS, root, rstd[:], n - 1)
                if n == 2:
                    for t in range(2):
                        l = nc.vector.tensor_scalar(xn[:, t], x_sb[:, bb % 2, t], mv[:, t, 0:1], rstd[:, t:t + 1], ALU.subtract, ALU.mult)
                    l.then_inc(xn_done, 1)

            def step(i, u, last):
                if here(u - 3, last):
                    dve.wait_ge(pt_hid, PAIR * i + u - 2)
                    low(pt_lo[:, (u - 3) % 2], ptb[:].rearrange("p (k s) -> p k s", k=2), pt_hi[:, (u - 3) % 2]).then_inc(pt_lod, 1)
                if here(u + 1, last):
                    low_item(i, (u + 1) // HEADS, SHARED + (u + 1) % HEADS)
                if here(u, last):
                    dve.wait_ge(s_ready, PAIR * i + u + 1)
                    dve.nop(nofuse=True)
                    out = sc[u % 2][:].rearrange("p (t s) -> p t s", t=2)
                    for t in range(2):
                        m = nc.vector.tensor_tensor_reduce(prob[:, u % 4, t], out[:, t], maskb[:, u // HEADS % 2], 1.0, NEG_INF, ALU.add, ALU.max,
                                                           mx[:, u % 2, t:t + 1])
                    m.then_inc(s_max, 1)
                    dve.wait_ge(s_max, PAIR * i + u + 3)
                    nc.vector.tensor_scalar(nbias[:, u % 2], mx[:, u % 2], MASKED / 2, -SCALE, ALU.max, ALU.mult).then_inc(s_bias, 1)
                if here(u - 1, last):
                    v = u - 1
                    dve.wait_ge(e_done, PAIR * i + v + 1)
                    nc.vector.tensor_scalar(rsafe[:, v % 2], rsum[:, v % 2], TINY, None, ALU.max).then_inc(r_half, 1)
                    dve.wait_ge(r_half, PAIR * i + v + 1)
                    nc.vector.reciprocal(rinv[:, v % 2], rsafe[:, v % 2]).then_inc(r_done, 1)
                if here(u - 4, last):
                    dve.wait_ge(ot_hid, PAIR * i + u - 3)
                    low(ot_lo[:, (u - 4) % 2], avb[:, 0:S], ot_hi[:, (u - 4) % 2]).then_inc(ot_lod, 1)
                if here(u - 5, last) and (u - 5) % HEADS == HEADS - 1:
                    bb = (u - 5) // HEADS
                    dve.wait_ge(o_ready, 2 * i + bb + 1)
                    dve.wait_ge(xr_loaded[bb], 16 * i + 16)
                    dve.wait_ge(x_stored[bb], 16 * i + 16)
                    for t in range(2):
                        o = nc.vector.scalar_tensor_tensor(xo_sb[:, bb, t], ob[t][:], gate_t[:, 0:1], xr_sb[:, bb, t], ALU.mult, ALU.add)
                    o.then_inc(o_free, 1)
                for bb, j in due(u, last, "shared"):
                    low_item(i, bb, j)
                for bb, n in due(u, last, "norm"):
                    normalize(i, u, bb, n)
                for bb, _ in due(u, last, "ctx"):
                    dve.wait_ge(c_hi, 2 * i + bb + 1)
                    low(ctx_lo[:], ctx_raw[:, bb % 2], ctx_hi[:]).then_inc(c_lo, 1)
                if u == -8:
                    split(0)
                    split(1)
                if u in SPLIT and SPLIT[u] < 4:
                    split(SPLIT[u])
                if u == 4:
                    dve.wait_ge(w_lo_pool, 2)

            all_steps(dve, step)
    clear(nc, used)

def route(nc, x_in, xn_out, slot_tokens, tile_table, logits_w, router_scale, expert_scale, gate, identity, earlier, iotas, pairs, empty_list, weights, tag):
    QT = 8
    TURNS = TOK // (QT * P)
    LN_LINKS = 4 + 2 * ROOT_LINKS
    LINKS = 18
    FC = D // P
    used = []
    with ExitStack() as ctx:
        def sb(name, shape, dt=F32):
            return ctx.enter_context(nc.sbuf_tensor(tag + name, shape, dt))

        def bank(name):
            return ctx.enter_context(nc.psum_tensor(tag + name, [P, 512], F32))

        def sem(name):
            used.append(nc.alloc_semaphore(tag + name))
            return used[-1]

        ident, before, ones = sb("ident", [P, P]), sb("before", [P, P]), sb("ones", [P, P])
        iota = sb("iota", [P, 3 * E + 1])
        expert_no, list_start, upto, tile_no = iota[:, 0:E], iota[:, E:2 * E], iota[:, 2 * E:3 * E], iota[:, 3 * E:3 * E + 1]
        pair_no = sb("pair_no", [P, TOK * TOPK // P], I32)
        wr_raw, wr, rscale = sb("wr_raw", [P, FC, E]), sb("wr", [P, FC, E]), sb("rscale", [P, FC])
        escale, gate_t = sb("escale", [P, E]), sb("gate_t", [P, 1])
        empty, blank = sb("empty", [P, SLOTS // P], I32), sb("blank", [P, D])
        x_sb, xn = sb("x_sb", [P, 2, QT, D]), sb("xn", [P, 2, QT, D])
        stats, mv = sb("stats", [P, QT, 6]), sb("mv", [P, QT, 2])
        rstd, var2, r2 = sb("rstd", [P, QT]), sb("var2", [P, QT]), sb("r2", [P, 2, QT])
        root = [sb(f"root{n}", [P, QT]) for n in range(3)]
        xt = sb("xt", [P, 2, FC, P])
        logits, best, best_no = sb("logits", [P, QT, E]), sb("best", [P, QT, 8]), sb("best_no", [P, QT, 8], U32)
        no_f, gap, odds, share = sb("no_f", [P, QT, 2]), sb("gap", [P, QT]), sb("odds", [P, QT]), sb("share", [P, QT, 2])
        hot, picked, total, here = sb("hot", [P, QT, 2, E]), sb("picked", [P, QT, E]), sb("total", [P, E]), sb("here", [P, E])
        rank, scratch = sb("rank", [P, QT, E]), sb("scratch", [P, QT, 2, E])
        pos_f, scale_of = sb("pos_f", [P, QT, 2]), sb("scale_of", [P, QT, 2])
        pair, pos_here = sb("pair", [P, 2, QT, 2], I32), sb("pos_here", [P, 2, QT, 2], I32)
        count, count_i, tiles, tiles_rep = sb("count", [P, 1]), sb("count_i", [P, 1], I32), sb("tiles", [P, 1]), sb("tiles_rep", [P, P])
        credit = sb("credit", [P, 4])
        cum, below, start = sb("cum", [P, E]), sb("below", [P, E]), sb("start", [P, E])
        tab_f, tab_i = sb("tab_f", [P, 4]), sb("tab_i", [P, 2], I32)

        tb = [bank("tb0"), bank("tb1")]
        lb, rb, cb = [bank("lb0"), bank("lb1")], bank("rb"), bank("cb")

        c_loaded, blank_done, cleared, x_loaded = sem("c_loaded"), sem("blank_done"), sem("cleared"), [sem("x_loaded0"), sem("x_loaded1")]
        gate_done, wr_done = sem("gate_done"), sem("wr_done")
        ln_link, link_done, xn_done, xn_stored = sem("ln_link"), sem("link_done"), sem("xn_done"), [sem("xn_stored0"), sem("xn_stored1")]
        t_ready, t_done, l_ready = sem("t_ready"), sem("t_done"), sem("l_ready")
        gap_done, odds_done, picked_done, rank_ready, pos_done = sem("gap_done"), sem("odds_done"), sem("picked_done"), sem("rank_ready"), sem("pos_done")
        listed, list_free, count_ready, tiles_done, cum_ready, tab_link, tab_done, tab_stored = (
            sem("listed"), sem("list_free"), sem("count_ready"), sem("tiles_done"), sem("cum_ready"), sem("tab_link"), sem("tab_done"), sem("tab_stored"))

        block = ctx.enter_context(nc.Block())
        LISTED = 16 * 2 * QT

        def pair_rows(x):
            return x[:].rearrange("p t k e -> p (t k) e")

        def rows(i):
            return bass.ds(i * QT * P, QT * P)

        def all_turns(eng, turn):
            with eng.Fori(0, TURNS // 2 - 1) as i:
                for b in range(2):
                    turn(i, b, 2)
            for b in range(2):
                turn(TURNS // 2 - 1, b, 1 - b)

        @block.sync
        def _(sp):
            def load_rows(turn, b):
                sp.dma_start(x_sb[:, b], x_in[rows(turn), :].rearrange("(t p) d -> p t d", p=P)).then_inc(x_loaded[b], 16)

            load_rows(0, 0)
            for dst, src in ((ident[:], identity), (before[:], earlier), (iota[:], iotas), (wr_raw[:], logits_w), (rscale[:], router_scale),
                             (escale[:], expert_scale), (gate_t[:], gate), (pair_no[:], pairs), (empty[:], empty_list)):
                sp.dma_start(dst, src).then_inc(c_loaded, 16)
            load_rows(1, 1)
            sp.wait_ge(c_loaded, 16 * 9)
            sp.dma_start(slot_tokens.rearrange("(p s) o -> p (s o)", p=P), empty[:]).then_inc(cleared, 16)
            sp.wait_ge(blank_done, 1)
            sp.dma_start(xn_out[TOK:TOK + P, :], blank[:]).then_inc(cleared, 16)
            with sp.Fori(1, TURNS // 2) as i:
                for b in range(2):
                    sp.wait_ge(xn_done, 2 * i + b + 1)
                    sp.nop(nofuse=True)
                    load_rows(2 * i + b, b)
            sp.wait_ge(tab_done, 1)
            sp.dma_start(tile_table, tab_i[:]).then_inc(tab_stored, 16)
            sp.wait_ge(tab_stored, 16)

        @block.tensor
        def _(pe):
            def logits_of(turn, b, t):
                pe.wait_ge(t_done, QT * turn + t + 3)
                for c in range(FC):
                    mm = nc.tensor.matmul(lb[b][:, t * E:(t + 1) * E], xt[:, t % 2, c], wr[:, c], start=(c == 0), stop=(c == FC - 1))
                if t == QT - 1:
                    mm.then_inc(l_ready, 1)

            def logits_turn(turn, b, between=None):
                pe.wait_ge(xn_done, turn + 3)
                for t in range(QT):
                    pe.wait_ge(t_done, QT * turn + t + 1)
                    for c in range(FC):
                        mm = nc.tensor.transpose(tb[t % 2][:, c * P:(c + 1) * P], xn[:, b, t, c * P:(c + 1) * P], ident[:])
                    mm.then_inc(t_ready, 1)
                    if t >= 1:
                        logits_of(turn, b, t - 1)
                    if t == QT // 2 and between is not None:
                        places(between)
                logits_of(turn, b, QT - 1)

            def places(turn):
                pe.wait_ge(picked_done, turn + 1)
                nc.tensor.matmul(rb[:, 0:QT * E], before[:], picked[:].rearrange("p t e -> p (t e)"), start=True, stop=False)
                for t in range(QT - 1):
                    later = rb[:, (t + 1) * E:QT * E].rearrange("p (t e) -> p t e", e=E)
                    nc.tensor.matmul(later, ones[:], picked[:, t:t + 1].to_broadcast([P, QT - 1 - t, E]), start=False, stop=False)
                mm = nc.tensor.matmul(rb[:, 0:QT * E].rearrange("p (t e) -> p t e", e=E), ones[:], total[:].unsqueeze(1).to_broadcast([P, QT, E]),
                                      start=False, stop=True)
                mm.then_inc(rank_ready, 1)

            pe.wait_ge(c_loaded, 16 * 9)
            pe.wait_ge(wr_done, 1)
            logits_turn(0, 0)

            def step(i, b, behind):
                if behind:
                    logits_turn(2 * i + b + 1, 1 - b, 2 * i + b)
                else:
                    places(2 * i + b)

            all_turns(pe, step)
            pe.wait_ge(pos_done, TURNS + 1)
            nc.tensor.matmul(cb[0:E, 0:1], total[:], ones[:, 0:1], start=True, stop=True).then_inc(count_ready, 1)
            pe.wait_ge(tiles_done, 1)
            nc.tensor.matmul(cb[:, E:2 * E], tiles_rep[0:E, :], upto[0:E, :], start=True, stop=True).then_inc(cum_ready, 1)

        @block.scalar
        def _(act):
            act.wait_ge(c_loaded, 16 * 9)
            nc.scalar.activation(gate_t[:], gate_t[:], ACT.Tanh).then_inc(gate_done, 1)

            def rows_of(turn, b, between=None):
                act.wait_ge(xn_done, turn + 3)
                act.dma_start(xn_out[rows(turn), :].rearrange("(t p) d -> p t d", p=P), xn[:, b]).then_inc(xn_stored[b], 16)
                for t in range(QT):
                    act.wait_ge(t_ready, QT * turn + t + 1)
                    nc.scalar.copy(xt[:, t % 2], tb[t % 2][:].rearrange("p (c s) -> p c s", c=FC)).then_inc(t_done, 1)
                    if t == 1 and between is not None:
                        odds_of(between)

            def odds_of(turn):
                act.wait_ge(gap_done, turn + 1)
                nc.scalar.activation(odds[:], gap[:], ACT.Exp).then_inc(odds_done, 1)

            def step(i, b, behind):
                if behind:
                    rows_of(2 * i + b + 1, 1 - b, 2 * i + b)
                else:
                    odds_of(2 * i + b)

            rows_of(0, 0)
            all_turns(act, step)
            for b in range(2):
                act.wait_ge(xn_stored[b], 16 * (TURNS // 2) + 16)

        @block.gpsimd
        def _(pool):
            nc.gpsimd.memset(blank[:], 0.0).then_inc(blank_done, 1)
            pool.wait_ge(cleared, 32)
            with pool.Fori(0, TURNS // 2) as i:
                for b in range(2):
                    turn = 2 * i + b
                    for t in range(QT):
                        for k in range(2):
                            if (t, k) == (0, 0):
                                pool.wait_ge(pos_done, turn + 2)
                                pool.nop(nofuse=True)
                            pool.indirect_dma_start(out=slot_tokens, out_offset=bass.IndirectOffsetOnAxis(ap=pos_here[:, b, t, k:k + 1], axis=0),
                                                    in_=pair[:, b, t, k:k + 1], in_offset=None).then_inc(listed, 16)
                    pool.wait_ge(listed, LISTED * (turn + 1))
                    pool.nop(nofuse=True).then_inc(list_free, 1)

        @block.vector
        def _(dve):
            V = nc.vector
            V.memset(total[:], 0.0).then_inc(xn_done, 2)
            V.memset(ones[:], 1.0).then_inc(t_done, 2)
            V.memset(credit[:, 0:1], 0.0).then_inc(xn_stored[0], 16)
            V.memset(credit[:, 1:2], 0.0).then_inc(xn_stored[1], 16)
            V.memset(credit[:, 2:3], 0.0).then_inc(pos_done, 1)
            V.memset(credit[:, 3:4], 0.0).then_inc(list_free, 2)
            dve.wait_ge(c_loaded, 16 * 9)
            for c in range(FC):
                w = V.tensor_scalar(wr[:, c], wr_raw[:, c], rscale[:, c:c + 1], float(D) ** -0.5, ALU.mult, ALU.mult)
            w.then_inc(wr_done, 1)
            dve.wait_ge(gate_done, 1)

            def normalize(i, b):
                turn = 2 * i + b
                done = [0]
                x, y = x_sb[:, b % 2], xn[:, b % 2]

                def link(op):
                    op.then_inc(ln_link, 1)
                    done[0] += 1
                    dve.wait_ge(ln_link, LN_LINKS * turn + done[0])
                    dve.nop(nofuse=True)

                dve.wait_ge(x_loaded[b % 2], 16 * (i + b // 2) + 16)
                for t in range(QT):
                    op = V.bn_stats(stats[:, t], x[:, t])
                link(op)
                for t in range(QT):
                    op = V.bn_aggr(mv[:, t], stats[:, t])
                link(op)
                inverse_root(dve, V, ln_link, LN_LINKS * turn + done[0], mv[:, :, 1], LN_EPS, root, rstd[:])
                done[0] += ROOT_LINKS
                dve.wait_ge(xn_stored[b % 2], 16 * (i + b // 2) + 16)
                for t in range(QT):
                    op = V.tensor_scalar(y[:, t], x[:, t], mv[:, t, 0:1], rstd[:, t:t + 1], ALU.subtract, ALU.mult)
                op.then_inc(xn_done, 1)
                link(V.tensor_tensor(var2[:], mv[:, :, 1], rstd[:], ALU.mult))
                link(V.tensor_tensor(var2[:], var2[:], rstd[:], ALU.mult))
                inverse_root(dve, V, ln_link, LN_LINKS * turn + done[0], var2[:], ROUTER_EPS, root, r2[:, b % 2])

            def step(i, b, behind):
                turn = 2 * i + b
                done = [0]

                def link(op):
                    op.then_inc(link_done, 1)
                    done[0] += 1
                    dve.wait_ge(link_done, LINKS * turn + done[0])
                    dve.nop(nofuse=True)

                dve.wait_ge(l_ready, turn + 1)
                for t in range(QT):
                    op = V.tensor_scalar(logits[:, t], lb[b][:, t * E:(t + 1) * E], r2[:, b, t:t + 1], None, ALU.mult)
                link(op)
                for t in range(QT):
                    op = V.max(best[:, t], logits[:, t])
                link(op)
                V.tensor_tensor(gap[:], best[:, :, 1], best[:, :, 0], ALU.subtract).then_inc(gap_done, 1)
                for t in range(QT):
                    op = V.max_index(best_no[:, t], best[:, t], logits[:, t])
                link(op)
                link(V.tensor_copy(no_f[:], best_no[:, :, 0:2]))
                link(V.tensor_tensor(pair_rows(hot), expert_no.unsqueeze(1).to_broadcast([P, 2 * QT, E]),
                                     no_f[:].rearrange("p t k -> p (t k)").unsqueeze(2).to_broadcast([P, 2 * QT, E]), ALU.is_equal))
                V.tensor_tensor(picked[:], hot[:, :, 0], hot[:, :, 1], ALU.add).then_inc(picked_done, 1)
                dve.wait_ge(odds_done, turn + 1)
                link(V.tensor_scalar(gap[:], odds[:], 1.0, None, ALU.add))
                link(V.reciprocal(share[:, :, 0], gap[:]))
                link(V.tensor_tensor(share[:, :, 1], share[:, :, 0], odds[:], ALU.mult))
                link(V.tensor_tensor(pair_rows(scratch), pair_rows(hot), escale[:].unsqueeze(1).to_broadcast([P, 2 * QT, E]), ALU.mult))
                link(V.tensor_reduce(scale_of[:], scratch[:], AX.X, ALU.add))
                link(V.tensor_tensor(share[:], share[:], scale_of[:], ALU.mult))
                op = V.tensor_scalar(weights[:, bass.ds(turn * 2 * QT, 2 * QT)], share[:].rearrange("p t k -> p (t k)"), gate_t[:, 0:1], None, ALU.mult)
                link(op)
                if behind > 1:
                    normalize(i, b + 2)
                dve.wait_ge(rank_ready, turn + 1)
                link(V.tensor_tensor(rank[:], rb[:, 0:QT * E].rearrange("p (t e) -> p t e", e=E), list_start.unsqueeze(1).to_broadcast([P, QT, E]), ALU.add))
                link(V.tensor_tensor(scratch[:], hot[:], rank[:].unsqueeze(2).to_broadcast([P, QT, 2, E]), ALU.mult))
                link(V.tensor_reduce(pos_f[:], scratch[:], AX.X, ALU.add))
                link(V.tensor_reduce(here[:], picked[:].rearrange("p t e -> p e t"), AX.X, ALU.add))
                link(V.tensor_tensor(total[:], total[:], here[:], ALU.add))
                dve.wait_ge(list_free, turn + 1)
                link(V.tensor_copy(pos_here[:, b], pos_f[:]))
                V.tensor_copy(pair[:, b].rearrange("p t k -> p (t k)"), pair_no[:, bass.ds(turn * 2 * QT, 2 * QT)]).then_inc(pos_done, 1)
                assert done[0] == LINKS, done[0]

            normalize(0, 0)
            normalize(0, 1)
            all_turns(dve, step)
            dve.wait_ge(count_ready, 1)
            made = [0]

            def last(op):
                op.then_inc(tab_link, 1)
                made[0] += 1
                dve.wait_ge(tab_link, made[0])

            last(V.tensor_scalar(count[0:E, :], cb[0:E, 0:1], float(TILE - 1), None, ALU.add))
            last(V.tensor_copy(count_i[0:E, :], count[0:E, :]))
            last(V.tensor_scalar(count_i[0:E, :], count_i[0:E, :], TILE.bit_length() - 1, None, ALU.logical_shift_right))
            last(V.tensor_copy(tiles[0:E, :], count_i[0:E, :]))
            V.tensor_scalar(tiles_rep[0:E, :], ones[0:E, :], tiles[0:E, :], None, ALU.mult).then_inc(tiles_done, 1)
            dve.wait_ge(cum_ready, 1)
            last(V.tensor_copy(cum[:], cb[:, E:2 * E]))
            last(V.tensor_scalar(below[:], cum[:], tile_no, None, ALU.is_le))
            last(V.tensor_tensor(start[:], cum[:], below[:], ALU.mult))
            last(V.tensor_reduce(tab_f[:, 0:1], below[:], AX.X, ALU.add))
            last(V.tensor_reduce(tab_f[:, 1:2], start[:], AX.X, ALU.max))
            last(V.tensor_tensor(tab_f[:, 2:3], tile_no, tab_f[:, 1:2], ALU.subtract))
            last(V.tensor_scalar(tab_f[:, 2:3], tab_f[:, 2:3], float(TILE), None, ALU.mult))
            last(V.tensor_scalar(tab_f[:, 3:4], tab_f[:, 0:1], float(TOK), tab_f[:, 2:3], ALU.mult, ALU.add))
            last(V.tensor_scalar(tab_f[:, 0:1], tab_f[:, 0:1], float(E - 1), None, ALU.min))
            last(V.tensor_copy(tab_i[:, 0:1], tab_f[:, 0:1]))
            V.tensor_copy(tab_i[:, 1:2], tab_f[:, 3:4]).then_inc(tab_done, 1)
    clear(nc, used)


def experts(nc, xn_rows, slot_tokens, tile_table, w_gate, w_out, y_rows, identity, tag):
    FC, HC, TT = D // P, H0 // P, TILE // P
    WCOL = 2 * H0 + D
    TURNS = TILES // 2
    LAST = 2 * TURNS
    used = []
    with ExitStack() as ctx:
        def sb(name, shape, dt=F32):
            return ctx.enter_context(nc.sbuf_tensor(tag + name, shape, dt))

        def bank(name):
            return ctx.enter_context(nc.psum_tensor(tag + name, [P, 512], F32))

        def sem(name):
            used.append(nc.alloc_semaphore(tag + name))
            return used[-1]

        ident = sb("ident", [P, P])
        table = sb("table", [1, 2 * P], I32)
        pairs, ids, rows = sb("pairs", [P, 2, TT], I32), sb("ids", [P, 2, TT], I32), sb("rows", [P, 2, TT], I32)
        xg = sb("xg", [P, 2, TT, D])
        xt_hi, xt_lo = sb("xt_hi", [P, 2, FC, TILE], F32R), sb("xt_lo", [P, 2, FC, TILE], F32R)
        w_raw = sb("w_raw", [P, 2, FC, WCOL])
        w_hi, w_lo = sb("w_hi", [P, 2, FC, WCOL], F32R), sb("w_lo", [P, 2, FC, WCOL], F32R)
        gelu = sb("gelu", [P, 2, TILE])
        act_f = sb("act_f", [P, HC, TILE])
        act_hi, act_lo = sb("act_hi", [P, 2, HC, TILE], F32R), sb("act_lo", [P, 2, HC, TILE], F32R)
        y_sb = sb("y_sb", [P, 2, TT, D])
        credit = sb("credit", [P, 9])
        zeros = sb("zeros", [P, TILE])

        tb = [bank("tb0"), bank("tb1")]
        gb = [bank(f"gb{h}") for h in range(HC)]
        ob = [bank(f"ob{t}") for t in range(TT)]

        id_loaded, tab_loaded = sem("id_loaded"), sem("tab_loaded")
        pairs_loaded, x_loaded, in_loaded, out_loaded = ([sem(f"{n}{b}") for b in range(2)] for n in ("pairs_loaded", "x_loaded", "in_loaded", "out_loaded"))
        t_ready, xt_hid, xt_lod = sem("t_ready"), sem("xt_hid"), sem("xt_lod")
        in_hid, in_lod, out_hid, out_lod = sem("in_hid"), sem("in_lod"), sem("out_hid"), sem("out_lod")
        g_ready, gelu_done, act_done, act_hid, act_lod = sem("g_ready"), sem("gelu_done"), sem("act_done"), sem("act_hid"), sem("act_lod")
        y_ready, y_done, y_stored, y_free = sem("y_ready"), sem("y_done"), sem("y_stored"), sem("y_free")
        ids_done, rows_done = sem("ids_done"), sem("rows_done")

        IN, OUT = slice(0, 2 * H0), slice(2 * H0, WCOL)

        block = ctx.enter_context(nc.Block())

        @block.sync
        def _(sp):
            sp.dma_start(ident[:], identity).then_inc(id_loaded, 16)
            sp.dma_start(table[:], tile_table.rearrange("t c -> (t c)").unsqueeze(0)).then_inc(tab_loaded, 16)
            sp.wait_ge(tab_loaded, 16)

            def fetch(n, b):
                e = sp.value_load(table[0:1, bass.ds(2 * n, 1)], min_val=0, max_val=E - 1)
                place = sp.value_load(table[0:1, bass.ds(2 * n + 1, 1)], min_val=0, max_val=SLOTS - TILE)
                sp.wait_ge(in_lod, FC * (n + 1))
                sp.nop(nofuse=True)
                sp.dma_start(w_raw[:, b, :, IN], w_gate[bass.ds(e, 1)].rearrange("o (c p) n -> p (o c) n", p=P)).then_inc(in_loaded[b], 16)
                fetch_pairs(n, b, place)
                sp.wait_ge(out_lod, FC * (n + 1))
                sp.nop(nofuse=True)
                sp.dma_start(w_raw[:, b, :, OUT], w_out[bass.ds(e, 1)].rearrange("o (c p) n -> p (o c) n", p=P)).then_inc(out_loaded[b], 16)

            def fetch_pairs(n, b, place):
                sp.wait_ge(rows_done, n + 1)
                sp.nop(nofuse=True)
                sp.dma_start(pairs[:, b], slot_tokens[bass.ds(place, TILE), :].rearrange("(p t) o -> p (t o)", p=P)).then_inc(pairs_loaded[b], 16)

            fetch(0, 0)
            fetch(1, 1)
            with sp.Fori(0, TURNS) as i:
                fetch(2 * i + 2, 0)
                fetch(2 * i + 3, 1)
            fetch_pairs(LAST + 2, 0, sp.value_load(table[0:1, bass.ds(2 * LAST + 5, 1)], min_val=0, max_val=SLOTS - TILE))
            sp.wait_ge(pairs_loaded[0], 16 * (TURNS + 2))
            sp.wait_ge(pairs_loaded[1], 16 * (TURNS + 1))
            for b in range(2):
                sp.wait_ge(in_loaded[b], 16 * (TURNS + 1))
                sp.wait_ge(out_loaded[b], 16 * (TURNS + 1))

        @block.gpsimd
        def _(pool):
            def gather(n, b):
                pool.wait_ge(ids_done, n + 1)
                pool.nop(nofuse=True)
                pool.wait_ge(t_ready, 2 * (n + 1))
                pool.nop(nofuse=True)
                for t in range(TT):
                    pool.indirect_dma_start(out=xg[:, b, t], out_offset=None, in_=xn_rows,
                                            in_offset=bass.IndirectOffsetOnAxis(ap=ids[:, b, t:t + 1], axis=0)).then_inc(x_loaded[b], 16)

            def scatter(n, b):
                pool.wait_ge(rows_done, n + 3)
                pool.nop(nofuse=True)
                pool.wait_ge(y_done, n + 2)
                pool.nop(nofuse=True)
                for t in range(TT):
                    pool.indirect_dma_start(out=y_rows, out_offset=bass.IndirectOffsetOnAxis(ap=rows[:, b, t:t + 1], axis=0),
                                            in_=y_sb[:, b, t], in_offset=None).then_inc(y_stored, 16)
                pool.wait_ge(y_stored, 32 * (n + 1))
                pool.nop(nofuse=True).then_inc(y_free, 1)

            def split(n, b):
                for h in range(HC):
                    pool.wait_ge(act_done, HC * (n + 1) + h + 1)
                    if h == 0:
                        pool.wait_ge(y_ready, n + 1)
                    nc.gpsimd.tensor_tensor(act_hi[:, b, h], act_f[:, h], zeros[:], ALU.add).then_inc(act_hid, 1)
                    pool.wait_ge(act_hid, HC * n + h + 1)
                    nc.gpsimd.tensor_tensor(act_lo[:, b, h], act_f[:, h], act_hi[:, b, h].bitcast(F32), ALU.subtract).then_inc(act_lod, 1)

            nc.gpsimd.memset(zeros[:], 0.0).then_inc(t_ready, 4)
            nc.gpsimd.memset(credit[:, 7:8], 0.0).then_inc(act_lod, HC)
            pool.wait_ge(t_ready, 4)
            gather(0, 0)
            gather(1, 1)
            split(0, 0)
            gather(2, 0)
            with pool.Fori(0, TURNS) as i:
                for b in range(2):
                    n = 2 * i + b
                    split(n + 1, 1 - b)
                    gather(n + 3, 1 - b)
                    scatter(n, b)
            scatter(LAST, 0)
            pool.wait_ge(x_loaded[0], 32 * (TURNS + 2))
            pool.wait_ge(x_loaded[1], 32 * (TURNS + 1))

        @block.tensor
        def _(pe):
            def three(out, a_hi, a_lo, b_hi, b_lo, start, stop):
                nc.tensor.matmul(out, a_hi, b_hi, start=start, stop=False)
                nc.tensor.matmul(out, a_hi, b_lo, start=False, stop=False)
                return nc.tensor.matmul(out, a_lo, b_hi, start=False, stop=stop)

            def turn(n, b, count):
                pe.wait_ge(x_loaded[b], 32 * count)
                for j in range(2):
                    pe.wait_ge(xt_lod, 2 * n + j + 1)
                    out = tb[j][:].rearrange("p (c s) -> p c s", c=2)
                    for c in range(2):
                        for t in range(TT):
                            mm = nc.tensor.transpose(out[:, c, t * P:(t + 1) * P], xg[:, b, t, (2 * j + c) * P:(2 * j + c + 1) * P], ident[:])
                    mm.then_inc(t_ready, 1)

            def gate_up(n, b):
                pe.wait_ge(xt_lod, 2 * n + 4)
                pe.wait_ge(in_lod, FC * (n + 3))
                for h in range(HC):
                    pe.wait_ge(act_done, HC * n + h + 1)
                    for k in range(2):
                        out = gb[h][:, k * TILE:(k + 1) * TILE]
                        w = k * H0 + h * P
                        for c in range(FC):
                            mm = three(out, w_hi[:, b, c, w:w + P], w_lo[:, b, c, w:w + P], xt_hi[:, b, c], xt_lo[:, b, c], c == 0, c == FC - 1)
                    mm.then_inc(g_ready, 1)

            def down(n, b):
                pe.wait_ge(y_done, n + 1)
                pe.wait_ge(act_lod, HC * (n + 2))
                pe.wait_ge(out_lod, FC * (n + 3))
                for t in range(TT):
                    for h in range(HC):
                        mm = three(ob[t][:], act_hi[:, b, h, t * P:(t + 1) * P], act_lo[:, b, h, t * P:(t + 1) * P],
                                   w_hi[:, b, h, OUT], w_lo[:, b, h, OUT], h == 0, h == HC - 1)
                mm.then_inc(y_ready, 1)

            pe.wait_ge(id_loaded, 16)
            turn(0, 0, 1)
            gate_up(0, 0)
            turn(1, 1, 1)
            with pe.Fori(0, TURNS) as i:
                for b in range(2):
                    n = 2 * i + b
                    gate_up(n + 1, 1 - b)
                    turn(n + 2, b, i + 2)
                    down(n, b)
            down(LAST, 0)

        @block.scalar
        def _(act):
            def in_high(n, b, q, count):
                act.wait_ge(in_loaded[b], 16 * count)
                nc.scalar.copy(w_hi[:, b, q, IN], w_raw[:, b, q, IN]).then_inc(in_hid, 1)

            def out_high(n, b, q, count):
                act.wait_ge(out_loaded[b], 16 * count)
                nc.scalar.copy(w_hi[:, b, q, OUT], w_raw[:, b, q, OUT]).then_inc(out_hid, 1)

            def turned(n, b):
                for j in range(2):
                    act.wait_ge(t_ready, 2 * n + j + 5)
                    nc.scalar.copy(xt_hi[:, b, 2 * j:2 * j + 2], tb[j][:].rearrange("p (c s) -> p c s", c=2)).then_inc(xt_hid, 1)

            def tile(n, b, count):
                for h in range(HC):
                    act.wait_ge(g_ready, HC * n + h + 1)
                    act.wait_ge(act_done, HC * n + h + 3)
                    nc.scalar.activation(gelu[:, h % 2], gb[h][:, 0:TILE], ACT.Gelu_apprx_tanh).then_inc(gelu_done, 1)
                    in_high(n + 1, 1 - b, h, count + b)
                    out_high(n, b, h, count)
                turned(n + 1, 1 - b)

            def rows_of_y(n, b):
                act.wait_ge(y_ready, n + 3)
                act.wait_ge(y_free, n + 1)
                for t in range(TT):
                    y = nc.scalar.copy(y_sb[:, b, t], ob[t][:])
                y.then_inc(y_done, 1)

            for q in range(FC):
                in_high(0, 0, q, 1)
            turned(0, 0)
            tile(0, 0, 1)
            with act.Fori(0, TURNS) as i:
                for b in range(2):
                    n = 2 * i + b
                    tile(n + 1, 1 - b, i + 1 + b)
                    rows_of_y(n, b)
            rows_of_y(LAST, 0)

        @block.vector
        def _(dve):
            def low(out, raw, hi):
                return nc.vector.tensor_tensor(out, raw, hi.bitcast(F32), ALU.subtract)

            def in_low(n, b, q):
                dve.wait_ge(in_hid, FC * n + q + 1)
                low(w_lo[:, b, q, IN], w_raw[:, b, q, IN], w_hi[:, b, q, IN]).then_inc(in_lod, 1)

            def out_low(n, b, q):
                dve.wait_ge(out_hid, FC * n + q + 1)
                low(w_lo[:, b, q, OUT], w_raw[:, b, q, OUT], w_hi[:, b, q, OUT]).then_inc(out_lod, 1)

            def turned(n, b):
                for j in range(2):
                    dve.wait_ge(xt_hid, 2 * n + j + 1)
                    low(xt_lo[:, b, 2 * j:2 * j + 2], tb[j][:].rearrange("p (c s) -> p c s", c=2), xt_hi[:, b, 2 * j:2 * j + 2]).then_inc(xt_lod, 1)

            def tokens(n, b, count):
                dve.wait_ge(pairs_loaded[b], 16 * count)
                dve.wait_ge(t_ready, 2 * n + 2)
                nc.vector.tensor_scalar(ids[:, b], pairs[:, b], 1, None, ALU.arith_shift_right).then_inc(ids_done, 1)

            def tile(n, b, count):
                for h in range(HC):
                    dve.wait_ge(gelu_done, HC * n + h + 1)
                    dve.wait_ge(act_lod, HC * n + h + 1)
                    nc.vector.tensor_tensor(act_f[:, h], gb[h][:, TILE:], gelu[:, h % 2], ALU.mult).then_inc(act_done, 1)
                    in_low(n + 1, 1 - b, h)
                    out_low(n, b, h)
                    if h == 2:
                        dve.wait_ge(y_free, n + 1)
                        nc.vector.tensor_copy(rows[:, b], pairs[:, b]).then_inc(rows_done, 1)
                turned(n + 1, 1 - b)
                tokens(n + 2, b, count + 1)

            nc.vector.memset(credit[:, 0:1], 0.0).then_inc(in_lod, 2 * FC)
            nc.vector.memset(credit[:, 8:9], 0.0).then_inc(out_lod, 2 * FC)
            nc.vector.memset(credit[:, 1:2], 0.0).then_inc(act_done, HC)
            nc.vector.memset(credit[:, 2:3], 0.0).then_inc(xt_lod, 2)
            nc.vector.memset(credit[:, 3:4], 0.0).then_inc(y_done, 1)
            nc.vector.memset(credit[:, 4:5], 0.0).then_inc(y_ready, 2)
            nc.vector.memset(credit[:, 5:6], 0.0).then_inc(y_free, 2)
            nc.vector.memset(credit[:, 6:7], 0.0).then_inc(rows_done, 2)
            tokens(0, 0, 1)
            tokens(1, 1, 1)
            for q in range(FC):
                in_low(0, 0, q)
            turned(0, 0)
            tile(0, 0, 1)
            with dve.Fori(0, TURNS) as i:
                for b in range(2):
                    tile(2 * i + b + 1, 1 - b, i + 1 + b)
    clear(nc, used)


def gated_normed_attention(nc, x_in, y_rows, weights, x_out, ctx_t, gate, wq, wkv, wkv_dca, wo, bq, bkv, ln_w, ln_b, bo, identity, tag):
    FC, CC, HD = D // P, DC // P, D // NHEAD1
    SCALE = HD ** -0.5
    N1 = NHEAD1
    PAIR = 2 * N1
    HG = P // HD
    GROUPS = NHEAD1 // HG
    LINKS = 5 + ROOT_LINKS
    HEAD_LINKS = 3 + ROOT_LINKS
    ST = 3 * HD
    used = []
    with ExitStack() as ctx:
        def sb(name, shape, dt=F32):
            return ctx.enter_context(nc.sbuf_tensor(tag + name, shape, dt))

        def bank(name):
            return ctx.enter_context(nc.psum_tensor(tag + name, [P, 512], F32))

        def sem(name):
            used.append(nc.alloc_semaphore(tag + name))
            return used[-1]

        wq_hi, wq_lo = sb("wq_hi", [P, FC, D], F32R), sb("wq_lo", [P, FC, D], F32R)
        wkv_hi, wkv_lo = sb("wkv_hi", [P, CC, 2 * D], F32R), sb("wkv_lo", [P, CC, 2 * D], F32R)
        wd_hi, wd_lo = sb("wd_hi", [P, CC, 2 * D], F32R), sb("wd_lo", [P, CC, 2 * D], F32R)
        wo_hi, wo_lo = sb("wo_hi", [P, FC, D], F32R), sb("wo_lo", [P, FC, D], F32R)
        ident = sb("ident", [P, P])
        bq_sb, bkv_sb, bo_sb = sb("bq_sb", [P, D]), sb("bkv_sb", [P, 2, 2 * D]), sb("bo_sb", [P, D])
        lnw_sb, lnb_sb = sb("lnw_sb", [P, 4, HD]), sb("lnb_sb", [P, 4, HD])
        gate_t = sb("gate_t", [P, 1])
        x2 = sb("x2", [P, 2, 2, D])
        x_sb = sb("x_sb", [P, 2, 2, D])
        y_sb = sb("y_sb", [P, 2, D])
        w_here = sb("w_here", [P, 4])
        stats, mv, rstd = sb("stats", [P, 2, 6]), sb("mv", [P, 2, 2]), sb("rstd", [P, 2])
        root = [sb(f"root{n}", [P, 2]) for n in range(3)]
        xt_hi, xt_lo = sb("xt_hi", [P, FC, S], F32R), sb("xt_lo", [P, FC, S], F32R)
        ctx_raw = sb("ctx_raw", [P, CC, S])
        ctx_hi, ctx_lo = sb("ctx_hi", [P, CC, S], F32R), sb("ctx_lo", [P, CC, S], F32R)
        dca_hi, dca_lo = sb("dca_hi", [P, CC, P], F32R), sb("dca_lo", [P, CC, P], F32R)
        nrm = sb("nrm", [P, 2, 4, D])
        sq = sb("sq", [P, 2, D])
        xn = sq
        hsum, hvar, hrstd = sb("hsum", [P, 4 * NHEAD1]), sb("hvar", [P, 4 * NHEAD1]), sb("hrstd", [P, 4 * NHEAD1])
        hroot = [sb(f"hroot{n}", [P, 4 * NHEAD1]) for n in range(3)]
        col_mean = [x[:].rearrange("p (a h) -> p a h", a=4) for x in [hsum, hvar] + hroot]
        v_raw = sb("v_raw", [P, 2, D])
        v_hi, v_lo = sb("v_hi", [P, 2, NHEAD1, P], F32R), sb("v_lo", [P, 2, NHEAD1, P], F32R)
        stack = sb("stack", [P, 2, 4, HG, ST])
        qk = sb("qk", [ST, 2, 2 * S], F32R)
        prob = sb("prob", [P, 4, 2, S])
        mx, nbias = sb("mx", [P, 2, 2, 2]), sb("nbias", [P, 2, 2, 2])
        rsum, rinv = sb("rsum", [P, 4, 2, 2]), sb("rinv", [P, 4, 2, 2])
        pt_hi, pt_lo = sb("pt_hi", [P, 2, 2, S], F32R), sb("pt_lo", [P, 2, 2, S], F32R)
        ot_hi, ot_lo = sb("ot_hi", [P, 2, S], F32R), sb("ot_lo", [P, 2, S], F32R)
        credit = sb("credit", [P, 11])

        pjb, qkb = bank("pjb"), bank("qkb")
        sc = [bank("sc0"), bank("sc1")]
        ptb, avb = bank("ptb"), bank("avb")
        ob = [bank("ob0"), bank("ob1")]

        c_loaded, b_loaded, w_loaded, w_hid, w_lod = sem("c_loaded"), sem("b_loaded"), [sem(f"w_loaded{n}") for n in range(4)], sem("w_hid"), sem("w_lod")
        gate_done, zeroed, bias_done = sem("gate_done"), sem("zeroed"), sem("bias_done")
        x_loaded, x_used, ctx_loaded, y_loaded = sem("x_loaded"), sem("x_used"), sem("ctx_loaded"), sem("y_loaded")
        x_stored, w_meaned, w_centered = [sem("x_stored0"), sem("x_stored1")], sem("w_meaned"), sem("w_centered")
        y_used, link_done, xn_done, ctx_hid, ctx_lod = sem("y_used"), sem("link_done"), sem("xn_done"), sem("ctx_hid"), sem("ctx_lod")
        pj_ready, pj_hid, pj_taken = sem("pj_ready"), sem("pj_hid"), sem("pj_taken")
        sq_done, head_link, nrm_link = sem("sq_done"), sem("head_link"), sem("nrm_link")
        st_hid, st_done, v_hid, v_done = sem("st_hid"), sem("st_done"), sem("v_hid"), sem("v_done")
        qk_ready, qk_done = sem("qk_ready"), sem("qk_done")
        s_ready, s_max, s_bias, e_done, r_done, p_done = sem("s_ready"), sem("s_max"), sem("s_bias"), sem("e_done"), sem("r_done"), sem("p_done")
        t_ready, pt_hid, pt_lod = sem("t_ready"), sem("pt_hid"), sem("pt_lod")
        av_ready, ot_hid, ot_lod = sem("av_ready"), sem("ot_hid"), sem("ot_lod")
        o_ready, o_free = sem("o_ready"), sem("o_free")

        pieces = [(wq, wq_hi[:], wq_lo[:]), (wkv, wkv_hi[:], wkv_lo[:]), (wkv_dca, wd_hi[:], wd_lo[:]), (wo, wo_hi[:], wo_lo[:])]
        consts = [(ident[:], identity), (lnw_sb[:], ln_w), (lnb_sb[:], ln_b), (gate_t[:], gate)]
        biases = [(bq_sb[:], bq), (bkv_sb[:], bkv), (bo_sb[:], bo)]

        def raw(n):
            a, b = pieces[n][0].shape[1:]
            if n < 2:
                room = nrm[:, n].rearrange("p r d -> p (r d)")
            elif n == 2:
                room = stack[:].rearrange("p g r h s -> p (g r h s)")[:, 0:a * b]
            else:
                room = prob[:].rearrange("p u t s -> p (u t s)")
            return room.rearrange("p (a b) -> p a b", a=a)

        WHEN = {}

        def plan(n, *what):
            WHEN.setdefault(n, []).append(what)

        for k in range(TOPK):
            plan(2 * k - 27, "sum", k)
        for n in range(3):
            plan(n - 24, "norm", n)
        for j in range(2):
            plan(j - 21, "turn", j)
            plan(j - 20, "turned", j)
        plan(-11, "res", 0)
        for j, steps in {2: (-19, -18), 3: (-17, -15), 4: (-14, -13), 5: (-12,), 6: (-11, -10), 7: (-7,)}.items():
            for half, n in enumerate(steps):
                plan(n, "proj", (j, half))
            plan(steps[-1] + (2 if j == 6 else 1), "take", j)
        for half in range(2):
            plan(3 * half - 14, "square", half)
            plan(3 * half - 13, "sumsq", half)
        for n in range(2):
            plan(n - 9, "root", n)
        for g in range(GROUPS):
            for n in range(3):
                plan(HG * g - 7 + n, "piece", (g, n))
            plan(HG * g - 4, "stack", g)
        for h in range(HG):
            plan(h - 4, "v", (0, h))
            plan(h + 2, "v", (1, h))
        FIRST, AHEAD = min(WHEN), 5

        def due(u, last, what):
            batches = range(2) if u < AHEAD or last else range(4)
            return [(bb, n) for bb in batches for w, n in WHEN.get(u - N1 * bb, []) if w == what]

        def here(u, last):
            return 0 <= u < PAIR or (u >= PAIR and not last)

        def all_steps(eng, step):
            for u in range(FIRST, AHEAD):
                step(0, u, False)
            with eng.Fori(0, B // 2 - 1) as i:
                for u in range(AHEAD, PAIR + AHEAD):
                    step(i, u, False)
            for u in range(AHEAD, PAIR + AHEAD):
                step(B // 2 - 1, u, True)

        def diag(v, g2, h):
            return v[:, :, 2 * g2 * HG:2 * (g2 + 1) * HG].rearrange("p k (g h) c -> p k g h c", h=HG)[:, :, :, h, h * HD:(h + 1) * HD]

        def v_cols(g2, h):
            return v_raw[:, :, 2 * g2 * P:2 * (g2 + 1) * P].rearrange("p k (g c) -> p k g c", c=P)[:, :, :, h * HD:(h + 1) * HD]

        def group_cols(bb, g):
            return nrm[:, bb, :, g * P:(g + 1) * P].rearrange("p r (h c) -> p r h c", h=HG)

        def head_cols(w):
            return w.rearrange("p a (h c) -> p a h c", h=N1)

        block = ctx.enter_context(nc.Block())

        @block.sync
        def _(sp):
            def load_x(b, bb):
                sp.dma_start(x2[:, bb], x_in[bass.ds(b * S, S), :].rearrange("(t p) d -> p t d", p=P)).then_inc(x_loaded, 16)

            def load_y(b, k):
                sp.wait_ge(y_used, 2 * b + k + 1)
                sp.nop(nofuse=True)
                sp.dma_start(y_sb[:], y_rows[bass.ds(TOPK * S * b, TOPK * S), :].rearrange("(t p k) d -> p t k d", t=2, k=TOPK)[:, :, k]).then_inc(y_loaded, 16)

            def load_ctx(b):
                sp.wait_ge(ctx_lod, b + 1)
                sp.nop(nofuse=True)
                sp.dma_start(ctx_raw[:], ctx_t[bass.ds(b, 1)].rearrange("o (c p) s -> p (o c) s", p=P)).then_inc(ctx_loaded, 16)

            load_x(0, 0)
            load_y(0, 0)
            for dst, src in consts:
                sp.dma_start(dst, src).then_inc(c_loaded, 16)
            for n in range(3):
                sp.dma_start(raw(n), pieces[n][0]).then_inc(w_loaded[n], 16)
                if n == 0:
                    load_y(0, 1)
            load_ctx(0)
            for dst, src in biases:
                sp.dma_start(dst, src).then_inc(b_loaded, 16)
            load_x(1, 1)
            for k in range(TOPK):
                load_y(1, k)
            load_ctx(1)
            with sp.Fori(1, B // 2) as i:
                for bb in range(2):
                    b = 2 * i + bb
                    sp.wait_ge(x_used, b + 1)
                    sp.nop(nofuse=True)
                    load_x(b, bb)
                    for k in range(TOPK):
                        load_y(b, k)
                    load_ctx(b)

        @block.tensor
        def _(pe):
            def three(out, a_hi, a_lo, b_hi, b_lo, start, stop):
                nc.tensor.matmul(out, a_hi, b_hi, start=start, stop=False)
                nc.tensor.matmul(out, a_hi, b_lo, start=False, stop=False)
                return nc.tensor.matmul(out, a_lo, b_hi, start=False, stop=stop)

            def turn_x(b, j):
                pe.wait_ge(xn_done, b + 1)
                pe.wait_ge(pj_taken, 8 * b + j + 1)
                out = pjb[:].rearrange("p (c s) -> p c s", c=2)
                for c in range(2):
                    for t in range(2):
                        mm = nc.tensor.transpose(out[:, c, t * P:(t + 1) * P], xn[:, t, (2 * j + c) * P:(2 * j + c + 1) * P], ident[:])
                mm.then_inc(pj_ready, 1)

            def projection(b, j, half, is_first):
                t = (j % 2) * P
                if half == 0:
                    pe.wait_ge(pj_taken, 8 * b + j + 1)
                    if is_first and j == 2:
                        pe.wait_ge(w_lod, 1)
                    elif is_first and j == 4:
                        pe.wait_ge(w_lod, 3)
                if j < 4:
                    for c in range(half * FC // 2, (half + 1) * FC // 2):
                        mm = three(pjb[:], xt_hi[:, c, t:t + P], xt_lo[:, c, t:t + P], wq_hi[:, c], wq_lo[:, c], c == 0, c == FC - 1)
                else:
                    w = slice((j - 4) // 2 * D, ((j - 4) // 2 + 1) * D)
                    if half == 0:
                        if j == 4:
                            pe.wait_ge(ctx_lod, b + 2)
                        for c in range(CC):
                            mm = three(pjb[:], ctx_hi[:, c, t:t + P], ctx_lo[:, c, t:t + P], wkv_hi[:, c, w], wkv_lo[:, c, w],
                                       c == 0, c == CC - 1 and t > 0)
                    elif t == 0:
                        for c in range(CC):
                            mm = three(pjb[:], dca_hi[:, c], dca_lo[:, c], wd_hi[:, c, w], wd_lo[:, c, w], False, c == CC - 1)
                if (half == 1) == (j < 4 or t == 0):
                    mm.then_inc(pj_ready, 1)

            def turn_qk(i, u):
                bb, h = divmod(u, N1)
                pe.wait_ge(st_done, GROUPS * (2 * i + bb) + h // HG + 1)
                pe.wait_ge(qk_done, PAIR * i + u + 1)
                for r in range(4):
                    mm = nc.tensor.transpose(qkb[0:ST, r * P:(r + 1) * P], stack[:, (h // HG) % 2, r, h % HG], ident[:])
                mm.then_inc(qk_ready, 1)

            def scores(i, u):
                pe.wait_ge(qk_done, PAIR * i + u + 2)
                pe.wait_ge(e_done, PAIR * i + u + 1)
                for t in range(2):
                    mm = nc.tensor.matmul(sc[u % 2][:, t * S:(t + 1) * S], qk[:, u % 2, t * P:(t + 1) * P], qk[:, u % 2, S:], start=True, stop=True)
                mm.then_inc(s_ready, 1)

            def turn_p(i, u):
                pe.wait_ge(p_done, PAIR * i + u + 1)
                pe.wait_ge(pt_lod, PAIR * i + u + 1)
                out = ptb[:].rearrange("p (k s) -> p k s", k=2)
                for k in range(2):
                    for t in range(2):
                        mm = nc.tensor.transpose(out[:, k, t * P:(t + 1) * P], prob[:, u % 4, t, k * P:(k + 1) * P], ident[:])
                mm.then_inc(t_ready, 1)

            def values(i, u):
                bb, h = divmod(u, N1)
                pe.wait_ge(pt_lod, PAIR * i + u + 2)
                if h % HG == 0:
                    pe.wait_ge(v_done, 2 * HG * (2 * i + bb) + HG * (h // (2 * HG) + 1))
                    pe.wait_ge(ot_lod, GROUPS * (2 * i + bb) + h // HG + 1)
                for k in range(2):
                    mm = three(avb[:, 0:S], v_hi[:, k, h], v_lo[:, k, h], pt_hi[:, u % 2, k], pt_lo[:, u % 2, k],
                               h % HG == 0 and k == 0, h % HG == HG - 1 and k == 1)
                mm.then_inc(av_ready, 1)

            def project(i, bb, g):
                pe.wait_ge(ot_lod, GROUPS * (2 * i + bb) + g + 2)
                if g == 0:
                    pe.wait_ge(o_free, 2 * i + bb + 1)
                for t in range(2):
                    mm = three(ob[t][:], ot_hi[:, g % 2, t * P:(t + 1) * P], ot_lo[:, g % 2, t * P:(t + 1) * P], wo_hi[:, g], wo_lo[:, g],
                               g == 0, g == GROUPS - 1)
                if g == GROUPS - 1:
                    mm.then_inc(o_ready, 1)

            pe.wait_ge(c_loaded, 16 * len(consts))

            def step(i, u, last):
                if u == 0:
                    pe.wait_ge(w_lod, len(pieces))
                if here(u + 2, last):
                    turn_qk(i, u + 2)
                if here(u + 1, last):
                    scores(i, u + 1)
                if here(u - 4, last):
                    values(i, u - 4)
                if here(u - 5, last) and (u - 5) % HG == HG - 1:
                    project(i, (u - 5) // N1, (u - 5) % N1 // HG)
                for bb, j in due(u, last, "turn"):
                    turn_x(2 * i + bb, j)
                for bb, (j, half) in due(u, last, "proj"):
                    projection(2 * i + bb, j, half, u < 0)
                if here(u - 2, last):
                    turn_p(i, u - 2)

            all_steps(pe, step)

        @block.scalar
        def _(act):
            act.wait_ge(c_loaded, 16 * len(consts))
            nc.scalar.activation(gate_t[:], gate_t[:], ACT.Tanh).then_inc(gate_done, 1)

            def split(n):
                if n < 3:
                    act.wait_ge(w_centered, n + 1)
                else:
                    act.wait_ge(w_loaded[n], 16)
                nc.scalar.copy(pieces[n][1], raw(n)).then_inc(w_hid, 1)

            act.dma_start(raw(3), pieces[3][0]).then_inc(w_loaded[3], 16)
            split(0)
            act.wait_ge(zeroed, 6)

            def step(i, u, last):
                for bb, j in due(u, last, "turned"):
                    b = 2 * i + bb
                    if j == 0:
                        act.wait_ge(ctx_loaded, 16 * b + 16)
                        act.wait_ge(pj_taken, 8 * b + 1)
                        nc.scalar.copy(ctx_hi[:, :, DCA:], ctx_raw[:, :, DCA:])
                        nc.scalar.copy(dca_hi[:, :, 0:DCA], ctx_raw[:, :, 0:DCA]).then_inc(ctx_hid, 1)
                    act.wait_ge(pj_ready, 8 * b + j + 1)
                    nc.scalar.copy(xt_hi[:, 2 * j:2 * j + 2], pjb[:].rearrange("p (c s) -> p c s", c=2)).then_inc(pj_hid, 1)
                if here(u - 3, last):
                    act.wait_ge(t_ready, PAIR * i + u - 2)
                    nc.scalar.copy(pt_hi[:, (u - 3) % 2], ptb[:].rearrange("p (k s) -> p k s", k=2)).then_inc(pt_hid, 1)
                if here(u, last):
                    act.wait_ge(s_bias, PAIR * i + u + 1)
                    s = sc[u % 2][:].rearrange("p (t s) -> p t s", t=2)
                    for k, keys in ((0, slice(0, DCA)), (1, slice(DCA, S))):
                        for t in range(2):
                            e = nc.scalar.activation(prob[:, u % 4, t, keys], s[:, t, keys], ACT.Exp, bias=nbias[:, u % 2, k, t:t + 1],
                                                     scale=SCALE, accum_out=rsum[:, u % 4, k, t:t + 1])
                    e.then_inc(e_done, 1)
                if here(u + 2, last):
                    act.wait_ge(qk_ready, PAIR * i + u + 3)
                    nc.scalar.copy(qk[:, u % 2], qkb[0:ST, :]).then_inc(qk_done, 1)
                if here(u - 4, last) and (u - 4) % HG == HG - 1:
                    act.wait_ge(av_ready, PAIR * i + u - 2)
                    nc.scalar.copy(ot_hi[:, (u - 4) // HG % 2], avb[:, 0:S]).then_inc(ot_hid, 1)
                for bb, half in due(u, last, "square"):
                    act.wait_ge(pj_taken, 8 * (2 * i + bb) + 5 + 2 * half)
                    if half:
                        act.wait_ge(head_link, HEAD_LINKS * (2 * i + bb) + 1)
                    nc.scalar.activation(sq[:], nrm[:, bb % 2, 2 * half:2 * half + 2], ACT.Square).then_inc(sq_done, 1)
                for bb, (g2, h) in due(u, last, "v"):
                    b = 2 * i + bb
                    act.wait_ge(pj_taken, 8 * b + 9)
                    if u >= AHEAD or bb > 0:
                        act.wait_ge(av_ready, N1 * b - N1 + (2 * g2 + 1) * HG + h + 2)
                    nc.scalar.copy(diag(v_hi, g2, h), v_cols(g2, h)).then_inc(v_hid, 1)
                for bb, g in due(u, last, "stack"):
                    b = 2 * i + bb
                    act.wait_ge(nrm_link, 3 * GROUPS * b + 3 * g + 3)
                    if g >= 2 or u >= AHEAD:
                        act.wait_ge(qk_ready, N1 * b + (g - 1) * HG)
                    out = stack[:, g % 2]
                    nc.scalar.copy(out[:, :, :, 0:HD].bitcast(F32R), group_cols(bb % 2, g))
                    nc.scalar.copy(out[:, 0:2, :, HD:2 * HD].bitcast(F32R), group_cols(bb % 2, g)[:, 0:2])
                    nc.scalar.copy(out[:, 2:4, :, 2 * HD:].bitcast(F32R), group_cols(bb % 2, g)[:, 2:4]).then_inc(st_hid, 1)
                if here(u - 5, last) and (u - 5) % N1 == N1 - 1:
                    bb = (u - 5) // N1
                    act.wait_ge(o_free, 2 * i + bb + 2)
                    act.dma_start(x_out[bass.ds((2 * i + bb) * S, S), :].rearrange("(t p) d -> p t d", p=P), x_sb[:, bb]).then_inc(x_stored[bb], 16)
                if -20 <= u <= -18:
                    split(u + 21)

            all_steps(act, step)
            for bb in range(2):
                act.wait_ge(x_stored[bb], 16 * (B // 2) + 16)

        @block.gpsimd
        def _(pool):
            T = nc.gpsimd.tensor_tensor
            for zeros in (ctx_hi, ctx_lo, dca_hi, dca_lo, v_hi, v_lo):
                nc.gpsimd.memset(zeros[:].bitcast(F32), 0.0).then_inc(zeroed, 1)
            for n in range(len(pieces)):
                pool.wait_ge(w_hid, n + 1)
                T(pieces[n][2], raw(n), pieces[n][1].bitcast(F32), ALU.subtract).then_inc(w_lod, 1)
            pool.wait_ge(c_loaded, 16 * len(consts))
            pool.wait_ge(bias_done, 1)

            def step(i, u, last):
                if here(u - 1, last):
                    pool.wait_ge(r_done, PAIR * i + u)
                    p = prob[:, (u - 1) % 4]
                    T(p[:, :, 0:DCA], p[:, :, 0:DCA], rinv[:, (u - 1) % 4, 0].unsqueeze(2).to_broadcast([P, 2, DCA]), ALU.mult)
                    T(p[:, :, DCA:], p[:, :, DCA:], rinv[:, (u - 1) % 4, 1].unsqueeze(2).to_broadcast([P, 2, S - DCA]), ALU.mult).then_inc(p_done, 1)
                for bb, _ in due(u, last, "res"):
                    pool.wait_ge(xn_done, 2 * i + bb + 1)
                    pool.wait_ge(x_stored[bb % 2], 16 * (i + bb // 2) + 16)
                    for t in range(2):
                        l = T(x_sb[:, bb % 2, t], x2[:, bb % 2, t], bo_sb[:], ALU.add)
                    l.then_inc(x_used, 1)
                for bb, (g2, h) in due(u, last, "v"):
                    pool.wait_ge(v_hid, 2 * HG * (2 * i + bb) + HG * g2 + h + 1)
                    T(diag(v_lo, g2, h), v_cols(g2, h), diag(v_hi, g2, h).bitcast(F32), ALU.subtract).then_inc(v_done, 1)
                for bb, (g, n) in due(u, last, "piece"):
                    b = 2 * i + bb
                    x = group_cols(bb % 2, g)
                    if n == 0:
                        pool.wait_ge(head_link, HEAD_LINKS * (b + 1))
                        r = hrstd[:].rearrange("p (r h) -> p r h", r=4)[:, :, g * HG:(g + 1) * HG].unsqueeze(3).to_broadcast([P, 4, HG, HD])
                        T(x, x, r, ALU.mult).then_inc(nrm_link, 1)
                    else:
                        pool.wait_ge(nrm_link, 3 * GROUPS * b + 3 * g + n)
                        c, op = ((lnw_sb, ALU.mult), (lnb_sb, ALU.add))[n - 1]
                        T(x, x, c[:].unsqueeze(2).to_broadcast([P, 4, HG, HD]), op).then_inc(nrm_link, 1)

                for bb, g in due(u, last, "stack"):
                    out = stack[:, g % 2]
                    pool.wait_ge(st_hid, GROUPS * (2 * i + bb) + g + 1)
                    T(out[:, 0:2, :, 2 * HD:], group_cols(bb % 2, g)[:, 0:2], out[:, 0:2, :, 0:HD], ALU.subtract)
                    T(out[:, 2:4, :, HD:2 * HD], group_cols(bb % 2, g)[:, 2:4], out[:, 2:4, :, 0:HD], ALU.subtract).then_inc(st_done, 1)

            all_steps(pool, step)

        @block.vector
        def _(dve):
            V = nc.vector
            def low(out, raw_in, hi):
                return V.tensor_tensor(out, raw_in, hi.bitcast(F32), ALU.subtract)

            V.memset(credit[:, 0:1], 0.0).then_inc(x_stored[0], 16)
            V.memset(credit[:, 1:2], 0.0).then_inc(x_stored[1], 16)
            V.memset(credit[:, 2:3], 0.0).then_inc(ctx_lod, 1)
            V.memset(credit[:, 3:4], 0.0).then_inc(pj_taken, 1)
            V.memset(credit[:, 9:10], 0.0).then_inc(qk_done, 1)
            V.memset(credit[:, 10:11], 0.0).then_inc(ot_lod, 1)
            V.memset(credit[:, 4:5], 0.0).then_inc(o_free, 1)
            V.memset(credit[:, 5:6], 0.0).then_inc(x_used, 2)
            V.memset(credit[:, 6:7], 0.0).then_inc(e_done, 2)
            V.memset(credit[:, 7:8], 0.0).then_inc(pt_lod, 1)
            V.memset(credit[:, 8:9], 0.0).then_inc(av_ready, 1)
            V.memset(rstd[:], 0.0).then_inc(y_used, 1)

            def center(n, cols):
                m = col_mean[n][:, 0:cols.shape[1]]
                V.tensor_reduce(m, head_cols(cols), AX.X, ALU.add).then_inc(w_meaned, 1)
                dve.wait_ge(w_meaned, 2 * n + 1)
                V.tensor_scalar(m, m, -1.0 / HD, None, ALU.mult).then_inc(w_meaned, 1)
                dve.wait_ge(w_meaned, 2 * n + 2)
                return V.tensor_tensor(head_cols(cols), head_cols(cols), m.unsqueeze(3).to_broadcast([P, cols.shape[1], N1, HD]), ALU.add)

            def center_weights(n):
                dve.wait_ge(w_loaded[n], 16)
                center(n, raw(n)[:, :, 0:D]).then_inc(w_centered, 1)

            def make_biases():
                dve.wait_ge(gate_done, 1)
                dve.wait_ge(b_loaded, 16 * len(biases))
                V.tensor_scalar(bo_sb[:], bo_sb[:], gate_t[:, 0:1], None, ALU.mult).then_inc(bias_done, 1)
                center(3, bq_sb[:].unsqueeze(1)).then_inc(bias_done, 1)
                center(4, bkv_sb[:, :, 0:D]).then_inc(bias_done, 1)
                dve.wait_ge(bias_done, 3)

            dve.wait_ge(zeroed, 4)

            def link(op, at):
                op.then_inc(link_done, 1)
                dve.wait_ge(link_done, at)
                return at

            def add_experts(i, bb, k):
                b = 2 * i + bb
                at = LINKS * b
                if k == 0:
                    dve.wait_ge(x_loaded, 16 * b + 16)
                    V.tensor_copy(w_here[:], weights[:, bass.ds(4 * b, 4)]).then_inc(link_done, 1)
                dve.wait_ge(y_loaded, 32 * b + 16 * k + 16)
                dve.wait_ge(link_done, at + 1 + k)
                for t in range(2):
                    l = V.scalar_tensor_tensor(x2[:, bb % 2, t], y_sb[:, t], w_here[:, 2 * t + k:2 * t + k + 1], x2[:, bb % 2, t], ALU.mult, ALU.add)
                l.then_inc(link_done, 1)
                dve.wait_ge(link_done, at + 2 + k)
                dve.nop(nofuse=True).then_inc(y_used, 1)

            def normalize(i, bb, n):
                b = 2 * i + bb
                at = LINKS * b + 3
                if n == 0:
                    for t in range(2):
                        l = V.bn_stats(stats[:, t], x2[:, bb % 2, t])
                    link(l, at + 1)
                    dve.nop(nofuse=True)
                    for t in range(2):
                        l = V.bn_aggr(mv[:, t], stats[:, t])
                    l.then_inc(link_done, 1)
                if n == 2:
                    dve.wait_ge(link_done, at + 2 + ROOT_LINKS)
                    for t in range(2):
                        l = V.tensor_scalar(xn[:, t], x2[:, bb % 2, t], mv[:, t, 0:1], rstd[:, t:t + 1], ALU.subtract, ALU.mult)
                    l.then_inc(xn_done, 1)

            def links(i, u, last, at):
                for bb, n in due(u, last, "norm"):
                    if n > 0:
                        root_link(dve, V, link_done, LINKS * (2 * i + bb) + 5, mv[:, :, 1], LN_EPS, root, rstd[:], 6 * (n - 1) + at)
                for bb, n in due(u, last, "root"):
                    root_link(dve, V, head_link, HEAD_LINKS * (2 * i + bb) + 3, hvar[:], HEAD_EPS, hroot, hrstd[:], 6 * n + at)

            def take(i, bb, j):
                dve.wait_ge(pj_ready, 8 * (2 * i + bb) + j + 1)
                if j == 6 and bb > 0:
                    dve.wait_ge(v_done, 2 * HG * (2 * i + bb))
                if j < 4:
                    V.tensor_tensor(nrm[:, bb % 2, j - 2], pjb[:], bq_sb[:], ALU.add).then_inc(pj_taken, 1)
                elif j < 6:
                    V.tensor_tensor(nrm[:, bb % 2, j - 2], pjb[:], bkv_sb[:, j - 4, 0:D], ALU.add).then_inc(pj_taken, 1)
                else:
                    V.tensor_tensor(v_raw[:, j - 6], pjb[:], bkv_sb[:, j - 6, D:], ALU.add).then_inc(pj_taken, 1)

            def step(i, u, last):
                for bb, n in due(u, last, "root"):
                    if n == 0:
                        b = 2 * i + bb
                        dve.wait_ge(head_link, HEAD_LINKS * b + 2)
                        V.tensor_scalar(hvar[:], hsum[:], 1.0 / HD, None, ALU.mult).then_inc(head_link, 1)
                        if u >= AHEAD:
                            dve.wait_ge(nrm_link, 3 * GROUPS * b - 2)
                for bb, j in due(u, last, "take"):
                    take(i, bb, j)
                links(i, u, last, 0)
                for bb, j in due(u, last, "turned"):
                    b = 2 * i + bb
                    if j == 0:
                        dve.wait_ge(ctx_hid, b + 1)
                        low(ctx_lo[:, :, DCA:], ctx_raw[:, :, DCA:], ctx_hi[:, :, DCA:])
                        low(dca_lo[:, :, 0:DCA], ctx_raw[:, :, 0:DCA], dca_hi[:, :, 0:DCA]).then_inc(ctx_lod, 1)
                    dve.wait_ge(pj_hid, 2 * b + j + 1)
                    low(xt_lo[:, 2 * j:2 * j + 2], pjb[:].rearrange("p (c s) -> p c s", c=2), xt_hi[:, 2 * j:2 * j + 2]).then_inc(pj_taken, 1)
                if here(u - 3, last):
                    v = u - 3
                    dve.wait_ge(pt_hid, PAIR * i + v + 1)
                    low(pt_lo[:, v % 2], ptb[:].rearrange("p (k s) -> p k s", k=2), pt_hi[:, v % 2]).then_inc(pt_lod, 1)
                links(i, u, last, 1)
                if here(u + 1, last):
                    v = u + 1
                    dve.wait_ge(s_ready, PAIR * i + v + 1)
                    s = sc[v % 2][:].rearrange("p (t s) -> p t s", t=2)
                    V.tensor_reduce(mx[:, v % 2, 0], s[:, :, 0:DCA], AX.X, ALU.max)
                    V.tensor_reduce(mx[:, v % 2, 1], s[:, :, DCA:], AX.X, ALU.max).then_inc(s_max, 1)
                links(i, u, last, 2)
                if here(u + 1, last):
                    dve.wait_ge(s_max, PAIR * i + v + 1)
                    V.tensor_scalar(nbias[:, v % 2], mx[:, v % 2], -SCALE, None, ALU.mult).then_inc(s_bias, 1)
                links(i, u, last, 3)
                if here(u - 1, last):
                    v = u - 1
                    dve.wait_ge(e_done, PAIR * i + v + 3)
                    V.reciprocal(rinv[:, v % 4], rsum[:, v % 4]).then_inc(r_done, 1)
                links(i, u, last, 4)
                if here(u - 4, last) and (u - 4) % HG == HG - 1:
                    n = (u - 4) // HG
                    dve.wait_ge(ot_hid, 2 * GROUPS * i + n + 1)
                    low(ot_lo[:, n % 2], avb[:, 0:S], ot_hi[:, n % 2]).then_inc(ot_lod, 1)
                if here(u - 5, last) and (u - 5) % N1 == N1 - 1:
                    bb = (u - 5) // N1
                    dve.wait_ge(o_ready, 2 * i + bb + 1)
                    dve.wait_ge(x_used, 2 * i + bb + 3)
                    for t in range(2):
                        o = V.scalar_tensor_tensor(x_sb[:, bb, t], ob[t][:], gate_t[:, 0:1], x_sb[:, bb, t], ALU.mult, ALU.add)
                    o.then_inc(o_free, 1)
                links(i, u, last, 5)
                for bb, k in due(u, last, "sum"):
                    add_experts(i, bb, k)
                for bb, n in due(u, last, "norm"):
                    normalize(i, bb, n)
                for bb, half in due(u, last, "sumsq"):
                    b = 2 * i + bb
                    dve.wait_ge(sq_done, 2 * b + half + 1)
                    V.tensor_reduce(hsum[:, half * 2 * N1:(half + 1) * 2 * N1], sq[:].rearrange("p r (h c) -> p (r h) c", h=N1),
                                    AX.X, ALU.add).then_inc(head_link, 1)
                if u in (-27, -22, -21):
                    center_weights((-27, -22, -21).index(u))
                if u == -18:
                    make_biases()

            all_steps(dve, step)
    clear(nc, used)

def feed_forward(nc, x_in, x_out, w1, b1, w2, b2, gate, identity, tag):
    CH = 512
    FC, TC, HC = D // P, CH // P, H1 // P
    CHUNKS = TOK // CH
    used = []
    with ExitStack() as ctx:
        def sb(name, shape, dt=F32):
            return ctx.enter_context(nc.sbuf_tensor(tag + name, shape, dt))

        def bank(name):
            return ctx.enter_context(nc.psum_tensor(tag + name, [P, 512], F32))

        def sem(name):
            used.append(nc.alloc_semaphore(tag + name))
            return used[-1]

        w1_hi, w1_lo = sb("w1_hi", [P, FC, H1], F32R), sb("w1_lo", [P, FC, H1], F32R)
        w2_hi, w2_lo = sb("w2_hi", [P, HC, D], F32R), sb("w2_lo", [P, HC, D], F32R)
        ident, b1_sb, b2_sb, gate_t = sb("ident", [P, P]), sb("b1_sb", [P, HC]), sb("b2_sb", [P, D]), sb("gate_t", [P, 1])
        x_sb = sb("x_sb", [P, 2, TC, D])
        xn = sb("xn", [P, TC, D])
        stats, mv, rstd = sb("stats", [P, TC, 6]), sb("mv", [P, TC, 2]), sb("rstd", [P, TC])
        root = [sb(f"root{n}", [P, TC]) for n in range(3)]
        xt_hi, xt_lo = sb("xt_hi", [P, 2, FC, CH], F32R), sb("xt_lo", [P, 2, FC, CH], F32R)
        h_f = sb("h_f", [P, 2, CH])
        h_hi, h_lo = sb("h_hi", [P, 2, CH], F32R), sb("h_lo", [P, 2, CH], F32R)
        w_raw = sb("w_raw", [P, H1])
        credit = sb("credit", [P, 4])

        tb = [bank("tb0"), bank("tb1")]
        hb = [bank("hb0"), bank("hb1")]
        ob = [bank(f"ob{t}") for t in range(TC)]

        c_loaded, w_loaded, w_hid = sem("c_loaded"), [sem(f"w_loaded{n}") for n in range(4)], sem("w_hid")
        w_lod, w_lod_pool = sem("w_lod"), sem("w_lod_pool")
        gate_done, bias_done, link_done = sem("gate_done"), sem("bias_done"), sem("link_done")
        x_loaded, x_stored = [sem("x_loaded0"), sem("x_loaded1")], [sem("x_stored0"), sem("x_stored1")]
        xn_done, t_ready, xt_hid, xt_lod = sem("xn_done"), sem("t_ready"), sem("xt_hid"), sem("xt_lod")
        h_ready, gelu_done, h_hid, h_lod = sem("h_ready"), sem("gelu_done"), sem("h_hid"), sem("h_lod")
        o_ready, o_done = sem("o_ready"), sem("o_done")

        consts = [(ident[:], identity), (b1_sb[:], b1), (b2_sb[:], b2), (gate_t[:], gate)]
        W2_STEPS = 4
        pieces = [(w1[:, c:c + 1], w1_hi[:, c:c + 1], w1_lo[:, c:c + 1]) for c in range(FC)]
        pieces += [(w2[:, h:h + W2_STEPS], w2_hi[:, h:h + W2_STEPS], w2_lo[:, h:h + W2_STEPS]) for h in range(0, HC, W2_STEPS)]

        ROOM = (0, 1, 2, 1, 2, 1, 1, 1)

        def raw(n):
            a = pieces[n][0].shape[1]
            rows = (xn[:].rearrange("p t d -> p (t d)"), w_raw[:], x_sb[:, 1].rearrange("p t d -> p (t d)"))[ROOM[n]]
            return rows.rearrange("p (a b) -> p a b", a=a)

        def low_done(eng, n):
            if n < 2:
                eng.wait_ge(w_lod, n + 1)
            else:
                eng.wait_ge(w_lod_pool, n - 1)

        NORM = {2: 0, 3: 1, 4: 2, 5: 3, 6: 4}
        TURN = {7 + c: c for c in range(FC)}

        def all_chunks(eng, first, chunk):
            first()
            for b in range(2):
                chunk(0, b, False, b == 0)
            with eng.Fori(1, CHUNKS // 2 - 1) as i:
                for b in range(2):
                    chunk(i, b, False)
            for b in range(2):
                chunk(CHUNKS // 2 - 1, b, b == 1)

        block = ctx.enter_context(nc.Block())

        @block.sync
        def _(sp):
            for dst, src in consts:
                sp.dma_start(dst, src).then_inc(c_loaded, 16)
            def load_rows(n, b):
                sp.dma_start(x_sb[:, b], x_in[bass.ds(n * CH, CH), :].rearrange("(t p) d -> p t d", p=P)).then_inc(x_loaded[b], 16)

            for n, (src, _, _) in enumerate(pieces):
                if ROOM[n] in ROOM[:n]:
                    low_done(sp, max(k for k in range(n) if ROOM[k] == ROOM[n]))
                sp.dma_start(raw(n), src).then_inc(w_loaded[n % 4], 16)
                if n == 2:
                    load_rows(0, 0)
                if n == 5:
                    low_done(sp, 4)
                    load_rows(1, 1)
            with sp.Fori(1, CHUNKS // 2) as i:
                for b in range(2):
                    sp.wait_ge(x_stored[b], 16 * i)
                    sp.nop(nofuse=True)
                    load_rows(2 * i + b, b)

        @block.tensor
        def _(pe):
            def three(out, a_hi, a_lo, b_hi, b_lo, start, stop):
                nc.tensor.matmul(out, a_hi, b_hi, start=start, stop=False)
                nc.tensor.matmul(out, a_hi, b_lo, start=False, stop=False)
                return nc.tensor.matmul(out, a_lo, b_hi, start=False, stop=stop)

            def turn(n, c):
                pe.wait_ge(xn_done, n + 1)
                pe.wait_ge(xt_lod, FC * n + c + 1)
                for t in range(TC):
                    mm = nc.tensor.transpose(tb[c % 2][:, t * P:(t + 1) * P], xn[:, t, c * P:(c + 1) * P], ident[:])
                mm.then_inc(t_ready, 1)

            def hidden(n, b, j):
                pe.wait_ge(gelu_done, HC * n + j + 1)
                if j == 0:
                    pe.wait_ge(xt_lod, FC * n + FC + 2)
                for c in range(FC):
                    mm = three(hb[j % 2][:], w1_hi[:, c, j * P:(j + 1) * P], w1_lo[:, c, j * P:(j + 1) * P], xt_hi[:, b, c], xt_lo[:, b, c], c == 0, c == FC - 1)
                mm.then_inc(h_ready, 1)

            def out(n, j):
                pe.wait_ge(h_lod, HC * n + j + 3)
                for t in range(TC):
                    if j == 0:
                        pe.wait_ge(o_done, TC * n + t + 1)
                    mm = three(ob[t][:], h_hi[:, j % 2, t * P:(t + 1) * P], h_lo[:, j % 2, t * P:(t + 1) * P], w2_hi[:, j], w2_lo[:, j], j == 0, j == HC - 1)
                    if j == HC - 1:
                        mm.then_inc(o_ready, 1)

            pe.wait_ge(c_loaded, 16 * len(consts))

            def first():
                for c in range(FC):
                    turn(0, c)
                for n in range(FC):
                    low_done(pe, n)
                hidden(0, 0, 0)

            def chunk(i, b, last, is_first=False):
                n = 2 * i + b
                for j in range(HC):
                    if j + 1 < HC:
                        hidden(n, b, j + 1)
                    elif not last:
                        hidden(n + 1, 1 - b, 0)
                    if is_first and j % W2_STEPS == 0:
                        low_done(pe, FC + j // W2_STEPS)
                    out(n, j)
                    if j in TURN and not last:
                        turn(n + 1, TURN[j])

            all_chunks(pe, first, chunk)

        @block.scalar
        def _(act):
            act.wait_ge(c_loaded, 16 * len(consts))
            nc.scalar.activation(gate_t[:], gate_t[:], ACT.Tanh).then_inc(gate_done, 1)

            def split(n):
                act.wait_ge(w_loaded[n % 4], 16 * (n // 4 + 1))
                nc.scalar.copy(pieces[n][1], raw(n)).then_inc(w_hid, 1)

            def turned(n, b, c):
                act.wait_ge(t_ready, FC * n + c + 1)
                nc.scalar.copy(xt_hi[:, b, c], tb[c % 2][:]).then_inc(xt_hid, 1)

            def first():
                for n in range(FC):
                    split(n)
                for c in range(FC):
                    turned(0, 0, c)
                split(FC)

            def chunk(i, b, last, is_first=False):
                n = 2 * i + b
                for j in range(HC):
                    act.wait_ge(h_ready, HC * n + j + 1)
                    act.wait_ge(h_lod, HC * n + j + 1)
                    nc.scalar.activation(h_f[:, j % 2], hb[j % 2][:], ACT.Gelu, bias=b1_sb[:, j:j + 1]).then_inc(gelu_done, 1)
                    act.wait_ge(gelu_done, HC * n + j + 3)
                    nc.scalar.copy(h_hi[:, j % 2], h_f[:, j % 2]).then_inc(h_hid, 1)
                    if j - 1 in TURN and not last:
                        turned(n + 1, 1 - b, TURN[j - 1])
                    if is_first and j % W2_STEPS == 1 and j + W2_STEPS < HC:
                        split(FC + 1 + j // W2_STEPS)
                act.wait_ge(o_done, TC * n + 2 * TC)
                act.dma_start(x_out[bass.ds(n * CH, CH), :].rearrange("(t p) d -> p t d", p=P), x_sb[:, b]).then_inc(x_stored[b], 16)

            all_chunks(act, first, chunk)
            for b in range(2):
                act.wait_ge(x_stored[b], 16 * (CHUNKS // 2))

        @block.gpsimd
        def _(pool):
            for n in range(2, len(pieces)):
                pool.wait_ge(w_hid, n + 1)
                nc.gpsimd.tensor_tensor(pieces[n][2], raw(n), pieces[n][1].bitcast(F32), ALU.subtract).then_inc(w_lod_pool, 1)

        @block.vector
        def _(dve):
            V = nc.vector
            LINKS = 2 + ROOT_LINKS + 1

            def low(out, raw_in, hi):
                return V.tensor_tensor(out, raw_in, hi.bitcast(F32), ALU.subtract)

            V.memset(credit[:, 0:1], 0.0).then_inc(gelu_done, 2)
            V.memset(credit[:, 1:2], 0.0).then_inc(xt_lod, 2)
            V.memset(credit[:, 2:3], 0.0).then_inc(o_done, TC)
            V.memset(credit[:, 3:4], 0.0).then_inc(h_lod, 2)
            dve.wait_ge(c_loaded, 16 * len(consts))
            dve.wait_ge(gate_done, 1)
            V.tensor_scalar(b2_sb[:], b2_sb[:], gate_t[:, 0:1], None, ALU.mult).then_inc(bias_done, 1)
            dve.wait_ge(bias_done, 1)

            def normalize(i, b, part):
                n = 2 * i + b
                at = LINKS * n
                x = x_sb[:, b % 2]
                if part == 0:
                    dve.wait_ge(x_loaded[b % 2], 16 * (i + b // 2) + 16)
                    for t in range(TC):
                        l = V.bn_stats(stats[:, t], x[:, t])
                    l.then_inc(link_done, 1)
                elif part == 1:
                    dve.wait_ge(link_done, at + 1)
                    dve.nop(nofuse=True)
                    for t in range(TC):
                        l = V.bn_aggr(mv[:, t], stats[:, t])
                    l.then_inc(link_done, 1)
                    inverse_root(dve, V, link_done, at + 2, mv[:, :, 1], LN_EPS, root, rstd[:], 0)
                elif part == 2:
                    inverse_root(dve, V, link_done, at + 2, mv[:, :, 1], LN_EPS, root, rstd[:], 1)
                elif part == 3:
                    for t in range(TC):
                        l = V.tensor_scalar(xn[:, t], x[:, t], mv[:, t, 0:1], rstd[:, t:t + 1], ALU.subtract, ALU.mult)
                    l.then_inc(xn_done, 1)
                else:
                    for t in range(TC):
                        l = V.tensor_tensor(x[:, t], x[:, t], b2_sb[:], ALU.add)
                    l.then_inc(link_done, 1)

            def turned(n, b, c):
                dve.wait_ge(xt_hid, FC * n + c + 1)
                low(xt_lo[:, b, c], tb[c % 2][:], xt_hi[:, b, c]).then_inc(xt_lod, 1)

            def first():
                for n in range(2):
                    dve.wait_ge(w_hid, n + 1)
                    low(pieces[n][2], raw(n), pieces[n][1]).then_inc(w_lod, 1)
                dve.wait_ge(w_lod, 1)
                for part in NORM.values():
                    normalize(0, 0, part)
                for c in range(FC):
                    turned(0, 0, c)

            def chunk(i, b, last, is_first=False):
                n = 2 * i + b
                for j in range(HC):
                    dve.wait_ge(h_hid, HC * n + j + 1)
                    low(h_lo[:, j % 2], h_f[:, j % 2], h_hi[:, j % 2]).then_inc(h_lod, 1)
                    if not last:
                        if j in NORM:
                            normalize(i, b + 1, NORM[j])
                        if j - 1 in TURN:
                            turned(n + 1, 1 - b, TURN[j - 1])
                dve.wait_ge(link_done, LINKS * n + LINKS)
                for t in range(TC):
                    dve.wait_ge(o_ready, TC * n + t + 1)
                    o = V.scalar_tensor_tensor(x_sb[:, b, t], ob[t][:], gate_t[:, 0:1], x_sb[:, b, t], ALU.mult, ALU.add)
                    o.then_inc(o_done, 1)

            all_chunks(dve, first, chunk)
    clear(nc, used)

def program(nc, a, out):
    def dram(name, shape, dt=F32):
        return nc.dram_tensor(name, shape, dt, kind="Internal").ap()

    def by_row(w):
        return w.rearrange("(c p) n -> p c n", p=P)

    x_half, x1, x3 = dram("x_half", [TOK, D]), dram("x1", [TOK, D]), dram("x3", [TOK, D])
    xn_rows, y_rows = dram("xn_rows", [TOK + P, D]), dram("y_rows", [TOPK * TOK + TILE, D])
    slot_tokens, tile_table = dram("slot_tokens", [SLOTS, 1], I32), dram("tile_table", [P, 2], I32)
    for half, (x_res, x_out) in enumerate(((a["x"], x_half), (x_half, x1))):
        gated_cross_attention(nc, half, a["x"], x_res, x_out, a["ctx_t"], a["mask"], a["g_xattn0"], by_row(a["wq0"]), by_row(a["wk0"]), by_row(a["wv0"]),
                              by_row(a["wo0"]), a["identity"], f"a{half}_")
    with ExitStack() as ctx:
        weights = ctx.enter_context(nc.sbuf_tensor("weights", [P, TOPK * TOK // P], F32))
        route(nc, x1, xn_rows, slot_tokens, tile_table, a["router_w"], a["router_scale"], a["expert_scale"], a["g_ffn0"], a["identity"], a["earlier"],
              a["iotas"], a["pairs"], a["empty_list"], weights, "r_")
        experts(nc, xn_rows, slot_tokens, tile_table, a["w_gate"], a["w_out"], y_rows, a["identity"], "e_")
        gated_normed_attention(nc, x1, y_rows, weights, x3, a["ctx_t"], a["g_xattn1"], by_row(a["wq1"]), by_row(a["wkv1"]), by_row(a["wkv_dca"]),
                               by_row(a["wo1"]), a["bq1"], a["bkv1"], a["ln_w"], a["ln_b"], a["bo1"], a["identity"], "d_")
    feed_forward(nc, x3, out, by_row(a["w1"]), a["b1"], by_row(a["w2"]), a["b2"], a["g_ffn1"], a["identity"], "f_")


def kernel(**inputs):
    import concourse.bacc as bacc
    from concourse.bass_utils import run_bass_kernel_spmd

    def all_rows(v):
        return np.broadcast_to(v, (P,) + np.shape(v))

    def columns(v, n):
        return np.reshape(v, (n, P)).T

    def k_then_v(v):
        hd = D // NHEAD1
        return np.reshape(v, v.shape[:-1] + (NHEAD1, 2, hd)).swapaxes(-3, -2).reshape(v.shape)

    i = {name: np.asarray(v) for name, v in inputs.items()}
    keys = np.r_[S - DCA:S, 0:S - DCA]
    bkv = np.array(all_rows(all_rows(k_then_v(np.concatenate([i["L1_xattn_bk"], i["L1_xattn_bv"]])))[0:2]))
    bkv[0:DCA, 0] = i["L1_xattn_bkv_dca"]
    ln = {}
    for n in "wb":
        ln[n] = np.stack([i[f"L1_xattn_{x}_{n}"] for x in ("qn", "qn", "kn", "kn")])
        ln[n] = np.array(all_rows(ln[n]))
        ln[n][0:DCA, 2] = i[f"L1_xattn_kn_dca_{n}"]
    iotas = np.zeros((P, 3 * E + 1), np.float32)
    iotas[:, 0:E], iotas[:, E:2 * E] = np.arange(E), np.arange(E) * TOK
    iotas[0:E, 2 * E:3 * E] = np.triu(np.ones((E, E)))
    iotas[:, 3 * E] = np.arange(P)
    arrays = {
        "x": i["x"].reshape(TOK, D), "ctx_t": i["ctx_1024"][:, keys].swapaxes(1, 2),
        "mask": np.ascontiguousarray(all_rows(i["mask_BxS2_bf1"][:, keys].reshape(-1))).view(np.uint8),
        "g_xattn0": all_rows(i["g_xattn"][0:1]), "g_xattn1": all_rows(i["g_xattn"][1:2]),
        "g_ffn0": all_rows(i["g_ffn"][0:1]), "g_ffn1": all_rows(i["g_ffn"][1:2]),
        "wq0": i["L0_xattn_Wq"], "wk0": i["L0_xattn_Wk"], "wv0": i["L0_xattn_Wv"], "wo0": i["L0_xattn_Wo"],
        "router_w": i["L0_ffn_router_logits"].reshape(D // P, P, E).swapaxes(0, 1), "router_scale": columns(i["L0_ffn_router_scale"], D // P),
        "expert_scale": all_rows(i["L0_ffn_per_expert_scale"]),
        "w_gate": i["L0_ffn_gating_einsum"].transpose(0, 3, 1, 2).reshape(E, D, 2 * H0), "w_out": i["L0_ffn_linear"],
        "wq1": i["L1_xattn_Wq"], "wkv1": k_then_v(np.concatenate([i["L1_xattn_Wk"], i["L1_xattn_Wv"]], axis=1)), "wkv_dca": i["L1_xattn_Wkv_dca"],
        "wo1": i["L1_xattn_Wo"], "bq1": all_rows(i["L1_xattn_bq"]), "bkv1": bkv, "ln_w": ln["w"], "ln_b": ln["b"], "bo1": all_rows(i["L1_xattn_bo"]),
        "w1": i["L1_ffn_proj1"].T, "b1": columns(i["L1_ffn_proj1_bias"], H1 // P), "w2": i["L1_ffn_proj2"].T, "b2": all_rows(i["L1_ffn_proj2_bias"]),
        "identity": np.eye(P, dtype=np.float32), "earlier": np.triu(np.ones((P, P), np.float32), 1), "iotas": iotas,
        "pairs": np.arange(TOPK * TOK, dtype=np.int32).reshape(TOK // P, P, TOPK).swapaxes(0, 1).reshape(P, -1),
        "empty_list": (TOPK * TOK + np.arange(SLOTS, dtype=np.int32) % TILE).reshape(P, -1),
    }
    arrays = {f"in_{name}": np.ascontiguousarray(v) for name, v in arrays.items()}
    nc = bacc.Bacc("TRN2", target_bir_lowering=False, num_devices=1)
    aps = {name[3:]: nc.dram_tensor(name, v.shape, mybir.dt.from_np(v.dtype), kind="ExternalInput").ap() for name, v in arrays.items()}
    out = nc.dram_tensor("out_x", [TOK, D], F32, kind="ExternalOutput").ap()
    program(nc, aps, out)
    r = run_bass_kernel_spmd(nc, [arrays], core_ids=[0])
    return r.results[0]["out_x"].reshape(B, S, D)
```
